# Optimizing a Trainium2 kernel written in Bass

```python
import numpy as np
import jax
import jax.numpy as jnp

def _softmax(x, axis=-1):
    return jax.nn.softmax(x, axis=axis)

def _gelu(x):
    return jax.nn.gelu(x, approximate=True)

def _silu(x):
    return jax.nn.silu(x)

def _sigmoid(x):
    return jax.nn.sigmoid(x)

def _layernorm(x, axis=-1, eps=1e-05):
    m = jnp.mean(x, axis=axis, keepdims=True)
    v = jnp.var(x, axis=axis, keepdims=True)
    return (x - m) / jnp.sqrt(v + eps)

def _scatter_add(tgt, idx, src, axis=0):
    return tgt.at[idx].add(src)

def _segment_sum(src, seg, n):
    return jax.ops.segment_sum(src, seg, n)
kernel_name = 'mk_cond_seq_d1_seqx_r2_8215a7'

def setup_inputs(seed: int=0):
    np.random.seed(seed)
    _w = jnp.asarray

    def _rec_inputs():
        import jax
        import jax.numpy as jnp
        _rk = jax.random.key(seed)
        x = 7.22e-05 + 1 * jax.random.normal(jax.random.fold_in(_rk, 1), (4, 1024, 512), jnp.float32)
        _lenS = 1024 - jax.random.randint(jax.random.fold_in(_rk, 7), (4,), 0, max(1, 1024 // 4) + 1, jnp.int32)
        _lenS2 = 1024 - jax.random.randint(jax.random.fold_in(_rk, 8), (4,), 0, max(1, 1024 // 4) + 1, jnp.int32)
        cond_1024 = 0.00782532 + 1.00527 * jax.random.normal(jax.random.fold_in(_rk, 11), (4, 512), jnp.float32)
        return (x, cond_1024)
    x, cond_1024 = _rec_inputs()

    def _L0_cond_setup():
        import jax, jax.numpy as jnp
        import numpy as np
        EPS = 1e-12

        def rmsnorm(x, g, dim):
            n = jnp.maximum(jnp.linalg.norm(x, axis=-1, keepdims=True), EPS)
            return x / n * dim ** 0.5 * g

        def modulate(x, scale, shift):
            return x * (1.0 + scale[:, None, :]) + shift[:, None, :]
        key = jax.random.key(seed)
        ks = jax.random.split(key, 12)
        B, T, D, H = (8, 512, 512, 16)
        Dm = 4 * D
        s = 0.02
        inp = {'x': jax.random.normal(ks[0], (B, T, D), jnp.float32), 'c': jax.random.normal(ks[1], (B, D), jnp.float32), 'g1': jnp.ones((1,), jnp.float32), 'g2': jnp.ones((1,), jnp.float32), 'gq': jnp.ones((1,), jnp.float32), 'gk': jnp.ones((1,), jnp.float32), 'Wqkv': jax.random.normal(ks[2], (3 * D, D), jnp.float32) * s, 'bqkv': jnp.zeros((3 * D,), jnp.float32), 'Wproj': jax.random.normal(ks[3], (D, D), jnp.float32) * s, 'bproj': jnp.zeros((D,), jnp.float32), 'Wfc1': jax.random.normal(ks[4], (Dm, D), jnp.float32) * s, 'bfc1': jnp.zeros((Dm,), jnp.float32), 'Wfc2': jax.random.normal(ks[5], (D, Dm), jnp.float32) * s, 'bfc2': jnp.zeros((D,), jnp.float32), 'Wada': jax.random.normal(ks[6], (6 * D, D), jnp.float32) * s, 'bada': jnp.zeros((6 * D,), jnp.float32)}
        return inp
    _L0_cond_all = _L0_cond_setup()
    _L0_cond_in = {k: v for k, v in _L0_cond_all.items() if k in ('g1', 'g2', 'gq', 'gk', 'Wqkv', 'bqkv', 'Wproj', 'bproj', 'Wfc1', 'bfc1', 'Wfc2', 'bfc2', 'Wada', 'bada')}
    del _L0_cond_all
    return {'x': x, 'cond_1024': cond_1024, 'L0_cond_g1': _L0_cond_in['g1'], 'L0_cond_g2': _L0_cond_in['g2'], 'L0_cond_gq': _L0_cond_in['gq'], 'L0_cond_gk': _L0_cond_in['gk'], 'L0_cond_Wqkv': _L0_cond_in['Wqkv'], 'L0_cond_bqkv': _L0_cond_in['bqkv'], 'L0_cond_Wproj': _L0_cond_in['Wproj'], 'L0_cond_bproj': _L0_cond_in['bproj'], 'L0_cond_Wfc1': _L0_cond_in['Wfc1'], 'L0_cond_bfc1': _L0_cond_in['bfc1'], 'L0_cond_Wfc2': _L0_cond_in['Wfc2'], 'L0_cond_bfc2': _L0_cond_in['bfc2'], 'L0_cond_Wada': _L0_cond_in['Wada'], 'L0_cond_bada': _L0_cond_in['bada']}

def reference(x, cond_1024, L0_cond_g1, L0_cond_g2, L0_cond_gq, L0_cond_gk, L0_cond_Wqkv, L0_cond_bqkv, L0_cond_Wproj, L0_cond_bproj, L0_cond_Wfc1, L0_cond_bfc1, L0_cond_Wfc2, L0_cond_bfc2, L0_cond_Wada, L0_cond_bada):
    import jax
    import jax.numpy as jnp

    def _L0_cond_ref(x, c, g1, g2, gq, gk, Wqkv, bqkv, Wproj, bproj, Wfc1, bfc1, Wfc2, bfc2, Wada, bada):
        import jax, jax.numpy as jnp
        import numpy as np
        EPS = 1e-12

        def rmsnorm(x, g, dim):
            n = jnp.maximum(jnp.linalg.norm(x, axis=-1, keepdims=True), EPS)
            return x / n * dim ** 0.5 * g

        def modulate(x, scale, shift):
            return x * (1.0 + scale[:, None, :]) + shift[:, None, :]
        B, T, D = x.shape
        H = 16
        hd = D // H
        ada = jax.nn.silu(c) @ Wada.T + bada
        shift_msa, scale_msa, gate_msa, shift_mlp, scale_mlp, gate_mlp = jnp.split(ada, 6, axis=-1)
        h = modulate(rmsnorm(x, g1, D), scale_msa, shift_msa)
        qkv = h @ Wqkv.T + bqkv
        qkv = qkv.reshape(B, T, 3, H, hd).transpose(2, 0, 3, 1, 4)
        q, k, v = (qkv[0], qkv[1], qkv[2])
        q = rmsnorm(q, gq, hd) * hd ** (-0.5)
        k = rmsnorm(k, gk, hd)
        attn = jax.nn.softmax(jnp.einsum('bhqd,bhkd->bhqk', q, k), axis=-1)
        o = jnp.einsum('bhqk,bhkd->bhqd', attn, v)
        o = o.transpose(0, 2, 1, 3).reshape(B, T, D)
        o = o @ Wproj.T + bproj
        x = x + gate_msa[:, None, :] * o
        h = modulate(rmsnorm(x, g2, D), scale_mlp, shift_mlp)
        h = jax.nn.gelu(h @ Wfc1.T + bfc1, approximate=True)
        h = h @ Wfc2.T + bfc2
        x = x + gate_mlp[:, None, :] * h
        return x
    x = _L0_cond_ref(x, cond_1024, L0_cond_g1, L0_cond_g2, L0_cond_gq, L0_cond_gk, L0_cond_Wqkv, L0_cond_bqkv, L0_cond_Wproj, L0_cond_bproj, L0_cond_Wfc1, L0_cond_bfc1, L0_cond_Wfc2, L0_cond_bfc2, L0_cond_Wada, L0_cond_bada)
    return x

_drawn_inputs = setup_inputs


def setup_inputs(seed=0):
    import zlib

    import numpy as np

    out = dict(_drawn_inputs(seed))
    spreads = {'L0_cond_bqkv': (0.0, 0.653),
     'L0_cond_bproj': (0.0, 0.275),
     'L0_cond_bfc1': (0.0, 0.547),
     'L0_cond_bfc2': (0.0, 0.286),
     'L0_cond_bada': (0.0, 0.1)}
    factors = {'L0_cond_Wqkv': 3.171, 'L0_cond_Wproj': 2.757}
    for name, (base, spread) in spreads.items():
        noise = np.random.default_rng([zlib.crc32(name.encode()), seed]).standard_normal(out[name].shape)
        drawn = base * np.exp(spread * noise) if base else spread * noise
        out[name] = jnp.asarray(drawn.astype(out[name].dtype))
    for name, factor in factors.items():
        out[name] = (out[name] * factor).astype(out[name].dtype)
    return out
```

```python
from contextlib import ExitStack

import concourse.bass as bass
from concourse import mybir

F32 = mybir.dt.float32
F32R = mybir.dt.float32r
ALU = mybir.AluOpType
ACT = mybir.ActivationFunctionType

P = 128
B, T, D = 4, 1024, 512
H, DH = 16, 32
FF = 4 * D
KT = D // P
HG = P // DH
NG = H // HG
CH = 512
NH = T // CH
NT = T // P
CT = CH // P
NC = B * NH
STEPS = NH * NT
BSTEPS = NG * STEPS
ADDS = NT - 1
NM = FF // P
RING = 3
EPS2 = 1e-24
LN_SCALE = 2.0 ** 16
LN_BIAS = 8 * 0.6931471805599453
SAFE = 64.0

UNITS = (("k", 0), ("q", 0), ("k", 1), ("q", 1))
NU = len(UNITS)
BUNITS = NG * NU

SLOW_GEMM = {3 * u + i: (u, i) for u in range(NU) for i in range(3)}
SLOW_RAW = {3 * u + 3: u for u in range(NU)}
SLOW_SUM = {3 * u + 4: u for u in range(NU)}
SLOW_FIN = {3 * u + 5: u for u in range(NU)}
FAST = {3: ("v", 0), 4: ("v", 1), 5: ("v", 2), 6: ("v", 3), 7: ("u", 0), 8: ("v", 4), 9: ("u", 1),
        10: ("u", 2), 11: ("v", 5), 12: ("u", 3), 13: ("v", 6), 14: ("v", 7)}
FAST_UNIT = {s: x[1] for s, x in FAST.items() if x[0] == "u"}
FAST_RAW = {s + 1: u for s, u in FAST_UNIT.items()}
FAST_SUM = {s + 2: u for s, u in FAST_UNIT.items()}
FAST_FIN = {s + 3: u for s, u in FAST_UNIT.items()}
FAST_V = {s: x[1] for s, x in FAST.items() if x[0] == "v"}
FAST_VOUT = {s + 1: t for s, t in FAST_V.items()}
FAST_STAT = {t: t for t in range(NT)}
FAST_TURN = {t + 1: t for t in range(NT)}


def full(ap):
    return ap.bitcast(F32)


def build_setup(nc, small, dram, wq_hi, wq_lo):
    with ExitStack() as ctx:
        def sb(name, shape, dt=F32):
            return ctx.enter_context(nc.sbuf_tensor(name, shape, dt))

        def sem(name):
            return ctx.enter_context(nc.semaphore(name))

        NA = 6 * D // CH
        wada = sb("wada", [P, KT, 6 * D])
        wstage = sb("wstage", [P, KT, 3 * D])
        ada = sb("ada", [B, 6 * D])
        bada = sb("bada_rows", [B, 6 * D])
        cT = sb("cT", [P, KT, B])
        ce = sb("c_exp", [P, KT, B])
        cs = sb("c_sigmoid", [P, KT, B])
        silu = sb("silu_c", [P, KT, B])
        gains = sb("gains", [P, 4])
        tmp = sb("tmp", [P, 4])
        pa = [ctx.enter_context(nc.psum_tensor(f"pa{n}", [P, CH], F32)) for n in range(NA)]

        c_in, bias_in, gain_in = sem("c_in"), sem("bias_in"), sem("gain_in")
        wada_in = [sem(f"wada_in{n}") for n in range(NA)]
        wqkv_in = [sem(f"wqkv_in{n}") for n in range(3)]
        exp_c, sig_c, silu_c = sem("exp_c"), sem("sig_c"), sem("silu_c_done")
        ada_mm, ada_out, ada_stored = sem("ada_mm"), sem("ada_out"), sem("ada_stored")
        high, low, gain_chain, zeroed, masks = sem("high"), sem("low"), sem("gain_chain"), sem("zeroed"), sem("masks")
        block = ctx.enter_context(nc.Block())

        @block.sync
        def _(sp):
            sp.dma_start(cT[:], dram["cT"].rearrange("(k p) b -> p k b", p=P)).then_inc(c_in, 16)
            for n, g in enumerate(("g1", "g2", "gq", "gk")):
                sp.dma_start(gains[:, n:n + 1], dram[g].rearrange("(a n) -> a n", a=1).broadcast_to([P, 1])).then_inc(gain_in, 16)
            sp.dma_start(bada[:], dram["bada"].rearrange("(a n) -> a n", a=1).broadcast_to([B, 6 * D])).then_inc(bias_in, 16)
            for n in range(NA):
                sp.dma_start(wada[:, :, n * CH:(n + 1) * CH],
                             dram["wadaT"][:, n * CH:(n + 1) * CH].rearrange("(k p) n -> p k n", p=P)).then_inc(wada_in[n], 16)
            sp.wait_ge(ada_out, NA)
            sp.dma_start(dram["ada_b"], ada[:]).then_inc(ada_stored, 16)
            for h in range(NH):
                sp.dma_start(dram["ada_c"].rearrange("(b h) n -> b h n", h=NH)[:, h, :], ada[:]).then_inc(ada_stored, 16)
            sp.wait_ge(ada_stored, 16 * (1 + NH))

        @block.gpsimd
        def _(pool):
            ident, bones = small["ident"], small["head_ones"]
            pool.memset(ident[:], 0.0).then_inc(zeroed, 1)
            pool.memset(bones[:], 0.0).then_inc(zeroed, 1)
            pool.memset(small["ones"][:], 1.0).then_inc(masks, 1)
            pool.memset(small["minus_half"][:], -0.5).then_inc(masks, 1)
            pool.memset(small["ln_bias"][:], LN_BIAS).then_inc(masks, 1)
            pool.wait_ge(zeroed, 2)
            pool.affine_select(out=ident[:], in_=ident[:], compare_op=ALU.not_equal, fill=1.0, base=0,
                               pattern=[[-1, P]], channel_multiplier=1).then_inc(masks, 1)
            for h in range(HG):
                r = slice(h * DH, (h + 1) * DH)
                pool.wait_ge(masks, 4 + h)
                pool.memset(bones[r, r], 1.0).then_inc(masks, 1)

        @block.scalar
        def _(act):
            for n in range(3):
                act.dma_start(wstage[:, :, n * D:(n + 1) * D],
                              dram["wqkvT"][:, n * D:(n + 1) * D].rearrange("(k p) n -> p k n", p=P)).then_inc(wqkv_in[n], 16)
            act.preload_act_table_set("natural_log_exp_and_others")
            act.wait_ge(c_in, 16)
            nc.scalar.activation(ce[:], cT[:], ACT.Exp, scale=-1.0).then_inc(exp_c, 1)
            for n in range(3):
                s = slice(n * D, (n + 1) * D)
                act.wait_ge(wqkv_in[n], 16)
                nc.scalar.activation(wq_hi[:, :, s], wstage[:, :, s], ACT.Copy).then_inc(high, 1)

        @block.tensor
        def _(pe):
            pe.wait_ge(silu_c, 1)
            for n in range(NA):
                pe.wait_ge(wada_in[n], 16)
                for k in range(KT):
                    mm = nc.tensor.matmul(pa[n][0:B, :], silu[:, k, :], wada[:, k, n * CH:(n + 1) * CH],
                                          start=(k == 0), stop=(k == KT - 1))
                mm.then_inc(ada_mm, 1)

        @block.vector
        def _(dve):
            dve.wait_ge(exp_c, 1)
            nc.vector.tensor_scalar(ce[:], ce[:], 1.0, None, ALU.add).then_inc(sig_c, 1)
            dve.wait_ge(sig_c, 1)
            nc.vector.reciprocal(cs[:], ce[:]).then_inc(sig_c, 1)
            dve.wait_ge(sig_c, 2)
            nc.vector.tensor_tensor(silu[:], cT[:], cs[:], ALU.mult).then_inc(silu_c, 1)
            dve.wait_ge(gain_in, 64)
            nc.vector.tensor_scalar(small["x_gain"][:], gains[:, 0:1], float(D) ** 0.5, None, ALU.mult).then_inc(gain_chain, 1)
            nc.vector.tensor_scalar(small["y_gain"][:], gains[:, 1:2], float(D) ** 0.5, None, ALU.mult).then_inc(gain_chain, 1)
            nc.vector.tensor_scalar(small["s_gain"][:], gains[:, 2:3], gains[:, 3:4], float(DH) ** 0.5,
                                    ALU.mult, ALU.mult).then_inc(gain_chain, 1)
            dve.wait_ge(gain_chain, 3)
            nc.vector.tensor_scalar(tmp[:, 0:1], small["s_gain"][:], -1.0, None, ALU.mult).then_inc(gain_chain, 1)
            dve.wait_ge(gain_chain, 4)
            nc.vector.tensor_tensor(tmp[:, 1:2], tmp[:, 0:1], small["s_gain"][:], ALU.max).then_inc(gain_chain, 1)
            dve.wait_ge(gain_chain, 5)
            nc.vector.tensor_scalar(tmp[:, 2:3], tmp[:, 1:2], -1.0, SAFE, ALU.mult, ALU.add).then_inc(gain_chain, 1)
            dve.wait_ge(gain_chain, 6)
            nc.vector.tensor_scalar(small["shift"][:], tmp[:, 2:3], 0.0, None, ALU.min).then_inc(gain_chain, 1)
            for n in range(3):
                s = slice(n * D, (n + 1) * D)
                dve.wait_ge(high, n + 1)
                nc.vector.tensor_tensor(wq_lo[:, :, s], wstage[:, :, s], full(wq_hi[:, :, s]), ALU.subtract).then_inc(low, 1)
            dve.wait_ge(bias_in, 16)
            for n in range(NA):
                dve.wait_ge(ada_mm, n + 1)
                s = slice(n * CH, (n + 1) * CH)
                nc.vector.tensor_tensor(ada[:, s], pa[n][0:B, :], bada[:, s], ALU.add).then_inc(ada_out, 1)


def build_attention(nc, small, dram, wq_hi, wq_lo):
    with ExitStack() as ctx:
        def sb(name, shape, dt=F32):
            return ctx.enter_context(nc.sbuf_tensor(name, shape, dt))

        def sem(name):
            return ctx.enter_context(nc.semaphore(name))

        h_hi = sb("h_hi", [P, KT, T], F32R)
        h_lo = sb("h_lo", [P, KT, T], F32R)
        v_next = sb("v_next", [P, NT, D])
        v_now = sb("v_now", [P, NT, D])
        k_stack = [sb(f"k_stack{s}", [P, HG, T], F32R) for s in range(2)]
        q_stack = [sb(f"q_stack{h}", [P, HG, CH], F32R) for h in range(NH)]
        probs = [sb(f"probs{s}", [P, HG, CH]) for s in range(RING)]
        sums = sb("sums", [P, HG, CH])
        raw = [sb(f"raw{s}", [P, CH]) for s in range(2)]
        squares = sb("squares", [P, CH])
        norms = sb("norms", [P, CH])
        parts = sb("parts", [P, 2, CH], F32R)
        inverse = sb("inverse", [P, CH])
        o_out = sb("o_out", [P, CH])
        xt = [sb(f"xt{s}", [P, D]) for s in range(2)]
        unused = sb("unused", [P, D])
        h_full = sb("h_full", [P, KT, P])
        v_bias = sb("v_bias", [P, D])
        qk_bias = sb("qk_bias", [P, 2 * NG])
        mod = sb("mod", [P, 2 * KT])
        scale1 = sb("scale1", [P, KT])
        x_sq = sb("x_sq", [P, NT])
        x_sqc = sb("x_sqc", [P, NT])
        x_inv = sb("x_inv", [P, NT])

        scores = [ctx.enter_context(nc.psum_tensor(f"scores{p}", [P, 2, CH], F32)) for p in range(2)]
        pv = [ctx.enter_context(nc.psum_tensor(f"pv{h}", [P, CH], F32)) for h in range(NH)]
        gemm = ctx.enter_context(nc.psum_tensor("gemm", [P, CH], F32))
        aux = ctx.enter_context(nc.psum_tensor("aux", [P, CH], F32))

        const_in = sem("const_in")
        mod_in, mod_ready = sem("mod_in"), sem("mod_ready")
        x_in = [sem(f"x_in{s}") for s in range(2)]
        stat, stat_clamped, inv_done, x_normed = sem("stat"), sem("stat_clamped"), sem("inv_done"), sem("x_normed")
        turned, h_moved, hi_done, lo_done = sem("turned"), sem("h_moved"), sem("hi_done"), sem("lo_done")
        v_mm, v_moved, v_copied = sem("v_mm"), sem("v_moved"), sem("v_copied")
        unit_mm, raw_done, sq_done = sem("unit_mm"), sem("raw_done"), sem("sq_done")
        ss_mm, ss_moved, ln_done, norm_done = sem("ss_mm"), sem("ss_moved"), sem("ln_done"), sem("norm_done")
        normed, part_hi, part_lo, parts_stored = sem("normed"), sem("part_hi"), sem("part_lo"), sem("parts_stored")
        k_in = [[sem(f"k_in{s}_{h}") for h in range(NH)] for s in range(2)]
        q_in = [sem(f"q_in{h}") for h in range(NH)]
        qk_mm, exp_done, pv_mm = sem("qk_mm"), sem("exp_done"), sem("pv_mm")
        add_v, add_p = sem("add_v"), sem("add_p")
        rs_mm, inverted, o_done, o_stored = sem("rs_mm"), sem("inverted"), sem("o_done"), sem("o_stored")
        block = ctx.enter_context(nc.Block())

        def unit_no(b, g, u):
            return b * BUNITS + g * NU + u

        def half_no(b, g, h):
            return b * (NG * NH) + g * NH + h

        def step_no(b, g, st):
            return b * BSTEPS + g * STEPS + st

        def adds_before(l):
            return ADDS * (l // NT) + max(1, l % NT)

        def units_at(table_slow, table_fast, b, g, st, more):
            if g < NG - 1:
                return (b, g + 1, table_slow[st]) if st in table_slow else None
            return (b + 1, 0, table_fast[st]) if more and st in table_fast else None

        def tile_at(table_fast, b, g, st, more):
            return (b + 1, table_fast[st]) if g == NG - 1 and more and st in table_fast else None

        def stages(attend, b_of_loop):
            for st in range(STEPS + 2):
                attend(-1, NG - 1, st, True, alone=True)
            with b_of_loop(0, B - 1) as b:
                for g in range(NG):
                    for st in range(STEPS):
                        attend(b, g, st, True)
                attend(b, NG - 1, STEPS, True)
            for g in range(NG):
                for st in range(STEPS):
                    attend(B - 1, g, st, False)
            attend(B - 1, NG - 1, STEPS, False)

        @block.sync
        def _(sp):
            sp.dma_start(v_bias[:], dram["bqkv"][2 * D:3 * D].rearrange("(a n) -> a n", a=1).broadcast_to([P, D])).then_inc(const_in, 16)
            sp.dma_start(qk_bias[:], dram["bqkT"]).then_inc(const_in, 16)

            def load_x(b, t):
                if t >= 2:
                    sp.wait_ge(turned, b * NT + t - 1)
                else:
                    sp.wait_ge(turned, b * NT)
                sp.dma_start(xt[t % 2][:], dram["x"][b, t * P:(t + 1) * P, :]).then_inc(x_in[t % 2], 16)

            def step(b, g, st, more, alone=False):
                fin = units_at(SLOW_FIN, FAST_FIN, b, g, st, more)
                t = tile_at(FAST_STAT, b, g, st, more)
                if t and t[1] == 0:
                    sp.wait_ge(h_moved, t[0] * NT)
                    sp.dma_start(mod[:], dram["ada_b"][t[0], 0:2 * D].rearrange("(j p) -> p j", p=P),
                                 allow_slow_non_contiguous=True).then_inc(mod_in, 16)
                    load_x(*t)
                if t and t[1] + 1 < NT:
                    load_x(t[0], t[1] + 1)
                if fin:
                    fb, fg, u = fin
                    which, half = UNITS[u]
                    n = unit_no(fb, fg, u)
                    scratch = dram["parts"][u]
                    sp.wait_ge(part_lo, n + 1)
                    sp.dma_start(scratch.rearrange("c p n -> p c n"), full(parts[:])).then_inc(parts_stored, 16)
                    sp.wait_ge(parts_stored, 16 * (n + 1))
                    src = scratch.rearrange("c (h d) n -> c d h n", h=HG)
                    if which == "k":
                        dst, got = k_stack[fg % 2][:, :, half * CH:(half + 1) * CH], k_in[fg % 2][half]
                        first_step = (fb * NG + fg - 1) * STEPS
                        if alone:
                            first_step = 0
                    else:
                        dst, got = q_stack[half], q_in[half]
                        if not alone:
                            sp.wait_ge(qk_mm, 2 * ((fb * NG + fg - 1) * STEPS + (half + 1) * NT))
                    if which == "k" and not alone:
                        sp.wait_ge(qk_mm, 2 * first_step)
                    for a in range(2):
                        for c in range(2):
                            r = slice((2 * a + c) * DH, (2 * a + c + 1) * DH)
                            part = a if which == "k" else c
                            sp.dma_start(full(dst[r]), src[part]).then_inc(got, 16)
                l = g * STEPS + st
                if not alone and l % NT == 3 and l > NT:
                    store_o(b, l // NT - 1)
                if not alone and st == STEPS:
                    store_o(b, NG * NH - 1)

            def store_o(b, hh):
                sp.wait_ge(o_done, b * NG * NH + hh + 1)
                sp.dma_start(dram["heads_out"][b * NH + hh % NH, (hh // NH) * P:(hh // NH + 1) * P, :], o_out[:]).then_inc(o_stored, 16)

            stages(step, sp.Fori)
            sp.wait_ge(o_stored, 16 * B * NG * NH)

        @block.tensor
        def _(pe):
            def aux_free(b, g, st, alone):
                pass

            def qk(b, g, st, p):
                half, j = st // NT, st % NT
                s = g % 2
                if p == 0:
                    if st == 0 or st == NT // 2:
                        pe.wait_ge(k_in[s][st // (NT // 2)], 64 * (2 * b + g // 2 + 1))
                    if st % NT == 0:
                        pe.wait_ge(q_in[half], 64 * (NG * b + g + 1))
                n = step_no(b, g, st)
                if st > 0 or g > 0:
                    pe.wait_ge(exp_done, 2 * (n - 1) + p + 1)
                else:
                    pe.wait_ge(exp_done, 2 * BSTEPS * b)
                for i in range(2):
                    h = 2 * p + i
                    mm = nc.tensor.matmul(scores[p][:, i, :], k_stack[s][:, h, j * P:(j + 1) * P], q_stack[half][:, h, :],
                                          start=True, stop=True)
                mm.then_inc(qk_mm, 1)

            def weigh(b, l):
                g, st = l // STEPS, l % STEPS
                half, j = st // NT, st % NT
                n = b * BSTEPS + l
                pe.wait_ge(exp_done, 2 * n + 2)
                if g == 0 and half == 0:
                    pe.wait_ge(v_copied, b * NT + j + 1)
                if j == 0:
                    pe.wait_ge(o_done, b * NG * NH + max(0, g * NH + half - NH + 1))
                for h in range(HG):
                    mm = nc.tensor.matmul(pv[half][h * DH:(h + 1) * DH, :], v_now[:, j, (g * HG + h) * DH:(g * HG + h + 1) * DH],
                                          probs[l % RING][:, h, :], start=(j == 0), stop=(j == NT - 1))
                mm.then_inc(pv_mm, 1)

            def row_sums(b, hh, waits):
                pe.wait_ge(add_v, (b * NG * NH + hh + 1) * ADDS)
                pe.wait_ge(add_p, (b * NG * NH + hh + 1) * ADDS)
                aux_wait(waits)
                for h in range(HG):
                    mm = nc.tensor.matmul(aux[h * DH:(h + 1) * DH, :], small["ones"][:], sums[:, h, :], start=True, stop=True)
                mm.then_inc(rs_mm, 1)

            def aux_wait(waits):
                for s, v in waits:
                    pe.wait_ge(s, v)

            def aux_before(b, g, st, alone, kind):
                fast = g == NG - 1
                done = []
                table = FAST_SUM if fast else SLOW_SUM
                k = sum(1 for s in table if s < st or (s == st and kind == "turn"))
                first = unit_no(b + 1, 0, 0) if fast else unit_no(b, g + 1, 0)
                done.append((ss_moved, first + k))
                if fast:
                    k = sum(1 for s in FAST_TURN if s < st)
                    done.append((h_moved, (b + 1) * NT + k))
                else:
                    done.append((h_moved, (b + 1) * NT))
                if not alone:
                    l = g * STEPS + st
                    k = sum(1 for m in range(NT + 1, l + 1, NT) if m < l or kind != "rows")
                    done.append((inverted, b * NG * NH + k))
                return done

            def gemm_free(b, g, st):
                fast = g == NG - 1
                if fast:
                    pe.wait_ge(v_moved, (b + 1) * NT + sum(1 for s in FAST_V if s < st))
                    pe.wait_ge(raw_done, unit_no(b + 1, 0, 0) + sum(1 for s in FAST_UNIT if s < st))
                else:
                    pe.wait_ge(v_moved, (b + 1) * NT)
                    pe.wait_ge(raw_done, unit_no(b, g + 1, SLOW_GEMM[st][0]))

            def unit_products(b, g, u, lo, hi):
                which, half = UNITS[u]
                at = (0 if which == "q" else D) + g * P
                c = slice(half * CH, (half + 1) * CH)
                terms = [(w, h, k) for k in range(KT) for w, h in ((wq_hi, h_hi), (wq_hi, h_lo), (wq_lo, h_hi))]
                for n in range(lo, hi):
                    w, h, k = terms[n]
                    mm = nc.tensor.matmul(gemm[:], w[:, k, at:at + P], h[:, k, c], start=(n == 0), stop=(n == len(terms) - 1))
                if hi == len(terms):
                    mm.then_inc(unit_mm, 1)

            def v_products(t, lo, hi):
                c = slice(t * P, (t + 1) * P)
                terms = [(h, w, k) for k in range(KT) for h, w in ((h_hi, wq_hi), (h_hi, wq_lo), (h_lo, wq_hi))]
                for n in range(lo, hi):
                    h, w, k = terms[n]
                    mm = nc.tensor.matmul(gemm[:], h[:, k, c], w[:, k, 2 * D:3 * D], start=(n == 0), stop=(n == len(terms) - 1))
                if hi == len(terms):
                    mm.then_inc(v_mm, 1)

            def fill(b, g, st, more, part, alone):
                N = 3 * KT
                if g < NG - 1 and st in SLOW_GEMM:
                    u, i = SLOW_GEMM[st]
                    if part == 0 and i == 0:
                        gemm_free(b, g, st)
                    lo = i * N // 3 + part * N // 6
                    unit_products(g=g + 1, b=b, u=u, lo=lo, hi=lo + N // 6)
                if g == NG - 1 and more and st in FAST:
                    kind, x = FAST[st]
                    if part == 0:
                        gemm_free(b, g, st)
                        if kind == "v":
                            pe.wait_ge(lo_done, (b + 1) * NT + x + 1)
                        else:
                            pe.wait_ge(lo_done, (b + 1) * NT + (UNITS[x][1] + 1) * CT)
                    lo = part * N // 2
                    if kind == "v":
                        v_products(x, lo, lo + N // 2)
                    else:
                        unit_products(b + 1, 0, x, lo, lo + N // 2)
                if part == 0:
                    un = units_at(SLOW_SUM, FAST_SUM, b, g, st, more)
                    if un:
                        pe.wait_ge(sq_done, unit_no(*un) + 1)
                        aux_wait(aux_before(b, g, st, alone, "squares"))
                        nc.tensor.matmul(aux[:], small["head_ones"][:], squares[:], start=True, stop=True).then_inc(ss_mm, 1)
                    t = tile_at(FAST_TURN, b, g, st, more)
                    if t:
                        pe.wait_ge(x_normed, t[0] * NT + t[1] + 1)
                        aux_wait(aux_before(b, g, st, alone, "turn"))
                        for k in range(KT):
                            mm = nc.tensor.transpose(aux[:, k * P:(k + 1) * P], xt[t[1] % 2][:, k * P:(k + 1) * P], small["ident"][:])
                        mm.then_inc(turned, 1)

            def step(b, g, st, more, alone=False):
                l = g * STEPS + st
                if alone:
                    fill(b, g, st, more, 0, True)
                    fill(b, g, st, more, 1, True)
                    return
                if st == STEPS:
                    weigh(b, l - 1)
                    row_sums(b, NG * NH - 1, [(ss_moved, unit_no(b + 1, 0, 0) + (NU if more else 0)),
                                              (h_moved, (b + 1) * NT + (NT if more else 0)),
                                              (inverted, b * NG * NH + NG * NH - 1)])
                    return
                qk(b, g, st, 0)
                if l > NT and l % NT == 1:
                    row_sums(b, l // NT - 1, aux_before(b, g, st, False, "rows") if (g < NG - 1 or more) else
                             [(ss_moved, unit_no(b + 1, 0, 0)), (inverted, b * NG * NH + l // NT - 1)])
                fill(b, g, st, more, 0, False)
                qk(b, g, st, 1)
                fill(b, g, st, more, 1, False)
                if l > 0:
                    weigh(b, l - 1)

            stages(step, pe.Fori)

        @block.scalar
        def _(act):
            act.preload_act_table_set("natural_log_exp_and_others")

            def step(b, g, st, more, alone=False):
                l = g * STEPS + st
                for p in range(2):
                    if not alone and st < STEPS:
                        if l >= RING:
                            if p == 0:
                                act.wait_ge(pv_mm, b * BSTEPS + l - RING + 1)
                                act.wait_ge(add_v, b * NG * NH * ADDS + adds_before(l - RING))
                            else:
                                act.wait_ge(add_p, b * NG * NH * ADDS + adds_before(l - RING))
                        elif l == 0:
                            act.wait_ge(pv_mm, b * BSTEPS)
                            act.wait_ge(add_v, b * NG * NH * ADDS)
                            act.wait_ge(add_p, b * NG * NH * ADDS)
                        act.wait_ge(qk_mm, 2 * step_no(b, g, st) + p + 1)
                        nc.scalar.activation(probs[l % RING][:, 2 * p:2 * p + 2, :], scores[p][:], ACT.Exp,
                                             bias=small["shift"][:]).then_inc(exp_done, 1)
                    if p == 0:
                        un = units_at(SLOW_SUM, FAST_SUM, b, g, st, more)
                        if un:
                            n = unit_no(*un)
                            act.wait_ge(ss_moved, n + 1)
                            nc.scalar.activation(norms[:], norms[:], ACT.Ln, scale=LN_SCALE).then_inc(ln_done, 1)
                            act.wait_ge(ln_done, n + 1)
                            nc.scalar.activation(norms[:], norms[:], ACT.Exp, scale=-0.5, bias=small["ln_bias"][:]).then_inc(norm_done, 1)
                t = tile_at(FAST_TURN, b, g, st, more)
                if t:
                    act.wait_ge(h_moved, t[0] * NT + t[1] + 1)
                    nc.scalar.activation(h_hi[:, :, t[1] * P:(t[1] + 1) * P], h_full[:], ACT.Copy).then_inc(hi_done, 1)

            stages(step, act.Fori)

        @block.gpsimd
        def _(pool):
            def add(b, l):
                j = l % NT
                hh = b * NG * NH + l // NT
                if j == 0:
                    return
                pool.wait_ge(exp_done, 2 * (b * BSTEPS + l) + 2)
                if j == 1:
                    pool.wait_ge(rs_mm, hh)
                    a = probs[(l - 1) % RING][:, 2:4, :]
                else:
                    pool.wait_ge(add_p, hh * ADDS + j - 1)
                    a = sums[:, 2:4, :]
                nc.gpsimd.tensor_tensor(sums[:, 2:4, :], a, probs[l % RING][:, 2:4, :], ALU.add).then_inc(add_p, 1)

            def step(b, g, st, more, alone=False):
                l = g * STEPS + st
                un = units_at(SLOW_RAW, FAST_RAW, b, g, st, more)
                if un:
                    n, r = unit_no(*un), raw[un[2] % 2]
                    pool.wait_ge(raw_done, n + 1)
                    pool.wait_ge(ss_mm, n)
                    nc.gpsimd.tensor_tensor(squares[:], r[:], r[:], ALU.mult).then_inc(sq_done, 1)
                t = tile_at(FAST_STAT, b, g, st, more)
                if t:
                    n, k = t[0] * NT + t[1], t[1]
                    pool.wait_ge(stat_clamped, n + 1)
                    nc.gpsimd.tensor_tensor(x_inv[:, k:k + 1], x_sqc[:, k:k + 1], small["minus_half"][:], ALU.pow).then_inc(inv_done, 1)
                if not alone and l > 0:
                    add(b, l - 1)
                t = tile_at(FAST_TURN, b, g, st, more)
                if t:
                    c = slice(t[1] * P, (t[1] + 1) * P)
                    pool.wait_ge(hi_done, t[0] * NT + t[1] + 1)
                    nc.gpsimd.tensor_tensor(h_lo[:, :, c], h_full[:], full(h_hi[:, :, c]), ALU.subtract).then_inc(lo_done, 1)

            stages(step, pool.Fori)

        @block.vector
        def _(dve):
            dve.wait_ge(const_in, 32)

            def add(b, l):
                j = l % NT
                hh = b * NG * NH + l // NT
                if j == 0:
                    return
                dve.wait_ge(exp_done, 2 * (b * BSTEPS + l) + 1)
                if j == 1:
                    dve.wait_ge(rs_mm, hh)
                    a = probs[(l - 1) % RING][:, 0:2, :]
                else:
                    dve.wait_ge(add_v, hh * ADDS + j - 1)
                    a = sums[:, 0:2, :]
                nc.vector.tensor_tensor(sums[:, 0:2, :], a, probs[l % RING][:, 0:2, :], ALU.add).then_inc(add_v, 1)

            def output(b, hh):
                n = b * NG * NH + hh
                dve.wait_ge(rs_mm, n + 1)
                dve.wait_ge(o_done, n)
                nc.vector.reciprocal(inverse[:], aux[:]).then_inc(inverted, 1)
                dve.wait_ge(inverted, n + 1)
                dve.wait_ge(pv_mm, b * BSTEPS + (hh + 1) * NT)
                dve.wait_ge(o_stored, 16 * n)
                nc.vector.tensor_tensor(o_out[:], pv[hh % NH][:], inverse[:], ALU.mult).then_inc(o_done, 1)

            def step(b, g, st, more, alone=False):
                l = g * STEPS + st
                if l == 0:
                    dve.wait_ge(pv_mm, b * BSTEPS)
                    dve.wait_ge(v_moved, (b + 1) * NT)
                    for j in range(NT):
                        nc.vector.tensor_copy(v_now[:, j, :], v_next[:, j, :]).then_inc(v_copied, 1)
                un = units_at(SLOW_RAW, FAST_RAW, b, g, st, more)
                if un:
                    n = unit_no(*un)
                    which, _ = UNITS[un[2]]
                    col = (0 if which == "q" else NG) + un[1]
                    dve.wait_ge(unit_mm, n + 1)
                    if not alone or un[2] >= 2:
                        dve.wait_ge(part_lo, n - 1)
                    nc.vector.tensor_scalar(raw[un[2] % 2][:], gemm[:], qk_bias[:, col:col + 1], None, ALU.add).then_inc(raw_done, 1)
                t = tile_at(FAST_VOUT, b, g, st, more)
                if t:
                    dve.wait_ge(v_mm, t[0] * NT + t[1] + 1)
                    dve.wait_ge(v_copied, t[0] * NT)
                    nc.vector.tensor_tensor(v_next[:, t[1], :], gemm[:], v_bias[:], ALU.add).then_inc(v_moved, 1)
                t = tile_at(FAST_STAT, b, g, st, more)
                if t:
                    n, k = t[0] * NT + t[1], t[1]
                    if k == 0:
                        dve.wait_ge(mod_in, 16 * (t[0] + 1))
                        dve.wait_ge(h_moved, t[0] * NT)
                        nc.vector.tensor_scalar(scale1[:], mod[:, KT:2 * KT], 1.0, None, ALU.add).then_inc(mod_ready, 1)
                    dve.wait_ge(x_in[k % 2], 16 * (t[0] * (NT // 2) + k // 2 + 1))
                    dve.wait_ge(stat_clamped, n)
                    nc.vector.tensor_tensor_reduce(unused[:], xt[k % 2][:], xt[k % 2][:], 1.0, 0.0, ALU.mult, ALU.add,
                                                   x_sq[:, k:k + 1]).then_inc(stat, 1)
                    dve.wait_ge(stat, n + 1)
                    nc.vector.tensor_scalar(x_sqc[:, k:k + 1], x_sq[:, k:k + 1], EPS2, None, ALU.max).then_inc(stat_clamped, 1)
                if not alone and l > 0:
                    add(b, l - 1)
                if t:
                    dve.wait_ge(inv_done, n + 1)
                    nc.vector.tensor_scalar(xt[k % 2][:], xt[k % 2][:], x_inv[:, k:k + 1], small["x_gain"][:],
                                            ALU.mult, ALU.mult).then_inc(x_normed, 1)
                if not alone and l > NT and l % NT == 1:
                    output(b, l // NT - 1)
                if not alone and st == STEPS:
                    output(b, NG * NH - 1)
                un = units_at(SLOW_FIN, FAST_FIN, b, g, st, more)
                if un:
                    n, r = unit_no(*un), raw[un[2] % 2]
                    dve.wait_ge(norm_done, n + 1)
                    nc.vector.scalar_tensor_tensor(r[:], norms[:], 1.0 / EPS2 ** 0.5, r[:], ALU.min, ALU.mult).then_inc(normed, 1)
                    dve.wait_ge(normed, n + 1)
                    dve.wait_ge(parts_stored, 16 * n)
                    gain = small["s_gain"][:] if UNITS[un[2]][0] == "q" else 1.0
                    nc.vector.tensor_scalar(parts[:, 0, :], r[:], gain, None, ALU.mult).then_inc(part_hi, 1)
                    dve.wait_ge(part_hi, n + 1)
                    nc.vector.scalar_tensor_tensor(parts[:, 1, :], r[:], gain, full(parts[:, 0, :]), ALU.mult, ALU.subtract).then_inc(part_lo, 1)
                un = units_at(SLOW_SUM, FAST_SUM, b, g, st, more)
                if un:
                    dve.wait_ge(ss_mm, unit_no(*un) + 1)
                    dve.wait_ge(normed, unit_no(*un))
                    nc.vector.tensor_scalar(norms[:], aux[:], EPS2, None, ALU.max).then_inc(ss_moved, 1)
                t = tile_at(FAST_TURN, b, g, st, more)
                if t:
                    n = t[0] * NT + t[1]
                    dve.wait_ge(turned, n + 1)
                    dve.wait_ge(mod_ready, t[0] + 1)
                    dve.wait_ge(lo_done, n)
                    for k in range(KT):
                        mv = nc.vector.tensor_scalar(h_full[:, k, :], aux[:, k * P:(k + 1) * P], scale1[:, k:k + 1],
                                                     mod[:, k:k + 1], ALU.mult, ALU.add)
                    mv.then_inc(h_moved, 1)

            stages(step, dve.Fori)


def build_mlp(nc, small, dram):
    with ExitStack() as ctx:
        def sb(name, shape, dt=F32):
            return ctx.enter_context(nc.sbuf_tensor(name, shape, dt))

        def sem(name):
            return ctx.enter_context(nc.semaphore(name))

        wp = [sb(f"wp_{x}", [P, KT, D], F32R) for x in ("hi", "lo")]
        w1 = [sb(f"w1_{x}", [P, KT, FF], F32R) for x in ("hi", "lo")]
        w2 = [sb(f"w2_{x}", [P, NM, D], F32R) for x in ("hi", "lo")]
        z = [sb(f"z_{x}", [P, KT, CH], F32R) for x in ("hi", "lo")]
        act_full = [sb(f"act_full{s}", [P, CH]) for s in range(2)]
        act_parts = [sb(f"act_parts{s}", [P, 2, CH], F32R) for s in range(2)]
        heads = [sb(f"heads{s}", [P, KT, P]) for s in range(2)]
        heads_parts = sb("heads_parts", [P, 2, KT, P], F32R)
        y = sb("y", [P, CT, D])
        y_next = sb("y_next", [P, CT, D])
        x_tile = sb("x_tile", [P, D])
        y_norm = [sb(f"y_norm{s}", [P, D]) for s in range(2)]
        z_full = [sb(f"z_full{s}", [P, KT, P]) for s in range(2)]
        result = [sb(f"result{s}", [P, D]) for s in range(2)]
        gate1, gate2 = sb("gate1", [P, D]), sb("gate2", [P, D])
        p_bias, f2_bias = sb("p_bias", [P, D]), sb("f2_bias", [P, D])
        f1_bias = sb("f1_bias", [P, NM])
        gated_bias = sb("gated_bias", [P, D])
        mod = sb("mod_mlp", [P, 2 * KT])
        scale1 = sb("scale1_mlp", [P, KT])
        y_sq, y_sqc, y_inv = sb("y_sq", [P, CT]), sb("y_sqc", [P, CT]), sb("y_inv", [P, CT])
        WS = CT
        stage = [y[:, s, :] for s in range(WS)]

        acc = [ctx.enter_context(nc.psum_tensor(f"acc{t}", [P, D], F32)) for t in range(CT)]
        up = [ctx.enter_context(nc.psum_tensor(f"up{s}", [P, CH], F32)) for s in range(2)]
        proj = ctx.enter_context(nc.psum_tensor("proj", [P, D], F32))
        turn = ctx.enter_context(nc.psum_tensor("turn", [P, KT * P], F32))

        const_in = sem("const_in_mlp")
        w_in = [sem(f"w_in{s}") for s in range(WS)]
        w_high, w_low = sem("w_high"), sem("w_low")
        x_in, gate1_in, gate2_in, mod_in = sem("x_in_mlp"), sem("gate1_in"), sem("gate2_in"), sem("mod_in_mlp")
        heads_hi, heads_lo, proj_mm, proj_moved = sem("heads_hi"), sem("heads_lo"), sem("proj_mm"), sem("proj_moved")
        heads_in = [sem(f"heads_in{s}") for s in range(2)]
        y_taken = sem("y_taken")
        y_chain, y_done, y_stat, y_clamped, y_inverse = sem("y_chain"), sem("y_done"), sem("y_stat"), sem("y_clamped"), sem("y_inverse")
        mod_ready, y_normed, turned, z_moved, z_hi, z_lo = (sem(x) for x in ("mod_ready_mlp", "y_normed", "turned_mlp", "z_moved", "z_hi_done", "z_lo_done"))
        up_mm, gelu_done, act_hi, act_lo = sem("up_mm"), sem("gelu_done"), sem("act_hi"), sem("act_lo")
        down_mm, acc_mm, acc_moved, out_done = (sem(x) for x in ("down_mm", "acc_mm", "acc_moved", "out_done"))
        bias_gated, y_biased = sem("bias_gated"), sem("y_biased")
        out_stored = [sem(f"out_stored{s}") for s in range(2)]
        block = ctx.enter_context(nc.Block())

        pieces = [(wp, slice(None), k) for k in range(KT)]
        for m in range(NM):
            pieces += [(w1, m, None), (w2, None, m)]
        NW = len(pieces)
        EARLY = KT + 8

        def piece(parts_of, which):
            w, a, b = parts_of
            if w is w1:
                return w[which][:, :, a * P:(a + 1) * P]
            return w[which][:, b, :]

        def piece_shape(n, ap):
            return ap.rearrange("p (k m) -> p k m", k=KT) if pieces[n][0] is w1 else ap

        SPLIT = {1 + 3 * t: t for t in range(CT)}
        PROJ = {2 + 3 * t: t for t in range(CT)}
        MAKE = {3 + 3 * t: t for t in range(CT)}
        NORM = 13
        BIAS = 2
        LAG = 2

        def chunks(prepare, turn_tile, mlp, finish, fori, first=None):
            if first:
                first()
            else:
                for m in range(NM):
                    prepare(0, m)
                for t in range(CT):
                    turn_tile(0, t)
            with fori(0, NC - 1) as c:
                for m in range(NM):
                    mlp(c, m)
                    prepare(c + 1, m)
                for t in range(CT):
                    turn_tile(c + 1, t)
                for t in range(CT):
                    finish(c, t)
            for m in range(NM):
                mlp(NC - 1, m)
            for t in range(CT):
                finish(NC - 1, t)

        @block.sync
        def _(sp):
            sp.dma_start(f1_bias[:], dram["bfc1T"]).then_inc(const_in, 16)
            for tile, name in ((p_bias, "bproj"), (f2_bias, "bfc2")):
                sp.dma_start(tile[:], dram[name].rearrange("(a n) -> a n", a=1).broadcast_to([P, D])).then_inc(const_in, 16)

            def prepare(c, m):
                if m == 0:
                    sp.wait_ge(y_done, CT * c)
                    sp.dma_start(gate1[:], dram["ada_c"][bass.ts(c, 1), 2 * D:3 * D].broadcast_to([P, D])).then_inc(gate1_in, 16)
                    sp.wait_ge(z_moved, CT * c)
                    sp.dma_start(mod[:], dram["ada_c"][c, 3 * D:5 * D].rearrange("(j p) -> p j", p=P),
                                 allow_slow_non_contiguous=True).then_inc(mod_in, 16)
                if m + 1 in SPLIT:
                    t = SPLIT[m + 1]
                    sp.wait_ge(heads_lo, CT * c + max(0, t - 1))
                    sp.dma_start(heads[t % 2][:], dram["heads_out"][c, :, t * P:(t + 1) * P].rearrange("(k p) n -> p k n", p=P)).then_inc(heads_in[t % 2], 16)
                    sp.wait_ge(y_done, CT * c + t)
                    sp.dma_start(x_tile[:], dram["x"].rearrange("b (h n) d -> (b h) n d", h=NH)[c, t * P:(t + 1) * P, :]).then_inc(x_in, 16)

            def mlp(c, m):
                if m == 0:
                    sp.wait_ge(out_done, CT * c)
                    sp.wait_ge(bias_gated, c)
                    sp.dma_start(gate2[:], dram["ada_c"][bass.ts(c, 1), 5 * D:6 * D].broadcast_to([P, D])).then_inc(gate2_in, 16)

            def finish(c, t):
                sp.wait_ge(out_done, CT * c + t + 1)
                sp.dma_start(dram["out"].rearrange("b (h n) d -> (b h) n d", h=NH)[c, t * P:(t + 1) * P, :],
                             result[t % 2][:]).then_inc(out_stored[t % 2], 16)

            chunks(prepare, lambda c, t: None, mlp, finish, sp.Fori)
            for s in range(2):
                sp.wait_ge(out_stored[s], 16 * NC * CT // 2)

        @block.scalar
        def _(act):
            act.preload_act_table(ACT.Gelu_apprx_tanh)
            w_dram = {id(wp): dram["wprojT"], id(w1): dram["wfc1T"], id(w2): dram["wfc2T"]}

            def load(n):
                w, a, b = pieces[n]
                src = w_dram[id(w)].rearrange("(k p) n -> p k n", p=P)
                src = src[:, :, a * P:(a + 1) * P] if w is w1 else src[:, b, :]
                if n >= WS:
                    act.wait_ge(w_low, n - WS + 1)
                act.dma_start(piece_shape(n, stage[n % WS]), src).then_inc(w_in[n % WS], 16)

            for n in range(WS):
                load(n)

            def split_high(lo, hi):
                for n in range(lo, hi):
                    act.wait_ge(w_in[n % WS], 16 * (n // WS + 1))
                    nc.scalar.activation(piece(pieces[n], 0), piece_shape(n, stage[n % WS]), ACT.Copy).then_inc(w_high, 1)
                    if n + WS - 1 < NW and n >= 1:
                        load(n + WS - 1)

            def turn_tile(c, t):
                act.wait_ge(up_mm, NM * c)
                act.wait_ge(z_moved, CT * c + t + 1)
                nc.scalar.activation(z[0][:, :, t * P:(t + 1) * P], z_full[t % 2][:], ACT.Copy).then_inc(z_hi, 1)

            def first():
                split_high(0, EARLY)
                for t in range(CT):
                    turn_tile(0, t)
                split_high(EARLY, NW)
                act.wait_ge(const_in, 48)

            def mlp(c, m):
                if True:
                    n = NM * c + m
                    act.wait_ge(up_mm, n + 1)
                    if m >= 2:
                        act.wait_ge(act_lo, n - 1)
                    else:
                        act.wait_ge(act_lo, NM * c)
                    nc.scalar.activation(act_full[m % 2][:], up[m % 2][:], ACT.Gelu_apprx_tanh, bias=f1_bias[:, m:m + 1]).then_inc(gelu_done, 1)
                    act.wait_ge(gelu_done, n + 1)
                    if m >= 2:
                        act.wait_ge(down_mm, (NM - 1) * c + m - 1)
                    else:
                        act.wait_ge(acc_mm, CT * c)
                    nc.scalar.activation(act_parts[m % 2][:, 0, :], act_full[m % 2][:], ACT.Copy).then_inc(act_hi, 1)

            chunks(lambda c, m: None, turn_tile, mlp, lambda c, t: None, act.Fori, first)

        @block.gpsimd
        def _(pool):
            pool.wait_ge(const_in, 48)

            def prepare(c, m):
                if m == NORM:
                    pool.wait_ge(y_clamped, c + 1)
                    half = small["minus_half"]
                    for t in range(CT):
                        pw = nc.gpsimd.tensor_tensor(y_inv[:, t:t + 1], y_sqc[:, t:t + 1], half[:], ALU.pow)
                    pw.then_inc(y_inverse, 1)

            def turn_tile(c, t):
                r = slice(t * P, (t + 1) * P)
                pool.wait_ge(z_hi, CT * c + t + 1)
                nc.gpsimd.tensor_tensor(z[1][:, :, r], z_full[t % 2][:], full(z[0][:, :, r]), ALU.subtract).then_inc(z_lo, 1)

            def mlp(c, m):
                if m == BIAS:
                    pool.wait_ge(gate2_in, 16 * (c + 1))
                    nc.gpsimd.tensor_tensor(gated_bias[:], gate2[:], f2_bias[:], ALU.mult).then_inc(bias_gated, 1)
                if BIAS < m <= BIAS + CT:
                    t = m - BIAS - 1
                    pool.wait_ge(bias_gated, c + 1)
                    pool.wait_ge(y_taken, c + 1)
                    nc.gpsimd.tensor_tensor(y[:, t, :], y[:, t, :], gated_bias[:], ALU.add).then_inc(y_biased, 1)
                pool.wait_ge(act_hi, NM * c + m + 1)
                nc.gpsimd.tensor_tensor(act_parts[m % 2][:, 1, :], act_full[m % 2][:], full(act_parts[m % 2][:, 0, :]), ALU.subtract).then_inc(act_lo, 1)

            chunks(prepare, turn_tile, mlp, lambda c, t: None, pool.Fori)

        @block.tensor
        def _(pe):
            pairs = ((0, 0), (0, 1), (1, 0))

            def prepare(c, m):
                if m in PROJ:
                    t = PROJ[m]
                    pe.wait_ge(heads_lo, CT * c + t + 1)
                    pe.wait_ge(proj_moved, CT * c + t)
                    if isinstance(c, int) and t == 0:
                        pe.wait_ge(w_low, KT)
                    for k in range(KT):
                        for i, (a, b) in enumerate(pairs):
                            mm = nc.tensor.matmul(proj[:], heads_parts[:, b, k, :], wp[a][:, k, :],
                                                  start=(k == 0 and i == 0), stop=(k == KT - 1 and i == 2))
                    mm.then_inc(proj_mm, 1)

            def turn_tile(c, t):
                pe.wait_ge(y_normed, CT * c + t + 1)
                pe.wait_ge(z_moved, CT * c + t)
                for k in range(KT):
                    mm = nc.tensor.transpose(turn[:, k * P:(k + 1) * P], y_norm[t % 2][:, k * P:(k + 1) * P], small["ident"][:])
                mm.then_inc(turned, 1)

            def down(c, m, tiles):
                if tiles[0] == 0:
                    pe.wait_ge(act_lo, NM * c + m + 1)
                    pe.wait_ge(w_low, KT + 2 * m + 2)
                for t in tiles:
                    if m == 0:
                        pe.wait_ge(acc_moved, CT * c)
                    for i, (a, b) in enumerate(pairs):
                        mm = nc.tensor.matmul(acc[t][:], act_parts[m % 2][:, b, t * P:(t + 1) * P], w2[a][:, m, :],
                                              start=(m == 0 and i == 0), stop=(m == NM - 1 and i == 2))
                    if m == NM - 1:
                        mm.then_inc(acc_mm, 1)
                    elif t == CT - 1:
                        mm.then_inc(down_mm, 1)

            def lift(c, m):
                n = NM * c + m
                if m == 0:
                    pe.wait_ge(z_lo, CT * (c + 1))
                pe.wait_ge(w_low, KT + 2 * m + 1)
                pe.wait_ge(gelu_done, n - 1 if m >= 2 else NM * c)
                for k in range(KT):
                    for i, (a, b) in enumerate(pairs):
                        mm = nc.tensor.matmul(up[m % 2][:], w1[a][:, k, m * P:(m + 1) * P], z[b][:, k, :],
                                              start=(k == 0 and i == 0), stop=(k == KT - 1 and i == 2))
                mm.then_inc(up_mm, 1)

            def chunk(c, more):
                first, second = (0, 1), (2, 3)
                for m in range(NM - 1):
                    lift(c, m)
                    if m >= LAG:
                        down(c, m - LAG, first + second)
                    if more:
                        prepare(c + 1, m)
                lift(c, NM - 1)
                for m, tiles, t in ((NM - 3, first, 0), (NM - 3, second, 1), (NM - 2, first, 2), (NM - 2, second, 3)):
                    if more:
                        turn_tile(c + 1, t)
                    down(c, m, tiles)
                down(c, NM - 1, first + second)

            for m in range(NM):
                prepare(0, m)
            for t in range(CT):
                turn_tile(0, t)
            with pe.Fori(0, NC - 1) as c:
                chunk(c, True)
            chunk(NC - 1, False)

        @block.vector
        def _(dve):
            def split_low(lo, hi):
                for n in range(lo, hi):
                    dve.wait_ge(w_high, n + 1)
                    nc.vector.tensor_tensor(piece(pieces[n], 1), piece_shape(n, stage[n % WS]), full(piece(pieces[n], 0)),
                                            ALU.subtract).then_inc(w_low, 1)

            def prepare(c, m):
                if m in SPLIT:
                    n = CT * c + SPLIT[m]
                    t = SPLIT[m]
                    dve.wait_ge(heads_in[t % 2], 16 * (c * (CT // 2) + t // 2 + 1))
                    dve.wait_ge(proj_mm, n)
                    nc.vector.tensor_copy(heads_parts[:, 0, :, :], heads[t % 2][:]).then_inc(heads_hi, 1)
                    dve.wait_ge(heads_hi, n + 1)
                    nc.vector.tensor_tensor(heads_parts[:, 1, :, :], heads[t % 2][:], full(heads_parts[:, 0, :, :]), ALU.subtract).then_inc(heads_lo, 1)
                if m in MAKE:
                    t = MAKE[m]
                    n = CT * c + t
                    yt = y_next[:, t, :]
                    dve.wait_ge(proj_mm, n + 1)
                    dve.wait_ge(y_taken, c)
                    nc.vector.tensor_tensor(yt, proj[:], p_bias[:], ALU.add).then_inc(proj_moved, 1)
                    if t == 0:
                        dve.wait_ge(gate1_in, 16 * (c + 1))
                    dve.wait_ge(proj_moved, n + 1)
                    nc.vector.tensor_tensor(yt, yt, gate1[:], ALU.mult).then_inc(y_chain, 1)
                    dve.wait_ge(y_chain, n + 1)
                    dve.wait_ge(x_in, 16 * (n + 1))
                    nc.vector.tensor_tensor(yt, yt, x_tile[:], ALU.add).then_inc(y_done, 1)
                    dve.wait_ge(y_done, n + 1)
                    dve.wait_ge(y_stat, n)
                    dve.wait_ge(y_clamped, c)
                    nc.vector.tensor_tensor_reduce(y_norm[t % 2][:], yt, yt, 1.0, 0.0, ALU.mult, ALU.add, y_sq[:, t:t + 1]).then_inc(y_stat, 1)
                if m == NORM:
                    dve.wait_ge(y_stat, CT * (c + 1))
                    dve.wait_ge(y_inverse, c)
                    dve.wait_ge(z_moved, CT * c)
                    nc.vector.tensor_scalar(y_sqc[:], y_sq[:], EPS2, None, ALU.max).then_inc(y_clamped, 1)
                    dve.wait_ge(mod_in, 16 * (c + 1))
                    nc.vector.tensor_scalar(scale1[:], mod[:, KT:2 * KT], 1.0, None, ALU.add).then_inc(mod_ready, 1)

            def normalise(c, t):
                nc.vector.tensor_scalar(y_norm[t % 2][:], y_next[:, t, :], y_inv[:, t:t + 1], small["y_gain"][:],
                                        ALU.mult, ALU.mult).then_inc(y_normed, 1)

            def turn_tile(c, t):
                n = CT * c + t
                if t == 0:
                    dve.wait_ge(y_inverse, c + 1)
                    dve.wait_ge(mod_ready, c + 1)
                    normalise(c, 0)
                    normalise(c, 1)
                dve.wait_ge(turned, n + 1)
                if t + 2 < CT:
                    normalise(c, t + 2)
                dve.wait_ge(z_lo, CT * c + max(0, t - 1))
                for k in range(KT):
                    mv = nc.vector.tensor_scalar(z_full[t % 2][:, k, :], turn[:, k * P:(k + 1) * P], scale1[:, k:k + 1], mod[:, k:k + 1],
                                                 ALU.mult, ALU.add)
                mv.then_inc(z_moved, 1)

            def take_over(c):
                dve.wait_ge(out_done, CT * (c + 1))
                nc.vector.tensor_copy(y[:], y_next[:]).then_inc(y_taken, 1)

            def first():
                split_low(0, KT)
                dve.wait_ge(const_in, 48)
                for m in range(NM):
                    prepare(0, m)
                split_low(KT, EARLY)
                for t in range(CT):
                    turn_tile(0, t)
                split_low(EARLY, NW)
                dve.wait_ge(w_low, NW)
                take_over(-1)

            def finish(c, t):
                n = CT * c + t
                r = result[t % 2]
                dve.wait_ge(acc_mm, n + 1)
                dve.wait_ge(out_stored[t % 2], 16 * (CT // 2 * c + t // 2))
                if t == 0:
                    dve.wait_ge(gate2_in, 16 * (c + 1))
                    dve.wait_ge(y_biased, CT * (c + 1))
                nc.vector.tensor_tensor(r[:], acc[t][:], gate2[:], ALU.mult).then_inc(acc_moved, 1)
                dve.wait_ge(acc_moved, n + 1)
                nc.vector.tensor_tensor(r[:], r[:], y[:, t, :], ALU.add).then_inc(out_done, 1)
                if t == CT - 1 and not isinstance(c, int):
                    take_over(c)

            chunks(prepare, turn_tile, lambda c, m: None, finish, dve.Fori, first)


def program(nc, x, cT, wadaT, bada, wqkvT, bqkv, bqkT, wprojT, bproj, wfc1T, bfc1T, wfc2T, bfc2, g1, g2, gq, gk, out):
    dram = dict(x=x, cT=cT, wadaT=wadaT, bada=bada, wqkvT=wqkvT, bqkv=bqkv, bqkT=bqkT, wprojT=wprojT, bproj=bproj,
                wfc1T=wfc1T, bfc1T=bfc1T, wfc2T=wfc2T, bfc2=bfc2, g1=g1, g2=g2, gq=gq, gk=gk, out=out)
    dram["ada_b"] = nc.dram_tensor("ada_b", [B, 6 * D], F32, kind="Internal").ap()
    dram["ada_c"] = nc.dram_tensor("ada_c", [NC, 6 * D], F32, kind="Internal").ap()
    dram["parts"] = nc.dram_tensor("parts_scratch", [NU, 2, P, CH], F32, kind="Internal").ap()
    dram["heads_out"] = nc.dram_tensor("heads_out", [NC, D, CH], F32, kind="Internal").ap()
    with ExitStack() as ctx:
        small = {}
        for name, cols in (("ident", P), ("head_ones", P), ("ones", DH), ("minus_half", 1), ("ln_bias", 1), ("shift", 1),
                           ("x_gain", 1), ("y_gain", 1), ("s_gain", 1)):
            small[name] = ctx.enter_context(nc.sbuf_tensor(name, [P, cols], F32))
        with ExitStack() as weights:
            wq_hi = weights.enter_context(nc.sbuf_tensor("wqkv_hi", [P, KT, 3 * D], F32R))
            wq_lo = weights.enter_context(nc.sbuf_tensor("wqkv_lo", [P, KT, 3 * D], F32R))
            build_setup(nc, small, dram, wq_hi, wq_lo)
            build_attention(nc, small, dram, wq_hi, wq_lo)
        build_mlp(nc, small, dram)


def kernel(x, cond_1024, L0_cond_g1, L0_cond_g2, L0_cond_gq, L0_cond_gk, L0_cond_Wqkv, L0_cond_bqkv, L0_cond_Wproj,
           L0_cond_bproj, L0_cond_Wfc1, L0_cond_bfc1, L0_cond_Wfc2, L0_cond_bfc2, L0_cond_Wada, L0_cond_bada):
    import numpy as np
    import concourse.bacc as bacc
    from concourse.bass_utils import run_bass_kernel_spmd

    def turned(a):
        return np.ascontiguousarray(np.asarray(a).T)

    bqkv = np.ascontiguousarray(L0_cond_bqkv)
    arrays = {
        "x": np.ascontiguousarray(x), "cT": turned(cond_1024), "wadaT": turned(L0_cond_Wada),
        "bada": np.ascontiguousarray(L0_cond_bada), "wqkvT": turned(L0_cond_Wqkv), "bqkv": bqkv,
        "bqkT": turned(bqkv[:2 * D].reshape(2 * NG, P)), "wprojT": turned(L0_cond_Wproj),
        "bproj": np.ascontiguousarray(L0_cond_bproj), "wfc1T": turned(L0_cond_Wfc1),
        "bfc1T": turned(np.asarray(L0_cond_bfc1).reshape(NM, P)), "wfc2T": turned(L0_cond_Wfc2),
        "bfc2": np.ascontiguousarray(L0_cond_bfc2), "g1": np.ascontiguousarray(L0_cond_g1),
        "g2": np.ascontiguousarray(L0_cond_g2), "gq": np.ascontiguousarray(L0_cond_gq), "gk": np.ascontiguousarray(L0_cond_gk),
    }
    nc = bacc.Bacc("TRN2", target_bir_lowering=False, num_devices=1, dynamic_dma_scratch_size=1024)
    args = [nc.dram_tensor(f"in_{n}", a.shape, mybir.dt.from_np(a.dtype), kind="ExternalInput").ap() for n, a in arrays.items()]
    args.append(nc.dram_tensor("out", (B, T, D), F32, kind="ExternalOutput").ap())
    program(nc, *args)
    r = run_bass_kernel_spmd(nc, [{f"in_{n}": a for n, a in arrays.items()}], core_ids=[0])
    return r.results[0]["out"]
```

```python
from contextlib import ExitStack

import concourse.bass as bass
from concourse import mybir

F32 = mybir.dt.float32
F32R = mybir.dt.float32r
ALU = mybir.AluOpType
ACT = mybir.ActivationFunctionType

P = 128
B, T, D = 4, 1024, 512
H, DH = 16, 32
FF = 4 * D
KT = D // P
HG = P // DH
NG = H // HG
CH = 512
NH = T // CH
NT = T // P
CT = CH // P
NC = B * NH
STEPS = NH * NT
BSTEPS = NG * STEPS
ADDS = NT - 1
NM = FF // P
RING = 3
EPS2 = 1e-24
LN_SCALE = 2.0 ** 16
LN_BIAS = 8 * 0.6931471805599453
SAFE = 64.0

UNITS = (("k", 0), ("q", 0), ("k", 1), ("q", 1))
NU = len(UNITS)
BUNITS = NG * NU

SLOW_GEMM = {3 * u + i: (u, i) for u in range(NU) for i in range(3)}
SLOW_END = {3 * u + 2: u for u in range(NU)}
FAST = {3: ("v", 0), 4: ("v", 1), 5: ("v", 2), 6: ("u", 0), 7: ("u", 1), 8: ("v", 3), 9: ("v", 4),
        10: ("u", 2), 11: ("u", 3), 12: ("v", 5), 13: ("v", 6), 14: ("v", 7)}
FAST_END = {s: x[1] for s, x in FAST.items() if x[0] == "u"}
FAST_V = {s: x[1] for s, x in FAST.items() if x[0] == "v"}


def later(table, steps):
    return {s + steps: x for s, x in table.items()}


SLOW_RAW, FAST_RAW = later(SLOW_END, 1), later(FAST_END, 1)
SLOW_SUM, FAST_SUM = later(SLOW_END, 2), later(FAST_END, 2)
SLOW_INV, FAST_INV = later(SLOW_END, 3), later(FAST_END, 3)
SLOW_FIN, FAST_FIN = later(SLOW_END, 4), later(FAST_END, 4)
FAST_VOUT = later(FAST_V, 1)
FAST_STAT = {t - 1: t for t in range(NT)}
FAST_TURN = later(FAST_STAT, 1)
FAST_HOUT = later(FAST_STAT, 2)
FAST_SPLIT = later(FAST_STAT, 3)
AHEAD = 3
XS = 3
ROWS, COMPACT, INVERT, INVERTED, SPREAD, OUT = 1, 2, 4, 4, 5, 7
SEEN = HG * CH // P


def full(ap):
    return ap.bitcast(F32)


def build_setup(nc, small, dram, wq_hi, wq_lo):
    with ExitStack() as ctx:
        def sb(name, shape, dt=F32):
            return ctx.enter_context(nc.sbuf_tensor(name, shape, dt))

        def sem(name):
            return ctx.enter_context(nc.semaphore(name))

        NA = 6 * D // CH
        wada = sb("wada", [P, KT, 6 * D])
        wstage = sb("wstage", [P, KT, 3 * D])
        ada = sb("ada", [B, 6 * D])
        bada = sb("bada_rows", [B, 6 * D])
        cT = sb("cT", [P, KT, B])
        ce = sb("c_exp", [P, KT, B])
        cs = sb("c_sigmoid", [P, KT, B])
        silu = sb("silu_c", [P, KT, B])
        gains = sb("gains", [P, 4])
        tmp = sb("tmp", [P, 4])
        pa = [ctx.enter_context(nc.psum_tensor(f"pa{n}", [P, CH], F32)) for n in range(NA)]

        c_in, bias_in, gain_in = sem("c_in"), sem("bias_in"), sem("gain_in")
        wada_in = [sem(f"wada_in{n}") for n in range(NA)]
        wqkv_in = [sem(f"wqkv_in{n}") for n in range(3)]
        exp_c, sig_c, silu_c = sem("exp_c"), sem("sig_c"), sem("silu_c_done")
        ada_mm, ada_out, ada_stored = sem("ada_mm"), sem("ada_out"), sem("ada_stored")
        high, low, gain_chain, zeroed, masks = sem("high"), sem("low"), sem("gain_chain"), sem("zeroed"), sem("masks")
        block = ctx.enter_context(nc.Block())

        @block.sync
        def _(sp):
            sp.dma_start(cT[:], dram["cT"].rearrange("(k p) b -> p k b", p=P)).then_inc(c_in, 16)
            for n, g in enumerate(("g1", "g2", "gq", "gk")):
                sp.dma_start(gains[:, n:n + 1], dram[g].rearrange("(a n) -> a n", a=1).broadcast_to([P, 1])).then_inc(gain_in, 16)
            sp.dma_start(bada[:], dram["bada"].rearrange("(a n) -> a n", a=1).broadcast_to([B, 6 * D])).then_inc(bias_in, 16)
            for n in range(NA):
                sp.dma_start(wada[:, :, n * CH:(n + 1) * CH],
                             dram["wadaT"][:, n * CH:(n + 1) * CH].rearrange("(k p) n -> p k n", p=P)).then_inc(wada_in[n], 16)
            sp.wait_ge(ada_out, NA)
            sp.dma_start(dram["ada_b"], ada[:]).then_inc(ada_stored, 16)
            for h in range(NH):
                sp.dma_start(dram["ada_c"].rearrange("(b h) n -> b h n", h=NH)[:, h, :], ada[:]).then_inc(ada_stored, 16)
            sp.wait_ge(ada_stored, 16 * (1 + NH))

        @block.gpsimd
        def _(pool):
            ident, bones = small["ident"], small["head_ones"]
            pool.memset(ident[:], 0.0).then_inc(zeroed, 1)
            pool.memset(bones[:], 0.0).then_inc(zeroed, 1)
            pool.memset(small["ones"][:], 1.0).then_inc(masks, 1)
            pool.memset(small["minus_half"][:], -0.5).then_inc(masks, 1)
            pool.memset(small["ln_bias"][:], LN_BIAS).then_inc(masks, 1)
            pool.wait_ge(zeroed, 2)
            pool.affine_select(out=ident[:], in_=ident[:], compare_op=ALU.not_equal, fill=1.0, base=0,
                               pattern=[[-1, P]], channel_multiplier=1).then_inc(masks, 1)
            for h in range(HG):
                r = slice(h * DH, (h + 1) * DH)
                pool.wait_ge(masks, 4 + h)
                pool.memset(bones[r, r], 1.0).then_inc(masks, 1)

        @block.scalar
        def _(act):
            for n in range(3):
                act.dma_start(wstage[:, :, n * D:(n + 1) * D],
                              dram["wqkvT"][:, n * D:(n + 1) * D].rearrange("(k p) n -> p k n", p=P)).then_inc(wqkv_in[n], 16)
            act.preload_act_table_set("natural_log_exp_and_others")
            act.wait_ge(c_in, 16)
            nc.scalar.activation(ce[:], cT[:], ACT.Exp, scale=-1.0).then_inc(exp_c, 1)
            for n in range(3):
                s = slice(n * D, (n + 1) * D)
                act.wait_ge(wqkv_in[n], 16)
                nc.scalar.activation(wq_hi[:, :, s], wstage[:, :, s], ACT.Copy).then_inc(high, 1)

        @block.tensor
        def _(pe):
            pe.wait_ge(silu_c, 1)
            for n in range(NA):
                pe.wait_ge(wada_in[n], 16)
                for k in range(KT):
                    mm = nc.tensor.matmul(pa[n][0:B, :], silu[:, k, :], wada[:, k, n * CH:(n + 1) * CH],
                                          start=(k == 0), stop=(k == KT - 1))
                mm.then_inc(ada_mm, 1)

        @block.vector
        def _(dve):
            dve.wait_ge(exp_c, 1)
            nc.vector.tensor_scalar(ce[:], ce[:], 1.0, None, ALU.add).then_inc(sig_c, 1)
            dve.wait_ge(sig_c, 1)
            nc.vector.reciprocal(cs[:], ce[:]).then_inc(sig_c, 1)
            dve.wait_ge(sig_c, 2)
            nc.vector.tensor_tensor(silu[:], cT[:], cs[:], ALU.mult).then_inc(silu_c, 1)
            dve.wait_ge(gain_in, 64)
            nc.vector.tensor_scalar(small["x_gain"][:], gains[:, 0:1], float(D) ** 0.5, None, ALU.mult).then_inc(gain_chain, 1)
            nc.vector.tensor_scalar(small["y_gain"][:], gains[:, 1:2], float(D) ** 0.5, None, ALU.mult).then_inc(gain_chain, 1)
            nc.vector.tensor_scalar(small["s_gain"][:], gains[:, 2:3], gains[:, 3:4], float(DH) ** 0.5,
                                    ALU.mult, ALU.mult).then_inc(gain_chain, 1)
            dve.wait_ge(gain_chain, 3)
            nc.vector.tensor_scalar(tmp[:, 0:1], small["s_gain"][:], -1.0, None, ALU.mult).then_inc(gain_chain, 1)
            dve.wait_ge(gain_chain, 4)
            nc.vector.tensor_tensor(tmp[:, 1:2], tmp[:, 0:1], small["s_gain"][:], ALU.max).then_inc(gain_chain, 1)
            dve.wait_ge(gain_chain, 5)
            nc.vector.tensor_scalar(tmp[:, 2:3], tmp[:, 1:2], -1.0, SAFE, ALU.mult, ALU.add).then_inc(gain_chain, 1)
            dve.wait_ge(gain_chain, 6)
            nc.vector.tensor_scalar(small["shift"][:], tmp[:, 2:3], 0.0, None, ALU.min).then_inc(gain_chain, 1)
            for n in range(3):
                s = slice(n * D, (n + 1) * D)
                dve.wait_ge(high, n + 1)
                nc.vector.tensor_tensor(wq_lo[:, :, s], wstage[:, :, s], full(wq_hi[:, :, s]), ALU.subtract).then_inc(low, 1)
            dve.wait_ge(bias_in, 16)
            for n in range(NA):
                dve.wait_ge(ada_mm, n + 1)
                s = slice(n * CH, (n + 1) * CH)
                nc.vector.tensor_tensor(ada[:, s], pa[n][0:B, :], bada[:, s], ALU.add).then_inc(ada_out, 1)


def build_attention(nc, small, dram, wq_hi, wq_lo):
    with ExitStack() as ctx:
        def sb(name, shape, dt=F32):
            return ctx.enter_context(nc.sbuf_tensor(name, shape, dt))

        def sem(name):
            return ctx.enter_context(nc.semaphore(name))

        h_hi = sb("h_hi", [P, KT, T], F32R)
        h_lo = sb("h_lo", [P, KT, T], F32R)
        v_next = sb("v_next", [P, NT, D])
        v_now = sb("v_now", [P, NT, D])
        k_stack = [sb(f"k_stack{s}", [P, HG, T], F32R) for s in range(2)]
        q_stack = [sb(f"q_stack{h}", [P, HG, CH], F32R) for h in range(NH)]
        probs = [sb(f"probs{s}", [P, HG, CH]) for s in range(RING)]
        sums = sb("sums", [P, HG, CH])
        raw = [sb(f"raw{s}", [P, CH]) for s in range(2)]
        squares = sb("squares", [P, CH])
        norms = sb("norms", [P, CH])
        parts = sb("parts", [P, 2, CH], F32R)
        inverse = sb("inverse", [P, CH])
        compact = sb("compact", [P, SEEN])
        o_out = sb("o_out", [P, CH])
        xt = [sb(f"xt{s}", [P, D]) for s in range(XS)]
        unused = sb("unused", [P, D])
        h_full = sb("h_full", [P, KT, P])
        v_bias = sb("v_bias", [P, D])
        qk_bias = sb("qk_bias", [P, 2 * NG])
        mod = sb("mod", [P, 2 * KT])
        scale1 = sb("scale1", [P, KT])
        x_sq = sb("x_sq", [P, NT])
        x_sqc = sb("x_sqc", [P, NT])
        x_inv = sb("x_inv", [P, NT])

        scores = [ctx.enter_context(nc.psum_tensor(f"scores{p}", [P, 2, CH], F32)) for p in range(2)]
        pv = [ctx.enter_context(nc.psum_tensor(f"pv{h}", [P, CH], F32)) for h in range(NH)]
        gemm = ctx.enter_context(nc.psum_tensor("gemm", [P, CH], F32))
        aux = ctx.enter_context(nc.psum_tensor("aux", [P, CH], F32))

        const_in = sem("const_in")
        mod_in, mod_ready = sem("mod_in"), sem("mod_ready")
        x_in = [sem(f"x_in{s}") for s in range(XS)]
        stat, stat_clamped, inv_done, x_normed = sem("stat"), sem("stat_clamped"), sem("inv_done"), sem("x_normed")
        turned, h_moved, hi_done, lo_done = sem("turned"), sem("h_moved"), sem("hi_done"), sem("lo_done")
        v_mm, v_moved, v_copied = sem("v_mm"), sem("v_moved"), sem("v_copied")
        unit_mm, raw_done, sq_done = sem("unit_mm"), sem("raw_done"), sem("sq_done")
        ss_mm, ss_moved, ln_done, norm_done = sem("ss_mm"), sem("ss_moved"), sem("ln_done"), sem("norm_done")
        normed, part_hi, part_lo, parts_stored = sem("normed"), sem("part_hi"), sem("part_lo"), sem("parts_stored")
        k_in = [[sem(f"k_in{s}_{h}") for h in range(NH)] for s in range(2)]
        q_in = [sem(f"q_in{h}") for h in range(NH)]
        qk_mm, exp_done, pv_mm = sem("qk_mm"), sem("exp_done"), sem("pv_mm")
        add_v, add_p = sem("add_v"), sem("add_p")
        rs_mm, rows_moved, o_done, o_stored = sem("rs_mm"), sem("rows_moved"), sem("o_done"), sem("o_stored")
        rows_stored, compact_in, inverted = sem("rows_stored"), sem("compact_in"), sem("inverted")
        inverse_stored, inverse_in = sem("inverse_stored"), sem("inverse_in")
        block = ctx.enter_context(nc.Block())

        def unit_no(b, g, u):
            return b * BUNITS + g * NU + u

        def half_no(b, g, h):
            return b * (NG * NH) + g * NH + h

        def step_no(b, g, st):
            return b * BSTEPS + g * STEPS + st

        def spread_no(b, hh):
            return b * (NG * NH - 1) + hh

        def ended_at(g, st, steps):
            l = g * STEPS + st - steps
            return l // NT - 1 if l >= NT and l % NT == 0 and (st < STEPS or steps >= NT) else None

        def adds_before(l):
            return ADDS * (l // NT) + max(1, l % NT)

        def units_at(table_slow, table_fast, b, g, st, more):
            if g < NG - 1:
                return (b, g + 1, table_slow[st]) if st in table_slow else None
            return (b + 1, 0, table_fast[st]) if more and st in table_fast else None

        def tile_at(table_fast, b, g, st, more):
            at = st - (NG - 1 - g) * STEPS
            return (b + 1, table_fast[at]) if more and at in table_fast else None

        def stages(attend, b_of_loop):
            for st in range(min(FAST_STAT), STEPS + 1):
                attend(-1, NG - 1, st, True, alone=True)
            with b_of_loop(0, B - 1) as b:
                for g in range(NG):
                    for st in range(STEPS):
                        attend(b, g, st, True)
                attend(b, NG - 1, STEPS, True)
            for g in range(NG):
                for st in range(STEPS):
                    attend(B - 1, g, st, False)
            attend(B - 1, NG - 1, STEPS, False)

        @block.sync
        def _(sp):
            sp.dma_start(v_bias[:], dram["bqkv"][2 * D:3 * D].rearrange("(a n) -> a n", a=1).broadcast_to([P, D])).then_inc(const_in, 16)
            sp.dma_start(qk_bias[:], dram["bqkT"]).then_inc(const_in, 16)

            def load_x(b, t):
                sp.wait_ge(turned, b * NT + max(0, t - XS + 1))
                sp.dma_start(xt[t % XS][:], dram["x"][b, t * P:(t + 1) * P, :]).then_inc(x_in[t % XS], 16)

            def step(b, g, st, more, alone=False):
                fin = units_at(SLOW_FIN, FAST_FIN, b, g, st, more)
                t = tile_at(FAST_STAT, b, g, st, more)
                if (alone and st == min(FAST_STAT)) or (more and g == NG - 2 and st == STEPS - NT):
                    sp.wait_ge(h_moved, (b + 1) * NT)
                    sp.dma_start(mod[:], dram["ada_b"][b + 1, 0:2 * D].rearrange("(j p) -> p j", p=P),
                                 allow_slow_non_contiguous=True).then_inc(mod_in, 16)
                    for k in range(XS - 1):
                        load_x(b + 1, k)
                if t and t[1] + XS - 1 < NT:
                    load_x(t[0], t[1] + XS - 1)
                hh = None if alone else ended_at(g, st, OUT)
                if hh is not None:
                    store_o(b, hh)
                if fin:
                    fb, fg, u = fin
                    which, half = UNITS[u]
                    n = unit_no(fb, fg, u)
                    scratch = dram["parts"][u]
                    sp.wait_ge(part_lo, n + 1)
                    sp.dma_start(scratch.rearrange("c p n -> p c n"), full(parts[:])).then_inc(parts_stored, 16)
                    sp.wait_ge(parts_stored, 16 * (n + 1))
                    src = scratch.rearrange("c (h d) n -> c d h n", h=HG)
                    if which == "k":
                        dst, got = k_stack[fg % 2][:, :, half * CH:(half + 1) * CH], k_in[fg % 2][half]
                        first_step = (fb * NG + fg - 1) * STEPS
                        if alone:
                            first_step = 0
                    else:
                        dst, got = q_stack[half], q_in[half]
                        if not alone:
                            sp.wait_ge(qk_mm, 2 * ((fb * NG + fg - 1) * STEPS + (half + 1) * NT))
                    if which == "k" and not alone:
                        sp.wait_ge(qk_mm, 2 * first_step)
                    for a in range(2):
                        for c in range(2):
                            r = slice((2 * a + c) * DH, (2 * a + c + 1) * DH)
                            part = a if which == "k" else c
                            sp.dma_start(full(dst[r]), src[part]).then_inc(got, 16)
                if not alone and st == STEPS:
                    store_o(b, NG * NH - 1)

            def store_o(b, hh):
                sp.wait_ge(o_done, b * NG * NH + hh + 1)
                sp.dma_start(dram["heads_out"][b * NH + hh % NH, (hh // NH) * P:(hh // NH + 1) * P, :], o_out[:]).then_inc(o_stored, 16)

            stages(step, sp.Fori)
            sp.wait_ge(o_stored, 16 * B * NG * NH)

        @block.tensor
        def _(pe):
            def qk(b, g, st, p):
                half, j = st // NT, st % NT
                s = g % 2
                if p == 0:
                    if st == 0 or st == NT // 2:
                        pe.wait_ge(k_in[s][st // (NT // 2)], 64 * (2 * b + g // 2 + 1))
                    if st % NT == 0:
                        pe.wait_ge(q_in[half], 64 * (NG * b + g + 1))
                n = step_no(b, g, st)
                if st > 0 or g > 0:
                    pe.wait_ge(exp_done, 2 * (n - 1) + p + 1)
                else:
                    pe.wait_ge(exp_done, 2 * BSTEPS * b)
                for i in range(2):
                    h = 2 * p + i
                    mm = nc.tensor.matmul(scores[p][:, i, :], k_stack[s][:, h, j * P:(j + 1) * P], q_stack[half][:, h, :],
                                          start=True, stop=True)
                mm.then_inc(qk_mm, 1)

            def weigh(b, l):
                g, st = l // STEPS, l % STEPS
                half, j = st // NT, st % NT
                n = b * BSTEPS + l
                pe.wait_ge(exp_done, 2 * n + 2)
                if g == 0 and half == 0:
                    pe.wait_ge(v_copied, b * NT + j + 1)
                if j == 0:
                    pe.wait_ge(o_done, b * NG * NH + max(0, g * NH + half - NH + 1))
                for h in range(HG):
                    mm = nc.tensor.matmul(pv[half][h * DH:(h + 1) * DH, :], v_now[:, j, (g * HG + h) * DH:(g * HG + h + 1) * DH],
                                          probs[l % RING][:, h, :], start=(j == 0), stop=(j == NT - 1))
                mm.then_inc(pv_mm, 1)

            def row_sums(b, hh, waits):
                pe.wait_ge(add_v, (b * NG * NH + hh + 1) * ADDS)
                pe.wait_ge(add_p, (b * NG * NH + hh + 1) * ADDS)
                aux_wait(waits)
                for h in range(HG):
                    mm = nc.tensor.matmul(aux[h * DH:(h + 1) * DH, :], small["ones"][:], sums[:, h, :], start=True, stop=True)
                mm.then_inc(rs_mm, 1)

            def aux_wait(waits):
                for s, v in waits:
                    pe.wait_ge(s, v)

            def aux_before(b, g, st, alone, kind):
                fast = g == NG - 1
                table = FAST_SUM if fast else SLOW_SUM
                summed = sum(1 for s in table if s < st or (s == st and kind == "turn"))
                done = [(ss_moved, (unit_no(b + 1, 0, 0) if fast else unit_no(b, g + 1, 0)) + summed)]
                done.append((h_moved, (b + 1) * NT + (sum(1 for s in FAST_TURN if s < st) if fast else 0)))
                if not alone:
                    l = g * STEPS + st
                    ended = sum(1 for m in range(NT + ROWS, l + 1, NT) if m < l or kind != "rows")
                    done.append((rows_moved, b * NG * NH + ended))
                return done

            def gemm_free(b, g, st):
                fast = g == NG - 1
                if fast:
                    pe.wait_ge(v_moved, (b + 1) * NT + sum(1 for s in FAST_V if s < st))
                    pe.wait_ge(raw_done, unit_no(b + 1, 0, 0) + sum(1 for s in FAST_END if s < st))
                else:
                    pe.wait_ge(v_moved, (b + 1) * NT)
                    pe.wait_ge(raw_done, unit_no(b, g + 1, SLOW_GEMM[st][0]))

            def unit_products(b, g, u, lo, hi):
                which, half = UNITS[u]
                at = (0 if which == "q" else D) + g * P
                c = slice(half * CH, (half + 1) * CH)
                terms = [(w, h, k) for k in range(KT) for w, h in ((wq_hi, h_hi), (wq_hi, h_lo), (wq_lo, h_hi))]
                for n in range(lo, hi):
                    w, h, k = terms[n]
                    mm = nc.tensor.matmul(gemm[:], w[:, k, at:at + P], h[:, k, c], start=(n == 0), stop=(n == len(terms) - 1))
                if hi == len(terms):
                    mm.then_inc(unit_mm, 1)

            def v_products(t, lo, hi):
                c = slice(t * P, (t + 1) * P)
                terms = [(h, w, k) for k in range(KT) for h, w in ((h_hi, wq_hi), (h_hi, wq_lo), (h_lo, wq_hi))]
                for n in range(lo, hi):
                    h, w, k = terms[n]
                    mm = nc.tensor.matmul(gemm[:], h[:, k, c], w[:, k, 2 * D:3 * D], start=(n == 0), stop=(n == len(terms) - 1))
                if hi == len(terms):
                    mm.then_inc(v_mm, 1)

            def fill(b, g, st, more, part, alone):
                N = 3 * KT
                if g < NG - 1 and st in SLOW_GEMM:
                    u, i = SLOW_GEMM[st]
                    if part == 0 and i == 0:
                        gemm_free(b, g, st)
                    lo = i * N // 3 + part * N // 6
                    unit_products(g=g + 1, b=b, u=u, lo=lo, hi=lo + N // 6)
                if g == NG - 1 and more and st in FAST:
                    kind, x = FAST[st]
                    if part == 0:
                        gemm_free(b, g, st)
                        if kind == "v":
                            pe.wait_ge(lo_done, (b + 1) * NT + x + 1)
                        else:
                            pe.wait_ge(lo_done, (b + 1) * NT + (UNITS[x][1] + 1) * CT)
                    lo = part * N // 2
                    if kind == "v":
                        v_products(x, lo, lo + N // 2)
                    else:
                        unit_products(b + 1, 0, x, lo, lo + N // 2)
                if part == 1:
                    un = units_at(SLOW_SUM, FAST_SUM, b, g, st, more)
                    if un:
                        pe.wait_ge(sq_done, unit_no(*un) + 1)
                        aux_wait(aux_before(b, g, st, alone, "squares"))
                        nc.tensor.matmul(aux[:], small["head_ones"][:], squares[:], start=True, stop=True).then_inc(ss_mm, 1)
                    t = tile_at(FAST_TURN, b, g, st, more)
                    if t:
                        pe.wait_ge(x_normed, t[0] * NT + t[1] + 1)
                        aux_wait(aux_before(b, g, st, alone, "turn"))
                        for k in range(KT):
                            mm = nc.tensor.transpose(aux[:, k * P:(k + 1) * P], xt[t[1] % XS][:, k * P:(k + 1) * P], small["ident"][:])
                        mm.then_inc(turned, 1)

            def step(b, g, st, more, alone=False):
                l = g * STEPS + st
                if alone:
                    fill(b, g, st, more, 0, True)
                    fill(b, g, st, more, 1, True)
                    return
                if st == STEPS:
                    weigh(b, l - 1)
                    row_sums(b, NG * NH - 1, [(ss_moved, unit_no(b + 1, 0, 0) + (NU if more else 0)),
                                              (h_moved, (b + 1) * NT + (NT if more else 0)),
                                              (rows_moved, b * NG * NH + NG * NH - 1)])
                    return
                qk(b, g, st, 0)
                if l > NT and l % NT == ROWS:
                    row_sums(b, l // NT - 1, aux_before(b, g, st, False, "rows") if (g < NG - 1 or more) else
                             [(ss_moved, unit_no(b + 1, 0, 0)), (rows_moved, b * NG * NH + l // NT - 1)])
                fill(b, g, st, more, 0, False)
                qk(b, g, st, 1)
                fill(b, g, st, more, 1, False)
                if l > 0:
                    weigh(b, l - 1)

            stages(step, pe.Fori)

        @block.scalar
        def _(act):
            act.preload_act_table_set("natural_log_exp_and_others")

            def step(b, g, st, more, alone=False):
                l = g * STEPS + st
                t = tile_at(FAST_SPLIT, b, g, st, more)
                if t:
                    act.wait_ge(h_moved, t[0] * NT + t[1] + 1)
                    nc.scalar.activation(h_hi[:, :, t[1] * P:(t[1] + 1) * P], h_full[:], ACT.Copy).then_inc(hi_done, 1)
                for p in range(2):
                    if not alone and st < STEPS:
                        if l >= RING:
                            if p == 0:
                                act.wait_ge(pv_mm, b * BSTEPS + l - RING + 1)
                                act.wait_ge(add_v, b * NG * NH * ADDS + adds_before(l - RING))
                            else:
                                act.wait_ge(add_p, b * NG * NH * ADDS + adds_before(l - RING))
                        elif l == 0:
                            act.wait_ge(pv_mm, b * BSTEPS)
                            act.wait_ge(add_v, b * NG * NH * ADDS)
                            act.wait_ge(add_p, b * NG * NH * ADDS)
                        act.wait_ge(qk_mm, 2 * step_no(b, g, st) + p + 1)
                        nc.scalar.activation(probs[l % RING][:, 2 * p:2 * p + 2, :], scores[p][:], ACT.Exp,
                                             bias=small["shift"][:]).then_inc(exp_done, 1)
                hh = None if alone else ended_at(g, st, ROWS)
                if hh is not None:
                    n = b * NG * NH + hh
                    act.wait_ge(rs_mm, n + 1)
                    act.wait_ge(o_done, n)
                    nc.scalar.activation(inverse[:], aux[:], ACT.Copy).then_inc(rows_moved, 1)
                    act.wait_ge(rows_moved, n + 1)
                    act.dma_start(dram["rows"], inverse[0:P:DH, :]).then_inc(rows_stored, 16)
                hh = None if alone else ended_at(g, st, COMPACT)
                if hh is not None:
                    act.wait_ge(rows_stored, 16 * (spread_no(b, hh) + 1))
                    act.dma_start(compact[:], dram["rows"].rearrange("h (r n) -> (h r) n", n=SEEN)).then_inc(compact_in, 16)
                hh = None if alone else ended_at(g, st, INVERTED)
                if hh is not None:
                    act.wait_ge(inverted, spread_no(b, hh) + 1)
                    act.dma_start(dram["inverse"].rearrange("h (r n) -> (h r) n", n=SEEN), compact[:]).then_inc(inverse_stored, 16)
                hh = None if alone else ended_at(g, st, SPREAD)
                if hh is not None:
                    act.wait_ge(inverse_stored, 16 * (spread_no(b, hh) + 1))
                    for h in range(HG):
                        act.dma_start(inverse[h * DH:(h + 1) * DH, :], dram["inverse"][h:h + 1, :].broadcast_to([DH, CH])).then_inc(inverse_in, 16)
                un = units_at(SLOW_INV, FAST_INV, b, g, st, more)
                if un:
                    n = unit_no(*un)
                    act.wait_ge(ss_moved, n + 1)
                    nc.scalar.activation(norms[:], norms[:], ACT.Ln, scale=LN_SCALE).then_inc(ln_done, 1)
                    act.wait_ge(ln_done, n + 1)
                    nc.scalar.activation(norms[:], norms[:], ACT.Exp, scale=-0.5, bias=small["ln_bias"][:]).then_inc(norm_done, 1)

            stages(step, act.Fori)

        @block.gpsimd
        def _(pool):
            def add(b, l):
                j = l % NT
                hh = b * NG * NH + l // NT
                if j == 0:
                    return
                pool.wait_ge(exp_done, 2 * (b * BSTEPS + l) + 2)
                if j == 1:
                    pool.wait_ge(rs_mm, hh)
                    a = probs[(l - 1) % RING][:, 2:4, :]
                else:
                    pool.wait_ge(add_p, hh * ADDS + j - 1)
                    a = sums[:, 2:4, :]
                nc.gpsimd.tensor_tensor(sums[:, 2:4, :], a, probs[l % RING][:, 2:4, :], ALU.add).then_inc(add_p, 1)

            def step(b, g, st, more, alone=False):
                l = g * STEPS + st
                t = tile_at(FAST_SPLIT, b, g, st, more)
                if t:
                    c = slice(t[1] * P, (t[1] + 1) * P)
                    pool.wait_ge(hi_done, t[0] * NT + t[1] + 1)
                    nc.gpsimd.tensor_tensor(h_lo[:, :, c], h_full[:], full(h_hi[:, :, c]), ALU.subtract).then_inc(lo_done, 1)
                if not alone and l > 0:
                    add(b, l - 1)
                t = tile_at(FAST_STAT, b, g, st, more)
                if t:
                    n, k = t[0] * NT + t[1], t[1]
                    pool.wait_ge(stat_clamped, n + 1)
                    nc.gpsimd.tensor_tensor(x_inv[:, k:k + 1], x_sqc[:, k:k + 1], small["minus_half"][:, 0:1], ALU.pow).then_inc(inv_done, 1)
                un = units_at(SLOW_RAW, FAST_RAW, b, g, st, more)
                if un:
                    n, r = unit_no(*un), raw[un[2] % 2]
                    pool.wait_ge(raw_done, n + 1)
                    pool.wait_ge(ss_mm, n)
                    nc.gpsimd.tensor_tensor(squares[:], r[:], r[:], ALU.mult).then_inc(sq_done, 1)

            stages(step, pool.Fori)

        @block.vector
        def _(dve):
            dve.wait_ge(const_in, 32)

            def add(b, l):
                j = l % NT
                hh = b * NG * NH + l // NT
                if j == 0:
                    return
                dve.wait_ge(exp_done, 2 * (b * BSTEPS + l) + 1)
                if j == 1:
                    dve.wait_ge(rs_mm, hh)
                    a = probs[(l - 1) % RING][:, 0:2, :]
                else:
                    dve.wait_ge(add_v, hh * ADDS + j - 1)
                    a = sums[:, 0:2, :]
                nc.vector.tensor_tensor(sums[:, 0:2, :], a, probs[l % RING][:, 0:2, :], ALU.add).then_inc(add_v, 1)

            def output(b, hh):
                n = b * NG * NH + hh
                if hh < NG * NH - 1:
                    dve.wait_ge(inverse_in, 16 * HG * (spread_no(b, hh) + 1))
                else:
                    dve.wait_ge(rs_mm, n + 1)
                    dve.wait_ge(o_done, n)
                    nc.vector.reciprocal(inverse[:], aux[:]).then_inc(rows_moved, 1)
                    dve.wait_ge(rows_moved, n + 1)
                dve.wait_ge(pv_mm, b * BSTEPS + (hh + 1) * NT)
                dve.wait_ge(o_stored, 16 * n)
                nc.vector.tensor_tensor(o_out[:], pv[hh % NH][:], inverse[:], ALU.mult).then_inc(o_done, 1)

            def invert(b, hh):
                dve.wait_ge(compact_in, 16 * (spread_no(b, hh) + 1))
                nc.vector.reciprocal(compact[:], compact[:]).then_inc(inverted, 1)

            def raw_out(un, alone):
                n = unit_no(*un)
                which, _ = UNITS[un[2]]
                col = (0 if which == "q" else NG) + un[1]
                dve.wait_ge(unit_mm, n + 1)
                if not alone or un[2] >= 2:
                    dve.wait_ge(part_lo, n - 1)
                nc.vector.tensor_scalar(raw[un[2] % 2][:], gemm[:], qk_bias[:, col:col + 1], None, ALU.add).then_inc(raw_done, 1)

            def v_out(b, t):
                dve.wait_ge(v_mm, b * NT + t + 1)
                dve.wait_ge(v_copied, b * NT)
                nc.vector.tensor_tensor(v_next[:, t, :], gemm[:], v_bias[:], ALU.add).then_inc(v_moved, 1)

            def statistics(b, t):
                n = b * NT + t
                if t == 0:
                    dve.wait_ge(mod_in, 16 * (b + 1))
                    dve.wait_ge(h_moved, n)
                    nc.vector.tensor_scalar(scale1[:], mod[:, KT:2 * KT], 1.0, None, ALU.add).then_inc(mod_ready, 1)
                dve.wait_ge(x_in[t % XS], 16 * (b * len(range(t % XS, NT, XS)) + t // XS + 1))
                dve.wait_ge(stat_clamped, n)
                nc.vector.tensor_tensor_reduce(unused[:], xt[t % XS][:], xt[t % XS][:], 1.0, 0.0, ALU.mult, ALU.add,
                                               x_sq[:, t:t + 1]).then_inc(stat, 1)
                dve.wait_ge(stat, n + 1)
                nc.vector.tensor_scalar(x_sqc[:, t:t + 1], x_sq[:, t:t + 1], EPS2, None, ALU.max).then_inc(stat_clamped, 1)

            def normalise(b, t):
                dve.wait_ge(inv_done, b * NT + t + 1)
                nc.vector.tensor_scalar(xt[t % XS][:], xt[t % XS][:], x_inv[:, t:t + 1], small["x_gain"][:],
                                        ALU.mult, ALU.mult).then_inc(x_normed, 1)

            def h_out(b, t):
                n = b * NT + t
                dve.wait_ge(turned, n + 1)
                dve.wait_ge(mod_ready, b + 1)
                dve.wait_ge(lo_done, n)
                for k in range(KT):
                    mv = nc.vector.tensor_scalar(h_full[:, k, :], aux[:, k * P:(k + 1) * P], scale1[:, k:k + 1],
                                                 mod[:, k:k + 1], ALU.mult, ALU.add)
                mv.then_inc(h_moved, 1)

            def sums_out(un):
                dve.wait_ge(ss_mm, unit_no(*un) + 1)
                dve.wait_ge(normed, unit_no(*un))
                nc.vector.tensor_scalar(norms[:], aux[:], EPS2, None, ALU.max).then_inc(ss_moved, 1)

            def make_parts(un):
                n, r = unit_no(*un), raw[un[2] % 2]
                dve.wait_ge(norm_done, n + 1)
                nc.vector.scalar_tensor_tensor(r[:], norms[:], 1.0 / EPS2 ** 0.5, r[:], ALU.min, ALU.mult).then_inc(normed, 1)
                dve.wait_ge(normed, n + 1)
                dve.wait_ge(parts_stored, 16 * n)
                gain = small["s_gain"][:] if UNITS[un[2]][0] == "q" else 1.0
                nc.vector.tensor_scalar(parts[:, 0, :], r[:], gain, None, ALU.mult).then_inc(part_hi, 1)
                dve.wait_ge(part_hi, n + 1)
                nc.vector.scalar_tensor_tensor(parts[:, 1, :], r[:], gain, full(parts[:, 0, :]), ALU.mult, ALU.subtract).then_inc(part_lo, 1)

            def step(b, g, st, more, alone=False):
                l = g * STEPS + st
                if not alone and l < NT - AHEAD:
                    take_v(b, l + AHEAD)
                raw_u = units_at(SLOW_RAW, FAST_RAW, b, g, st, more)
                sum_u = units_at(SLOW_INV, FAST_INV, b, g, st, more)
                fin_u = units_at(SLOW_FIN, FAST_FIN, b, g, st, more)
                fin_first = fin_u and raw_u and (raw_u[2] - fin_u[2]) % 2 == 0
                fin_second = fin_u and sum_u and not fin_first
                if fin_first:
                    make_parts(fin_u)
                if raw_u:
                    raw_out(raw_u, alone)
                t = tile_at(FAST_VOUT, b, g, st, more)
                if t:
                    v_out(*t)
                t = tile_at(FAST_TURN, b, g, st, more)
                if t:
                    normalise(*t)
                t = tile_at(FAST_HOUT, b, g, st, more)
                if t:
                    h_out(*t)
                if fin_second:
                    make_parts(fin_u)
                if not alone and ended_at(g, st, OUT) is not None:
                    output(b, ended_at(g, st, OUT))
                if not alone and ended_at(g, st, INVERT) is not None:
                    invert(b, ended_at(g, st, INVERT))
                if sum_u:
                    sums_out(sum_u)
                if not alone and l > 0:
                    add(b, l - 1)
                t = tile_at(FAST_STAT, b, g, st, more)
                if t:
                    statistics(*t)
                if fin_u and not fin_first and not fin_second:
                    make_parts(fin_u)
                if st == STEPS and more:
                    dve.wait_ge(pv_mm, (b + 1) * BSTEPS)
                    for j in range(AHEAD):
                        take_v(b + 1, j)
                if not alone and st == STEPS:
                    output(b, NG * NH - 1)

            def take_v(b, j):
                dve.wait_ge(v_moved, b * NT + j + 1)
                nc.vector.tensor_copy(v_now[:, j, :], v_next[:, j, :]).then_inc(v_copied, 1)

            stages(step, dve.Fori)


def build_mlp(nc, small, dram):
    with ExitStack() as ctx:
        def sb(name, shape, dt=F32):
            return ctx.enter_context(nc.sbuf_tensor(name, shape, dt))

        def sem(name):
            return ctx.enter_context(nc.semaphore(name))

        wp = [sb(f"wp_{x}", [P, KT, D], F32R) for x in ("hi", "lo")]
        w1 = [sb(f"w1_{x}", [P, KT, FF], F32R) for x in ("hi", "lo")]
        w2 = [sb(f"w2_{x}", [P, NM, D], F32R) for x in ("hi", "lo")]
        z = [sb(f"z_{x}", [P, KT, CH], F32R) for x in ("hi", "lo")]
        act_full = [sb(f"act_full{s}", [P, CH]) for s in range(2)]
        act_parts = [sb(f"act_parts{s}", [P, 2, CH], F32R) for s in range(2)]
        heads = [sb(f"heads{s}", [P, KT, P]) for s in range(2)]
        heads_parts = sb("heads_parts", [P, 2, KT, P], F32R)
        y = sb("y", [P, CT, D])
        y_next = sb("y_next", [P, CT, D])
        x_tile = sb("x_tile", [P, D])
        y_norm = [sb(f"y_norm{s}", [P, D]) for s in range(2)]
        z_full = [sb(f"z_full{s}", [P, KT, P]) for s in range(2)]
        result = [sb(f"result{s}", [P, D]) for s in range(2)]
        gate1, gate2 = sb("gate1", [P, D]), sb("gate2", [P, D])
        p_bias, f2_bias = sb("p_bias", [P, D]), sb("f2_bias", [P, D])
        f1_bias = sb("f1_bias", [P, NM])
        gated_bias = sb("gated_bias", [P, D])
        mod = sb("mod_mlp", [P, 2 * KT])
        scale1 = sb("scale1_mlp", [P, KT])
        y_sq, y_sqc, y_inv = sb("y_sq", [P, CT]), sb("y_sqc", [P, CT]), sb("y_inv", [P, CT])
        heads_first = [heads[0][:], heads[1][:]] + [a.rearrange("p (k n) -> p k n", k=KT) for a in (act_full[0], act_full[1])]
        x_first = [x_tile[:]] + [a.rearrange("p k n -> p (k n)") for a in (z_full[0], z_full[1])] + [gated_bias[:]]
        stage = [y[:, s, :] for s in range(CT)] + [result[0][:], result[1][:]]

        acc = [ctx.enter_context(nc.psum_tensor(f"acc{t}", [P, D], F32)) for t in range(CT)]
        up = [ctx.enter_context(nc.psum_tensor(f"up{s}", [P, CH], F32)) for s in range(2)]
        proj = ctx.enter_context(nc.psum_tensor("proj", [P, D], F32))
        turn = ctx.enter_context(nc.psum_tensor("turn", [P, KT * P], F32))

        const_in, p_bias_in = sem("const_in_mlp"), sem("p_bias_in")
        w_in = [sem(f"w_in{s}") for s in range(len(stage))]
        heads_first_in = [sem(f"heads_first_in{t}") for t in range(CT)]
        x_first_in = [sem(f"x_first_in{t}") for t in range(CT)]
        w_high, w_low = sem("w_high"), sem("w_low")
        x_in, gate1_in, gate2_in, mod_in = sem("x_in_mlp"), sem("gate1_in"), sem("gate2_in"), sem("mod_in_mlp")
        heads_hi, heads_lo, proj_mm, proj_moved = sem("heads_hi"), sem("heads_lo"), sem("proj_mm"), sem("proj_moved")
        heads_in = [sem(f"heads_in{s}") for s in range(2)]
        y_taken = sem("y_taken")
        y_gated, y_done, y_stat, y_clamped, y_inverse = sem("y_gated"), sem("y_done"), sem("y_stat"), sem("y_clamped"), sem("y_inverse")
        mod_ready, y_normed, turned, z_moved, z_hi, z_lo = (sem(x) for x in ("mod_ready_mlp", "y_normed", "turned_mlp", "z_moved", "z_hi_done", "z_lo_done"))
        up_mm, gelu_done, act_hi, act_lo = sem("up_mm"), sem("gelu_done"), sem("act_hi"), sem("act_lo")
        down_mm, acc_mm, acc_moved, out_done = (sem(x) for x in ("down_mm", "acc_mm", "acc_moved", "out_done"))
        bias_gated, y_biased = sem("bias_gated"), sem("y_biased")
        out_stored = [sem(f"out_stored{s}") for s in range(2)]
        block = ctx.enter_context(nc.Block())

        pieces = [(wp, slice(None), k) for k in range(KT)]
        for m in range(NM):
            pieces += [(w1, m, None), (w2, None, m)]
        NW = len(pieces)
        EARLY = 2 * len(stage)
        LATE = len(stage) - CT
        slot = [n % len(stage) if n < EARLY else CT + (n - EARLY) % LATE for n in range(NW)]
        turn_of = [slot[:n].count(slot[n]) for n in range(NW)]
        before = [max([k for k in range(n) if slot[k] == slot[n]], default=None) for n in range(NW)]

        def piece(parts_of, which):
            w, a, b = parts_of
            if w is w1:
                return w[which][:, :, a * P:(a + 1) * P]
            return w[which][:, b, :]

        def piece_shape(n, ap):
            return ap.rearrange("p (k m) -> p k m", k=KT) if pieces[n][0] is w1 else ap

        SPLIT = {2 + 3 * t: t for t in range(CT)}
        PROJ = {3 + 3 * t: t for t in range(CT)}
        MAKE = {4 + 3 * t: t for t in range(CT)}
        NORM = 13
        BIAS = 2
        LAG = 2

        def turn_bank(c, t):
            return acc[t] if isinstance(c, int) and c == 0 else turn

        def late(m):
            return range(EARLY + LATE * m, min(NW, EARLY + LATE * (m + 1)))

        def nothing(*_):
            pass

        def chunks(first, prepare, turn_tile, mlp, finish, fori):
            def chunk(c, more):
                for m in range(NM - 1):
                    mlp(c, m)
                    if more:
                        prepare(c + 1, m)
                for t in range(CT):
                    if t == CT // 2:
                        mlp(c, NM - 1)
                    if more:
                        turn_tile(c + 1, t)
                for t in range(CT):
                    finish(c, t)

            first()
            chunk(0, True)
            with fori(1, NC - 1) as c:
                chunk(c, True)
            chunk(NC - 1, False)

        @block.sync
        def _(sp):
            def load_heads(c, t, tile, signal):
                sp.dma_start(tile, dram["heads_out"][c, :, t * P:(t + 1) * P].rearrange("(k p) n -> p k n", p=P)).then_inc(signal, 16)

            def load_x(c, t, tile, signal):
                sp.dma_start(tile, dram["x"].rearrange("b (h n) d -> (b h) n d", h=NH)[c, t * P:(t + 1) * P, :]).then_inc(signal, 16)

            def load_gate(c):
                sp.dma_start(gate1[:], dram["ada_c"][bass.ts(c, 1), 2 * D:3 * D].broadcast_to([P, D])).then_inc(gate1_in, 16)

            def load_mod(c):
                sp.dma_start(mod[:], dram["ada_c"][c, 3 * D:5 * D].rearrange("(j p) -> p j", p=P),
                             allow_slow_non_contiguous=True).then_inc(mod_in, 16)

            def first():
                for t in range(CT):
                    load_heads(0, t, heads_first[t], heads_first_in[t])
                    if t == 0:
                        sp.dma_start(p_bias[:], dram["bproj"].rearrange("(a n) -> a n", a=1).broadcast_to([P, D])).then_inc(p_bias_in, 16)
                        load_gate(0)
                    load_x(0, t, x_first[t], x_first_in[t])
                load_mod(0)
                sp.dma_start(f1_bias[:], dram["bfc1T"]).then_inc(const_in, 16)
                sp.dma_start(f2_bias[:], dram["bfc2"].rearrange("(a n) -> a n", a=1).broadcast_to([P, D])).then_inc(const_in, 16)

            def prepare(c, m):
                if m == 0:
                    sp.wait_ge(y_done, CT * c)
                    load_gate(c)
                    sp.wait_ge(z_moved, CT * c)
                    load_mod(c)
                if m + 1 in SPLIT:
                    t = SPLIT[m + 1]
                    sp.wait_ge(heads_lo, CT * c + max(0, t - 1))
                    load_heads(c, t, heads[t % 2][:], heads_in[t % 2])
                    sp.wait_ge(y_done, CT * c + t)
                    load_x(c, t, x_tile[:], x_in)

            def mlp(c, m):
                if m == 0:
                    sp.wait_ge(out_done, CT * c)
                    sp.wait_ge(bias_gated, c)
                    sp.dma_start(gate2[:], dram["ada_c"][bass.ts(c, 1), 5 * D:6 * D].broadcast_to([P, D])).then_inc(gate2_in, 16)

            def finish(c, t):
                sp.wait_ge(out_done, CT * c + t + 1)
                sp.dma_start(dram["out"].rearrange("b (h n) d -> (b h) n d", h=NH)[c, t * P:(t + 1) * P, :],
                             result[t % 2][:]).then_inc(out_stored[t % 2], 16)

            chunks(first, prepare, nothing, mlp, finish, sp.Fori)
            for s in range(2):
                sp.wait_ge(out_stored[s], 16 * NC * CT // 2)

        @block.scalar
        def _(act):
            w_dram = {id(wp): dram["wprojT"], id(w1): dram["wfc1T"], id(w2): dram["wfc2T"]}

            def load(n):
                w, a, b = pieces[n]
                src = w_dram[id(w)].rearrange("(k p) n -> p k n", p=P)
                src = src[:, :, a * P:(a + 1) * P] if w is w1 else src[:, b, :]
                if before[n] is not None:
                    act.wait_ge(w_low, before[n] + 1)
                act.dma_start(piece_shape(n, stage[slot[n]]), src).then_inc(w_in[slot[n]], 16)

            def split_high(n):
                act.wait_ge(w_in[slot[n]], 16 * (turn_of[n] + 1))
                nc.scalar.activation(piece(pieces[n], 0), piece_shape(n, stage[slot[n]]), ACT.Copy).then_inc(w_high, 1)

            def first():
                for n in range(len(stage)):
                    load(n)
                act.preload_act_table(ACT.Gelu_apprx_tanh)
                for k in range(KT):
                    split_high(k)
                    act.wait_ge(heads_first_in[k], 16)
                    nc.scalar.activation(z[0][:, :, k * P:(k + 1) * P], heads_first[k], ACT.Copy).then_inc(heads_hi, 1)
                for n in range(KT, len(stage)):
                    split_high(n)
                for n in range(len(stage), EARLY):
                    load(n)
                for t in range(CT):
                    split_high(len(stage) + t)
                    turn_tile(0, t)
                for n in range(len(stage) + CT, EARLY):
                    split_high(n)
                act.wait_ge(const_in, 32)

            def turn_tile(c, t):
                act.wait_ge(up_mm, NM * c)
                act.wait_ge(z_moved, CT * c + t + 1)
                nc.scalar.activation(z[0][:, :, t * P:(t + 1) * P], z_full[t % 2][:], ACT.Copy).then_inc(z_hi, 1)

            def mlp(c, m):
                n = NM * c + m
                more_weights = late(m) if isinstance(c, int) and c == 0 else ()
                for k in more_weights:
                    load(k)
                act.wait_ge(up_mm, n + 1)
                if m >= 2:
                    act.wait_ge(act_lo, n - 1)
                else:
                    act.wait_ge(act_lo, NM * c)
                nc.scalar.activation(act_full[m % 2][:], up[m % 2][:], ACT.Gelu_apprx_tanh, bias=f1_bias[:, m:m + 1]).then_inc(gelu_done, 1)
                act.wait_ge(gelu_done, n + 1)
                if m >= 2:
                    act.wait_ge(down_mm, (NM - 1) * c + m - 1)
                else:
                    act.wait_ge(acc_mm, CT * c)
                nc.scalar.activation(act_parts[m % 2][:, 0, :], act_full[m % 2][:], ACT.Copy).then_inc(act_hi, 1)
                for k in more_weights:
                    split_high(k)

            chunks(first, nothing, turn_tile, mlp, nothing, act.Fori)

        @block.gpsimd
        def _(pool):
            def first():
                prepare(0, NORM)
                for t in range(CT):
                    turn_tile(0, t)
                pool.wait_ge(const_in, 32)

            def prepare(c, m):
                if m == NORM:
                    pool.wait_ge(y_clamped, c + 1)
                    nc.gpsimd.tensor_tensor(y_inv[:], y_sqc[:], small["minus_half"][:, 0:CT], ALU.pow).then_inc(y_inverse, 1)

            def turn_tile(c, t):
                r = slice(t * P, (t + 1) * P)
                pool.wait_ge(z_hi, CT * c + t + 1)
                nc.gpsimd.tensor_tensor(z[1][:, :, r], z_full[t % 2][:], full(z[0][:, :, r]), ALU.subtract).then_inc(z_lo, 1)

            def mlp(c, m):
                if m == BIAS:
                    pool.wait_ge(gate2_in, 16 * (c + 1))
                    nc.gpsimd.tensor_tensor(gated_bias[:], gate2[:], f2_bias[:], ALU.mult).then_inc(bias_gated, 1)
                if BIAS < m <= BIAS + CT:
                    t = m - BIAS - 1
                    pool.wait_ge(bias_gated, c + 1)
                    pool.wait_ge(y_taken, c + 1)
                    nc.gpsimd.tensor_tensor(y[:, t, :], y[:, t, :], gated_bias[:], ALU.add).then_inc(y_biased, 1)
                pool.wait_ge(act_hi, NM * c + m + 1)
                nc.gpsimd.tensor_tensor(act_parts[m % 2][:, 1, :], act_full[m % 2][:], full(act_parts[m % 2][:, 0, :]), ALU.subtract).then_inc(act_lo, 1)

            chunks(first, prepare, turn_tile, mlp, nothing, pool.Fori)

        @block.tensor
        def _(pe):
            pairs = ((0, 0), (0, 1), (1, 0))

            def prepare(c, m):
                if m in PROJ:
                    t = PROJ[m]
                    pe.wait_ge(heads_lo, CT * c + t + 1)
                    pe.wait_ge(proj_moved, CT * c + t)
                    for k in range(KT):
                        for i, (a, b) in enumerate(pairs):
                            mm = nc.tensor.matmul(proj[:], heads_parts[:, b, k, :], wp[a][:, k, :],
                                                  start=(k == 0 and i == 0), stop=(k == KT - 1 and i == 2))
                    mm.then_inc(proj_mm, 1)

            def turn_tile(c, t):
                pe.wait_ge(y_normed, CT * c + t + 1)
                bank = turn_bank(c, t)
                if bank is turn:
                    pe.wait_ge(z_moved, CT * c + t)
                for k in range(KT):
                    mm = nc.tensor.transpose(bank[:, k * P:(k + 1) * P], y_norm[t % 2][:, k * P:(k + 1) * P], small["ident"][:])
                mm.then_inc(turned, 1)

            def down(c, m, tiles):
                if tiles[0] == 0:
                    pe.wait_ge(act_lo, NM * c + m + 1)
                    pe.wait_ge(w_low, KT + 2 * m + 2)
                for t in tiles:
                    if m == 0:
                        pe.wait_ge(acc_moved, CT * c)
                    for i, (a, b) in enumerate(pairs):
                        mm = nc.tensor.matmul(acc[t][:], act_parts[m % 2][:, b, t * P:(t + 1) * P], w2[a][:, m, :],
                                              start=(m == 0 and i == 0), stop=(m == NM - 1 and i == 2))
                    if m == NM - 1:
                        mm.then_inc(acc_mm, 1)
                    elif t == CT - 1:
                        mm.then_inc(down_mm, 1)

            def lift(c, m):
                n = NM * c + m
                if m == 0:
                    pe.wait_ge(z_lo, CT * (c + 1))
                pe.wait_ge(w_low, KT + 2 * m + 1)
                pe.wait_ge(gelu_done, n - 1 if m >= 2 else NM * c)
                for k in range(KT):
                    for i, (a, b) in enumerate(pairs):
                        mm = nc.tensor.matmul(up[m % 2][:], w1[a][:, k, m * P:(m + 1) * P], z[b][:, k, :],
                                              start=(k == 0 and i == 0), stop=(k == KT - 1 and i == 2))
                mm.then_inc(up_mm, 1)

            def chunk(c, more):
                first_two, last_two = (0, 1), (2, 3)
                for m in range(NM - 1):
                    lift(c, m)
                    if more and m == NM - 2:
                        turn_tile(c + 1, 0)
                    if m >= LAG:
                        down(c, m - LAG, first_two + last_two)
                    if more:
                        prepare(c + 1, m)
                if more:
                    turn_tile(c + 1, 1)
                lift(c, NM - 1)
                down(c, NM - 3, first_two + last_two)
                if more:
                    turn_tile(c + 1, 2)
                down(c, NM - 2, first_two)
                if more:
                    turn_tile(c + 1, 3)
                down(c, NM - 2, last_two)
                down(c, NM - 1, first_two + last_two)

            for t in range(CT):
                r = slice(t * P, (t + 1) * P)
                pe.wait_ge(heads_lo, t + 1)
                for k in range(KT):
                    if t == 0:
                        pe.wait_ge(w_low, k + 1)
                    for i, (a, b) in enumerate(pairs):
                        mm = nc.tensor.matmul(acc[t][:], z[b][:, k, r], wp[a][:, k, :],
                                              start=(k == 0 and i == 0), stop=(k == KT - 1 and i == 2))
                mm.then_inc(proj_mm, 1)
            for t in range(CT):
                turn_tile(0, t)
            chunk(0, True)
            with pe.Fori(1, NC - 1) as c:
                chunk(c, True)
            chunk(NC - 1, False)

        @block.vector
        def _(dve):
            def split_low(n):
                dve.wait_ge(w_high, n + 1)
                nc.vector.tensor_tensor(piece(pieces[n], 1), piece_shape(n, stage[slot[n]]), full(piece(pieces[n], 0)),
                                        ALU.subtract).then_inc(w_low, 1)

            def make_y(c, t, product, x_of_tile):
                n = CT * c + t
                yt = y_next[:, t, :]
                dve.wait_ge(proj_mm, n + 1)
                dve.wait_ge(y_taken, c)
                nc.vector.tensor_tensor(yt, product[:], p_bias[:], ALU.add).then_inc(proj_moved, 1)
                if t == 0:
                    dve.wait_ge(gate1_in, 16 * (c + 1))
                dve.wait_ge(proj_moved, n + 1)
                nc.vector.tensor_tensor(yt, yt, gate1[:], ALU.mult).then_inc(y_gated, 1)
                dve.wait_ge(y_gated, n + 1)
                if isinstance(c, int) and c == 0:
                    dve.wait_ge(x_first_in[t], 16)
                else:
                    dve.wait_ge(x_in, 16 * (n + 1 - CT))
                nc.vector.tensor_tensor(yt, yt, x_of_tile, ALU.add).then_inc(y_done, 1)
                dve.wait_ge(y_done, n + 1)
                dve.wait_ge(y_stat, n)
                dve.wait_ge(y_clamped, c)
                nc.vector.tensor_tensor_reduce(y_norm[t % 2][:], yt, yt, 1.0, 0.0, ALU.mult, ALU.add, y_sq[:, t:t + 1]).then_inc(y_stat, 1)

            def prepare(c, m):
                if m in SPLIT:
                    n = CT * c + SPLIT[m]
                    t = SPLIT[m]
                    dve.wait_ge(heads_in[t % 2], 16 * ((c - 1) * (CT // 2) + t // 2 + 1))
                    dve.wait_ge(proj_mm, n)
                    nc.vector.tensor_copy(heads_parts[:, 0, :, :], heads[t % 2][:]).then_inc(heads_hi, 1)
                    dve.wait_ge(heads_hi, n + 1)
                    nc.vector.tensor_tensor(heads_parts[:, 1, :, :], heads[t % 2][:], full(heads_parts[:, 0, :, :]), ALU.subtract).then_inc(heads_lo, 1)
                if m in MAKE:
                    make_y(c, MAKE[m], proj, x_tile[:])
                if m == NORM:
                    clamp(c)

            def clamp(c):
                dve.wait_ge(y_stat, CT * (c + 1))
                dve.wait_ge(y_inverse, c)
                dve.wait_ge(z_moved, CT * c)
                nc.vector.tensor_scalar(y_sqc[:], y_sq[:], EPS2, None, ALU.max).then_inc(y_clamped, 1)
                dve.wait_ge(mod_in, 16 * (c + 1))
                nc.vector.tensor_scalar(scale1[:], mod[:, KT:2 * KT], 1.0, None, ALU.add).then_inc(mod_ready, 1)

            def normalise(c, t):
                nc.vector.tensor_scalar(y_norm[t % 2][:], y_next[:, t, :], y_inv[:, t:t + 1], small["y_gain"][:],
                                        ALU.mult, ALU.mult).then_inc(y_normed, 1)

            def turn_tile(c, t):
                n = CT * c + t
                if t == 0:
                    dve.wait_ge(y_inverse, c + 1)
                    dve.wait_ge(mod_ready, c + 1)
                    normalise(c, 0)
                    normalise(c, 1)
                dve.wait_ge(turned, n + 1)
                if t + 2 < CT:
                    normalise(c, t + 2)
                dve.wait_ge(z_lo, CT * c + max(0, t - 1))
                for k in range(KT):
                    mv = nc.vector.tensor_scalar(z_full[t % 2][:, k, :], turn_bank(c, t)[:, k * P:(k + 1) * P], scale1[:, k:k + 1], mod[:, k:k + 1],
                                                 ALU.mult, ALU.add)
                mv.then_inc(z_moved, 1)

            def take_over(c):
                dve.wait_ge(out_done, CT * (c + 1))
                nc.vector.tensor_copy(y[:], y_next[:]).then_inc(y_taken, 1)

            def mlp(c, m):
                if isinstance(c, int) and c == 0:
                    for n in late(m):
                        split_low(n)

            def first():
                for k in range(KT):
                    split_low(k)
                    r = slice(k * P, (k + 1) * P)
                    dve.wait_ge(heads_hi, k + 1)
                    nc.vector.tensor_tensor(z[1][:, :, r], heads_first[k], full(z[0][:, :, r]), ALU.subtract).then_inc(heads_lo, 1)
                dve.wait_ge(p_bias_in, 16)
                for t in range(CT):
                    make_y(0, t, acc[t], x_first[t])
                clamp(0)
                for n in range(KT, len(stage)):
                    split_low(n)
                for t in range(CT):
                    turn_tile(0, t)
                    split_low(len(stage) + t)
                for n in range(len(stage) + CT, EARLY):
                    split_low(n)
                dve.wait_ge(w_low, EARLY)
                take_over(-1)

            def finish(c, t):
                n = CT * c + t
                r = result[t % 2]
                dve.wait_ge(acc_mm, n + 1)
                dve.wait_ge(out_stored[t % 2], 16 * (CT // 2 * c + t // 2))
                if t == 0:
                    dve.wait_ge(gate2_in, 16 * (c + 1))
                    dve.wait_ge(y_biased, CT * (c + 1))
                nc.vector.tensor_tensor(r[:], acc[t][:], gate2[:], ALU.mult).then_inc(acc_moved, 1)
                dve.wait_ge(acc_moved, n + 1)
                nc.vector.tensor_tensor(r[:], r[:], y[:, t, :], ALU.add).then_inc(out_done, 1)
                if t == CT - 1 and not (isinstance(c, int) and c == NC - 1):
                    take_over(c)

            chunks(first, prepare, turn_tile, mlp, finish, dve.Fori)


def program(nc, x, cT, wadaT, bada, wqkvT, bqkv, bqkT, wprojT, bproj, wfc1T, bfc1T, wfc2T, bfc2, g1, g2, gq, gk, out):
    dram = dict(x=x, cT=cT, wadaT=wadaT, bada=bada, wqkvT=wqkvT, bqkv=bqkv, bqkT=bqkT, wprojT=wprojT, bproj=bproj,
                wfc1T=wfc1T, bfc1T=bfc1T, wfc2T=wfc2T, bfc2=bfc2, g1=g1, g2=g2, gq=gq, gk=gk, out=out)
    dram["ada_b"] = nc.dram_tensor("ada_b", [B, 6 * D], F32, kind="Internal").ap()
    dram["ada_c"] = nc.dram_tensor("ada_c", [NC, 6 * D], F32, kind="Internal").ap()
    dram["parts"] = nc.dram_tensor("parts_scratch", [NU, 2, P, CH], F32, kind="Internal").ap()
    dram["rows"] = nc.dram_tensor("rows_scratch", [HG, CH], F32, kind="Internal").ap()
    dram["inverse"] = nc.dram_tensor("inverse_scratch", [HG, CH], F32, kind="Internal").ap()
    dram["heads_out"] = nc.dram_tensor("heads_out", [NC, D, CH], F32, kind="Internal").ap()
    with ExitStack() as ctx:
        small = {}
        for name, cols in (("ident", P), ("head_ones", P), ("ones", DH), ("minus_half", CT), ("ln_bias", 1), ("shift", 1),
                           ("x_gain", 1), ("y_gain", 1), ("s_gain", 1)):
            small[name] = ctx.enter_context(nc.sbuf_tensor(name, [P, cols], F32))
        with ExitStack() as weights:
            wq_hi = weights.enter_context(nc.sbuf_tensor("wqkv_hi", [P, KT, 3 * D], F32R))
            wq_lo = weights.enter_context(nc.sbuf_tensor("wqkv_lo", [P, KT, 3 * D], F32R))
            build_setup(nc, small, dram, wq_hi, wq_lo)
            build_attention(nc, small, dram, wq_hi, wq_lo)
        build_mlp(nc, small, dram)


def kernel(x, cond_1024, L0_cond_g1, L0_cond_g2, L0_cond_gq, L0_cond_gk, L0_cond_Wqkv, L0_cond_bqkv, L0_cond_Wproj,
           L0_cond_bproj, L0_cond_Wfc1, L0_cond_bfc1, L0_cond_Wfc2, L0_cond_bfc2, L0_cond_Wada, L0_cond_bada):
    import numpy as np
    import concourse.bacc as bacc
    from concourse.bass_utils import run_bass_kernel_spmd

    def turned(a):
        return np.ascontiguousarray(np.asarray(a).T)

    bqkv = np.ascontiguousarray(L0_cond_bqkv)
    arrays = {
        "x": np.ascontiguousarray(x), "cT": turned(cond_1024), "wadaT": turned(L0_cond_Wada),
        "bada": np.ascontiguousarray(L0_cond_bada), "wqkvT": turned(L0_cond_Wqkv), "bqkv": bqkv,
        "bqkT": turned(bqkv[:2 * D].reshape(2 * NG, P)), "wprojT": turned(L0_cond_Wproj),
        "bproj": np.ascontiguousarray(L0_cond_bproj), "wfc1T": turned(L0_cond_Wfc1),
        "bfc1T": turned(np.asarray(L0_cond_bfc1).reshape(NM, P)), "wfc2T": turned(L0_cond_Wfc2),
        "bfc2": np.ascontiguousarray(L0_cond_bfc2), "g1": np.ascontiguousarray(L0_cond_g1),
        "g2": np.ascontiguousarray(L0_cond_g2), "gq": np.ascontiguousarray(L0_cond_gq), "gk": np.ascontiguousarray(L0_cond_gk),
    }
    nc = bacc.Bacc("TRN2", target_bir_lowering=False, num_devices=1, dynamic_dma_scratch_size=1024)
    args = [nc.dram_tensor(f"in_{n}", a.shape, mybir.dt.from_np(a.dtype), kind="ExternalInput").ap() for n, a in arrays.items()]
    args.append(nc.dram_tensor("out", (B, T, D), F32, kind="ExternalOutput").ap())
    program(nc, *args)
    r = run_bass_kernel_spmd(nc, [{f"in_{n}": a for n, a in arrays.items()}], core_ids=[0])
    return r.results[0]["out"]
```

```python
from contextlib import ExitStack

import concourse.bass as bass
from concourse import mybir

F32 = mybir.dt.float32
F32R = mybir.dt.float32r
ALU = mybir.AluOpType
ACT = mybir.ActivationFunctionType

P = 128
B, T, D = 4, 1024, 512
H, DH = 16, 32
FF = 4 * D
KT = D // P
HG = P // DH
NG = H // HG
CH = 512
NH = T // CH
NT = T // P
CT = CH // P
NC = B * NH
STEPS = NH * NT
BSTEPS = NG * STEPS
ADDS = NT - 1
NM = FF // P
RING = 3
EPS2 = 1e-24
LN_SCALE = 2.0 ** 16
LN_BIAS = 8 * 0.6931471805599453
NA_NOW = 2 * D // CH
NA_LATER = 6 * D // CH - NA_NOW
SAFE = 64.0

UNITS = (("k", 0), ("q", 0), ("k", 1), ("q", 1))
NU = len(UNITS)
BUNITS = NG * NU

def products(*steps):
    return {sum(steps[:u]) + i: (u, i, steps[u]) for u in range(NU) for i in range(steps[u])}


SLOW = [products(4, 4, 4, 4)] * (NG - 2) + [products(3, 3, 3, 3)]
SLOW_END = [{st: u for st, (u, i, steps) in t.items() if i == steps - 1} for t in SLOW]
FAST = {3: ("v", 0), 4: ("v", 1), 5: ("v", 2), 6: ("u", 0), 7: ("u", 1), 8: ("v", 3), 9: ("v", 4),
        10: ("u", 2), 11: ("u", 3), 12: ("v", 5), 13: ("v", 6), 14: ("v", 7)}
FAST_END = {s: x[1] for s, x in FAST.items() if x[0] == "u"}
FAST_V = {s: x[1] for s, x in FAST.items() if x[0] == "v"}


def later(table, steps):
    return {s + steps: x for s, x in table.items()}


def of_batch(slow, tight, fast):
    table = {}
    for g in range(NG):
        after = (slow, tight, fast)[max(0, g - NG + 3)]
        for st, u in later(SLOW_END[g] if g < NG - 1 else FAST_END, after).items():
            table[g * STEPS + st] = (0, g + 1, u) if g < NG - 1 else (1, 0, u)
    return {l % BSTEPS: (ahead - l // BSTEPS, g, u) for l, (ahead, g, u) in table.items()}


RAW, SUM, INV, FIN = of_batch(1, 1, 1), of_batch(3, 2, 2), of_batch(4, 3, 3), of_batch(5, 4, 4)
FAST_VOUT = later(FAST_V, 1)
FAST_STAT = {t - 1: t for t in range(NT)}
FAST_TURN = later(FAST_STAT, 1)
FAST_HOUT = later(FAST_STAT, 2)
FAST_SPLIT = later(FAST_STAT, 3)
AHEAD = 3
XS = 3
ROWS, COMPACT, INVERT, INVERTED, SPREAD, OUT = 1, 2, 4, 4, 5, 7
SEEN = HG * CH // P


def full(ap):
    return ap.bitcast(F32)


def build_setup(nc, small, dram, wq_hi, wq_lo):
    with ExitStack() as ctx:
        def sb(name, shape, dt=F32):
            return ctx.enter_context(nc.sbuf_tensor(name, shape, dt))

        def sem(name):
            return ctx.enter_context(nc.semaphore(name))

        NA = NA_NOW
        wada = sb("wada", [P, KT, NA * CH])
        wstage = sb("wstage", [P, KT, 3 * D])
        ada = sb("ada", [B, NA * CH])
        bada = sb("bada_rows", [B, NA * CH])
        cT = sb("cT", [P, KT, B])
        ce = sb("c_exp", [P, KT, B])
        cs = sb("c_sigmoid", [P, KT, B])
        silu = small["silu"][:].rearrange("p (k b) -> p k b", k=KT)
        gains = sb("gains", [P, 4])
        tmp = sb("tmp", [P, 4])
        pa = [ctx.enter_context(nc.psum_tensor(f"pa{n}", [P, CH], F32)) for n in range(NA)]

        c_in, bias_in, gain_in = sem("c_in"), sem("bias_in"), sem("gain_in")
        wada_in = [sem(f"wada_in{n}") for n in range(NA)]
        wqkv_in = [sem(f"wqkv_in{n}") for n in range(3)]
        exp_c, sig_c, silu_c = sem("exp_c"), sem("sig_c"), sem("silu_c_done")
        ada_mm, ada_out, ada_stored = sem("ada_mm"), sem("ada_out"), sem("ada_stored")
        high, low, gain_chain, zeroed, masks = sem("high"), sem("low"), sem("gain_chain"), sem("zeroed"), sem("masks")
        block = ctx.enter_context(nc.Block())

        @block.sync
        def _(sp):
            sp.dma_start(cT[:], dram["cT"].rearrange("(k p) b -> p k b", p=P)).then_inc(c_in, 16)
            for n, g in enumerate(("g1", "g2", "gq", "gk")):
                sp.dma_start(gains[:, n:n + 1], dram[g].rearrange("(a n) -> a n", a=1).broadcast_to([P, 1])).then_inc(gain_in, 16)
            sp.dma_start(bada[:], dram["bada"][0:NA * CH].rearrange("(a n) -> a n", a=1).broadcast_to([B, NA * CH])).then_inc(bias_in, 16)
            for n in range(NA):
                sp.dma_start(wada[:, :, n * CH:(n + 1) * CH],
                             dram["wadaT"][:, n * CH:(n + 1) * CH].rearrange("(k p) n -> p k n", p=P)).then_inc(wada_in[n], 16)
            sp.wait_ge(ada_out, NA)
            sp.dma_start(dram["ada_b"], ada[:]).then_inc(ada_stored, 16)
            sp.wait_ge(ada_stored, 16)

        @block.gpsimd
        def _(pool):
            ident, bones = small["ident"], small["head_ones"]
            pool.memset(ident[:], 0.0).then_inc(zeroed, 1)
            pool.memset(bones[:], 0.0).then_inc(zeroed, 1)
            pool.memset(small["ones"][:], 1.0).then_inc(masks, 1)
            pool.memset(small["minus_half"][:], -0.5).then_inc(masks, 1)
            pool.memset(small["ln_bias"][:], LN_BIAS).then_inc(masks, 1)
            pool.wait_ge(zeroed, 2)
            pool.affine_select(out=ident[:], in_=ident[:], compare_op=ALU.not_equal, fill=1.0, base=0,
                               pattern=[[-1, P]], channel_multiplier=1).then_inc(masks, 1)
            for h in range(HG):
                r = slice(h * DH, (h + 1) * DH)
                pool.wait_ge(masks, 4 + h)
                pool.memset(bones[r, r], 1.0).then_inc(masks, 1)

        @block.scalar
        def _(act):
            def load(n):
                act.dma_start(wstage[:, :, n * D:(n + 1) * D],
                              dram["wqkvT"][:, n * D:(n + 1) * D].rearrange("(k p) n -> p k n", p=P)).then_inc(wqkv_in[n], 16)

            load(0)
            act.preload_act_table_set("natural_log_exp_and_others")
            act.wait_ge(c_in, 16)
            nc.scalar.activation(ce[:], cT[:], ACT.Exp, scale=-1.0).then_inc(exp_c, 1)
            act.wait_ge(wada_in[0], 16)
            load(1)
            load(2)
            for n in range(3):
                s = slice(n * D, (n + 1) * D)
                act.wait_ge(wqkv_in[n], 16)
                nc.scalar.activation(wq_hi[:, :, s], wstage[:, :, s], ACT.Copy).then_inc(high, 1)

        @block.tensor
        def _(pe):
            pe.wait_ge(silu_c, 1)
            for n in range(NA):
                pe.wait_ge(wada_in[n], 16)
                for k in range(KT):
                    mm = nc.tensor.matmul(pa[n][0:B, :], silu[:, k, :], wada[:, k, n * CH:(n + 1) * CH],
                                          start=(k == 0), stop=(k == KT - 1))
                mm.then_inc(ada_mm, 1)

        @block.vector
        def _(dve):
            dve.wait_ge(exp_c, 1)
            nc.vector.tensor_scalar(ce[:], ce[:], 1.0, None, ALU.add).then_inc(sig_c, 1)
            dve.wait_ge(sig_c, 1)
            nc.vector.reciprocal(cs[:], ce[:]).then_inc(sig_c, 1)
            dve.wait_ge(sig_c, 2)
            nc.vector.tensor_tensor(silu, cT[:], cs[:], ALU.mult).then_inc(silu_c, 1)
            dve.wait_ge(gain_in, 64)
            nc.vector.tensor_scalar(small["x_gain"][:], gains[:, 0:1], float(D) ** 0.5, None, ALU.mult).then_inc(gain_chain, 1)
            nc.vector.tensor_scalar(small["y_gain"][:], gains[:, 1:2], float(D) ** 0.5, None, ALU.mult).then_inc(gain_chain, 1)
            nc.vector.tensor_scalar(small["s_gain"][:], gains[:, 2:3], gains[:, 3:4], float(DH) ** 0.5,
                                    ALU.mult, ALU.mult).then_inc(gain_chain, 1)
            dve.wait_ge(gain_chain, 3)
            nc.vector.tensor_scalar(tmp[:, 0:1], small["s_gain"][:], -1.0, None, ALU.mult).then_inc(gain_chain, 1)
            dve.wait_ge(gain_chain, 4)
            nc.vector.tensor_tensor(tmp[:, 1:2], tmp[:, 0:1], small["s_gain"][:], ALU.max).then_inc(gain_chain, 1)
            dve.wait_ge(gain_chain, 5)
            nc.vector.tensor_scalar(tmp[:, 2:3], tmp[:, 1:2], -1.0, SAFE, ALU.mult, ALU.add).then_inc(gain_chain, 1)
            dve.wait_ge(gain_chain, 6)
            nc.vector.tensor_scalar(small["shift"][:], tmp[:, 2:3], 0.0, None, ALU.min).then_inc(gain_chain, 1)
            for n in range(3):
                s = slice(n * D, (n + 1) * D)
                dve.wait_ge(high, n + 1)
                nc.vector.tensor_tensor(wq_lo[:, :, s], wstage[:, :, s], full(wq_hi[:, :, s]), ALU.subtract).then_inc(low, 1)
            dve.wait_ge(bias_in, 16)
            for n in range(NA):
                dve.wait_ge(ada_mm, n + 1)
                s = slice(n * CH, (n + 1) * CH)
                nc.vector.tensor_tensor(ada[:, s], pa[n][0:B, :], bada[:, s], ALU.add).then_inc(ada_out, 1)


def build_attention(nc, small, dram, wq_hi, wq_lo):
    with ExitStack() as ctx:
        def sb(name, shape, dt=F32):
            return ctx.enter_context(nc.sbuf_tensor(name, shape, dt))

        def sem(name):
            return ctx.enter_context(nc.semaphore(name))

        h_hi = sb("h_hi", [P, KT, T], F32R)
        h_lo = sb("h_lo", [P, KT, T], F32R)
        v_next = sb("v_next", [P, NT, D])
        v_now = sb("v_now", [P, NT, D])
        k_stack = [sb(f"k_stack{s}", [P, HG, T], F32R) for s in range(2)]
        q_stack = [sb(f"q_stack{h}", [P, HG, CH], F32R) for h in range(NH)]
        probs = [sb(f"probs{s}", [P, HG, CH]) for s in range(RING)]
        sums = sb("sums", [P, HG, CH])
        raw = [sb(f"raw{s}", [P, CH]) for s in range(2)]
        squares = sb("squares", [P, CH])
        norms = sb("norms", [P, CH])
        parts = sb("parts", [P, 2, CH], F32R)
        inverse = sb("inverse", [P, CH])
        compact = sb("compact", [P, SEEN])
        o_out = sb("o_out", [P, CH])
        xt = [sb(f"xt{s}", [P, D]) for s in range(XS)]
        unused = sb("unused", [P, D])
        h_full = sb("h_full", [P, KT, P])
        v_bias = sb("v_bias", [P, D])
        qk_bias = sb("qk_bias", [P, 2 * NG])
        mod = sb("mod", [P, 2 * KT])
        scale1 = sb("scale1", [P, KT])
        x_sq = sb("x_sq", [P, NT])
        x_sqc = sb("x_sqc", [P, NT])
        x_inv = sb("x_inv", [P, NT])

        scores = [ctx.enter_context(nc.psum_tensor(f"scores{p}", [P, 2, CH], F32)) for p in range(2)]
        pv = [ctx.enter_context(nc.psum_tensor(f"pv{h}", [P, CH], F32)) for h in range(NH)]
        gemm = ctx.enter_context(nc.psum_tensor("gemm", [P, CH], F32))
        aux = ctx.enter_context(nc.psum_tensor("aux", [P, CH], F32))

        ada_w = [t[:] for t in probs] + [sums[:]]
        ada_rows = [slice(i * DH, i * DH + B) for i in range(NA_LATER)]
        silu = small["silu"][:].rearrange("p (k b) -> p k b", k=KT)
        ada_w_in = [sem(f"ada_w_in{i}") for i in range(NA_LATER)]
        ada_bias_in, ada_mm, ada_made, ada_stored = sem("ada_bias_in"), sem("ada_mm_later"), sem("ada_made"), sem("ada_stored_later")
        ADA_LOAD = {3 + 2 * i: i for i in range(NA_LATER)}
        ADA_MM, ADA_MADE, ADA_STORED = 12, 13, 14

        const_in = sem("const_in")
        mod_in, mod_ready = sem("mod_in"), sem("mod_ready")
        x_in = [sem(f"x_in{s}") for s in range(XS)]
        stat, stat_clamped, inv_done, x_normed = sem("stat"), sem("stat_clamped"), sem("inv_done"), sem("x_normed")
        turned, h_moved, hi_done, lo_done = sem("turned"), sem("h_moved"), sem("hi_done"), sem("lo_done")
        v_mm, v_moved, v_copied = sem("v_mm"), sem("v_moved"), sem("v_copied")
        unit_mm, raw_done, sq_done = sem("unit_mm"), sem("raw_done"), sem("sq_done")
        ss_mm, ss_moved, ln_done, norm_done = sem("ss_mm"), sem("ss_moved"), sem("ln_done"), sem("norm_done")
        normed, part_hi, part_lo, parts_stored = sem("normed"), sem("part_hi"), sem("part_lo"), sem("parts_stored")
        k_in = [[sem(f"k_in{s}_{h}") for h in range(NH)] for s in range(2)]
        q_in = [sem(f"q_in{h}") for h in range(NH)]
        qk_mm, exp_done, pv_mm = sem("qk_mm"), sem("exp_done"), sem("pv_mm")
        add_v, add_p = sem("add_v"), sem("add_p")
        rs_mm, rows_moved, o_done, o_stored = sem("rs_mm"), sem("rows_moved"), sem("o_done"), sem("o_stored")
        rows_stored, compact_in, inverted = sem("rows_stored"), sem("compact_in"), sem("inverted")
        inverse_stored, inverse_in = sem("inverse_stored"), sem("inverse_in")
        block = ctx.enter_context(nc.Block())

        def unit_no(b, g, u):
            return b * BUNITS + g * NU + u

        def step_no(b, g, st):
            return b * BSTEPS + g * STEPS + st

        def spread_no(b, hh):
            return b * (NG * NH - 1) + hh

        def ended_at(g, st, steps):
            l = g * STEPS + st - steps
            return l // NT - 1 if l >= NT and l % NT == 0 and (st < STEPS or steps >= NT) else None

        def heads_of(engine, b, l):
            last = isinstance(b, int) and b == B - 1 and l // STEPS == NG - 1
            split = 3 if last else 2
            return slice(0, split) if engine == "vector" else slice(split, HG)

        def adds_before(l):
            return ADDS * (l // NT) + max(1, l % NT)

        def unit_at(stage, b, g, st, more, alone):
            ahead, group, u = stage.get(g * STEPS + st, (None, None, None)) if st < STEPS else (None, None, None)
            if ahead is None or (ahead == 1 and not more) or (ahead == 0 and alone):
                return None
            return b + ahead, group, u

        def tile_at(table_fast, b, g, st, more):
            at = st - (NG - 1 - g) * STEPS
            return (b + 1, table_fast[at]) if more and at in table_fast else None

        def stages(attend, b_of_loop):
            for st in range(min(FAST_STAT), STEPS + 1):
                attend(-1, NG - 1, st, True, alone=True)
            with b_of_loop(0, B - 1) as b:
                for g in range(NG):
                    for st in range(STEPS):
                        attend(b, g, st, True)
                attend(b, NG - 1, STEPS, True)
            for g in range(NG):
                for st in range(STEPS):
                    attend(B - 1, g, st, False)
            attend(B - 1, NG - 1, STEPS, False)

        @block.sync
        def _(sp):

            def load_x(b, t):
                sp.wait_ge(turned, b * NT + max(0, t - XS + 1))
                sp.dma_start(xt[t % XS][:], dram["x"][b, t * P:(t + 1) * P, :]).then_inc(x_in[t % XS], 16)

            def step(b, g, st, more, alone=False):
                fin = unit_at(FIN, b, g, st, more, alone)
                t = tile_at(FAST_STAT, b, g, st, more)
                if (alone and st == min(FAST_STAT)) or (more and g == NG - 2 and st == STEPS - NT):
                    load_x(b + 1, 0)
                    sp.wait_ge(h_moved, (b + 1) * NT)
                    sp.dma_start(mod[:], dram["ada_b"][b + 1, 0:2 * D].rearrange("(j p) -> p j", p=P),
                                 allow_slow_non_contiguous=True).then_inc(mod_in, 16)
                    for k in range(1, XS - 1):
                        load_x(b + 1, k)
                if alone and st == min(FAST_STAT):
                    sp.dma_start(v_bias[:], dram["bqkv"][2 * D:3 * D].rearrange("(a n) -> a n", a=1).broadcast_to([P, D])).then_inc(const_in, 16)
                    sp.dma_start(qk_bias[:], dram["bqkT"]).then_inc(const_in, 16)
                if t and t[1] + XS - 1 < NT:
                    load_x(t[0], t[1] + XS - 1)
                hh = None if alone else ended_at(g, st, OUT)
                if hh is not None:
                    store_o(b, hh)
                if fin:
                    fb, fg, u = fin
                    which, half = UNITS[u]
                    n = unit_no(fb, fg, u)
                    scratch = dram["parts"][u]
                    sp.wait_ge(part_lo, n + 1)
                    sp.dma_start(scratch.rearrange("c p n -> p c n"), full(parts[:])).then_inc(parts_stored, 16)
                    sp.wait_ge(parts_stored, 16 * (n + 1))
                    src = scratch.rearrange("c (h d) n -> c d h n", h=HG)
                    if which == "k":
                        dst, got = k_stack[fg % 2][:, :, half * CH:(half + 1) * CH], k_in[fg % 2][half]
                        first_step = (fb * NG + fg - 1) * STEPS
                        if alone:
                            first_step = 0
                    else:
                        dst, got = q_stack[half], q_in[half]
                        if not alone:
                            sp.wait_ge(qk_mm, 2 * ((fb * NG + fg - 1) * STEPS + (half + 1) * NT))
                    if which == "k" and not alone:
                        sp.wait_ge(qk_mm, 2 * first_step)
                    for a in range(2):
                        for c in range(2):
                            r = slice((2 * a + c) * DH, (2 * a + c + 1) * DH)
                            part = a if which == "k" else c
                            sp.dma_start(full(dst[r]), src[part]).then_inc(got, 16)
                if not alone and st == STEPS:
                    store_o(b, NG * NH - 1)

                if alone and st == ADA_STORED:
                    sp.wait_ge(ada_made, NA_LATER)
                    for i, r in enumerate(ada_rows):
                        for h in range(NH):
                            sp.dma_start(dram["ada_c"].rearrange("(b h) n -> b h n", h=NH)[:, h, i * CH:(i + 1) * CH], o_out[r, :]).then_inc(ada_stored, 16)

            def store_o(b, hh):
                sp.wait_ge(o_done, b * NG * NH + hh + 1)
                sp.dma_start(dram["heads_out"][b * NH + hh % NH, (hh // NH) * P:(hh // NH + 1) * P, :], o_out[:]).then_inc(o_stored, 16)

            stages(step, sp.Fori)
            sp.wait_ge(o_stored, 16 * B * NG * NH)
            sp.wait_ge(ada_stored, 16 * NA_LATER * NH)

        @block.tensor
        def _(pe):
            def qk(b, g, st, p):
                half, j = st // NT, st % NT
                s = g % 2
                if p == 0:
                    if st == 0 or st == NT // 2:
                        pe.wait_ge(k_in[s][st // (NT // 2)], 64 * (2 * b + g // 2 + 1))
                    if st % NT == 0:
                        pe.wait_ge(q_in[half], 64 * (NG * b + g + 1))
                n = step_no(b, g, st)
                if st > 0 or g > 0:
                    pe.wait_ge(exp_done, 2 * (n - 1) + p + 1)
                else:
                    pe.wait_ge(exp_done, 2 * BSTEPS * b)
                for i in range(2):
                    h = 2 * p + i
                    mm = nc.tensor.matmul(scores[p][:, i, :], k_stack[s][:, h, j * P:(j + 1) * P], q_stack[half][:, h, :],
                                          start=True, stop=True)
                mm.then_inc(qk_mm, 1)

            def weigh(b, l):
                g, st = l // STEPS, l % STEPS
                half, j = st // NT, st % NT
                n = b * BSTEPS + l
                pe.wait_ge(exp_done, 2 * n + 2)
                if g == 0 and half == 0:
                    pe.wait_ge(v_copied, b * NT + j + 1)
                if j == 0:
                    pe.wait_ge(o_done, b * NG * NH + max(0, g * NH + half - NH + 1))
                for h in range(HG):
                    mm = nc.tensor.matmul(pv[half][h * DH:(h + 1) * DH, :], v_now[:, j, (g * HG + h) * DH:(g * HG + h + 1) * DH],
                                          probs[l % RING][:, h, :], start=(j == 0), stop=(j == NT - 1))
                mm.then_inc(pv_mm, 1)

            def row_sums(b, hh, waits):
                pe.wait_ge(add_v, (b * NG * NH + hh + 1) * ADDS)
                pe.wait_ge(add_p, (b * NG * NH + hh + 1) * ADDS)
                aux_wait(waits)
                for h in range(HG):
                    mm = nc.tensor.matmul(aux[h * DH:(h + 1) * DH, :], small["ones"][:], sums[:, h, :], start=True, stop=True)
                mm.then_inc(rs_mm, 1)

            def aux_wait(waits):
                for s, v in waits:
                    pe.wait_ge(s, v)

            def aux_before(b, g, st, more, alone, kind):
                first = g * STEPS + st + (kind == "turn")
                coming = [(l // BSTEPS + SUM[l % BSTEPS][0], *SUM[l % BSTEPS][1:]) for l in range(first, first + BSTEPS)
                          if l % BSTEPS in SUM]
                ahead, group, u = [x for x in coming if not (alone and x[0] == 0)][0]
                if not more and ahead > 0:
                    group, u = 0, 0
                done = [(ss_moved, unit_no(b + ahead, group, u))]
                done.append((h_moved, (b + 1) * NT + (sum(1 for s in FAST_TURN if s < st) if more and g == NG - 1 else 0)))
                if not alone:
                    l = g * STEPS + st
                    ended = sum(1 for m in range(NT + ROWS, l + 1, NT) if m < l or kind != "rows")
                    done.append((rows_moved, b * NG * NH + ended))
                return done

            def gemm_free(b, g, st):
                fast = g == NG - 1
                if fast:
                    pe.wait_ge(v_moved, (b + 1) * NT + sum(1 for s in FAST_V if s < st))
                    pe.wait_ge(raw_done, unit_no(b + 1, 0, 0) + sum(1 for s in FAST_END if s < st))
                else:
                    pe.wait_ge(v_moved, (b + 1) * NT)
                    pe.wait_ge(raw_done, unit_no(b, g + 1, SLOW[g][st][0]))

            def unit_products(b, g, u, lo, hi):
                which, half = UNITS[u]
                at = (0 if which == "q" else D) + g * P
                c = slice(half * CH, (half + 1) * CH)
                terms = [(w, h, k) for k in range(KT) for w, h in ((wq_hi, h_hi), (wq_hi, h_lo), (wq_lo, h_hi))]
                for n in range(lo, hi):
                    w, h, k = terms[n]
                    mm = nc.tensor.matmul(gemm[:], w[:, k, at:at + P], h[:, k, c], start=(n == 0), stop=(n == len(terms) - 1))
                if hi == len(terms):
                    mm.then_inc(unit_mm, 1)

            def v_products(t, lo, hi):
                c = slice(t * P, (t + 1) * P)
                terms = [(h, w, k) for k in range(KT) for h, w in ((h_hi, wq_hi), (h_hi, wq_lo), (h_lo, wq_hi))]
                for n in range(lo, hi):
                    h, w, k = terms[n]
                    mm = nc.tensor.matmul(gemm[:], h[:, k, c], w[:, k, 2 * D:3 * D], start=(n == 0), stop=(n == len(terms) - 1))
                if hi == len(terms):
                    mm.then_inc(v_mm, 1)

            def fill(b, g, st, more, part, alone):
                N = 3 * KT
                if g < NG - 1 and st in SLOW[g]:
                    u, i, steps = SLOW[g][st]
                    if part == 0 and i == 0:
                        gemm_free(b, g, st)
                    lo, mid, hi = i * N // steps, i * N // steps + N // steps // 2, (i + 1) * N // steps
                    unit_products(b, g + 1, u, *((lo, mid) if part == 0 else (mid, hi)))
                if g == NG - 1 and more and st in FAST:
                    kind, x = FAST[st]
                    if part == 0:
                        gemm_free(b, g, st)
                        if kind == "v":
                            pe.wait_ge(lo_done, (b + 1) * NT + x + 1)
                        else:
                            pe.wait_ge(lo_done, (b + 1) * NT + (UNITS[x][1] + 1) * CT)
                    lo = part * N // 2
                    if kind == "v":
                        v_products(x, lo, lo + N // 2)
                    else:
                        unit_products(b + 1, 0, x, lo, lo + N // 2)
                if part == 1:
                    un = unit_at(SUM, b, g, st, more, alone)
                    if un:
                        pe.wait_ge(sq_done, unit_no(*un) + 1)
                        aux_wait(aux_before(b, g, st, more, alone, "squares"))
                        nc.tensor.matmul(aux[:], small["head_ones"][:], squares[:], start=True, stop=True).then_inc(ss_mm, 1)
                    t = tile_at(FAST_TURN, b, g, st, more)
                    if t:
                        pe.wait_ge(x_normed, t[0] * NT + t[1] + 1)
                        aux_wait(aux_before(b, g, st, more, alone, "turn"))
                        for k in range(KT):
                            mm = nc.tensor.transpose(aux[:, k * P:(k + 1) * P], xt[t[1] % XS][:, k * P:(k + 1) * P], small["ident"][:])
                        mm.then_inc(turned, 1)

            def step(b, g, st, more, alone=False):
                l = g * STEPS + st
                if alone:
                    fill(b, g, st, more, 0, True)
                    fill(b, g, st, more, 1, True)
                    if st == ADA_MM:
                        for k in range(KT):
                            for i, r in enumerate(ada_rows):
                                if k == 0:
                                    pe.wait_ge(ada_w_in[i], 16)
                                mm = nc.tensor.matmul(scores[0][r, 0, :], silu[:, k, :], ada_w[i][:, k, :], start=(k == 0), stop=(k == KT - 1))
                        mm.then_inc(ada_mm, 1)
                    if st == STEPS:
                        pe.wait_ge(ada_made, NA_LATER)
                    return
                if st == STEPS:
                    weigh(b, l - 1)
                    row_sums(b, NG * NH - 1, aux_before(b, g, st, more, False, "rows"))
                    return
                qk(b, g, st, 0)
                fill(b, g, st, more, 0, False)
                qk(b, g, st, 1)
                if l > NT and l % NT == ROWS:
                    row_sums(b, l // NT - 1, aux_before(b, g, st, more, False, "rows"))
                fill(b, g, st, more, 1, False)
                if l > 0:
                    weigh(b, l - 1)

            stages(step, pe.Fori)

        @block.scalar
        def _(act):
            act.preload_act_table_set("natural_log_exp_and_others")

            def step(b, g, st, more, alone=False):
                l = g * STEPS + st
                if alone and st in ADA_LOAD:
                    i = ADA_LOAD[st]
                    cols = slice((NA_NOW + i) * CH, (NA_NOW + i + 1) * CH)
                    act.dma_start(ada_w[i], dram["wadaT"][:, cols].rearrange("(k p) n -> p k n", p=P)).then_inc(ada_w_in[i], 16)
                    act.dma_start(inverse[ada_rows[i], :], dram["bada"][cols].rearrange("(a n) -> a n", a=1).broadcast_to([B, CH])).then_inc(ada_bias_in, 16)
                if alone and st == STEPS:
                    act.wait_ge(ada_made, NA_LATER)
                t = tile_at(FAST_SPLIT, b, g, st, more)
                if t:
                    act.wait_ge(h_moved, t[0] * NT + t[1] + 1)
                    nc.scalar.activation(h_hi[:, :, t[1] * P:(t[1] + 1) * P], h_full[:], ACT.Copy).then_inc(hi_done, 1)
                for p in range(2):
                    if not alone and st < STEPS:
                        if l >= RING:
                            if p == 0:
                                act.wait_ge(pv_mm, b * BSTEPS + l - RING + 1)
                                act.wait_ge(add_v, b * NG * NH * ADDS + adds_before(l - RING))
                            else:
                                act.wait_ge(add_p, b * NG * NH * ADDS + adds_before(l - RING))
                        elif l == 0:
                            act.wait_ge(pv_mm, b * BSTEPS)
                            act.wait_ge(add_v, b * NG * NH * ADDS)
                            act.wait_ge(add_p, b * NG * NH * ADDS)
                        act.wait_ge(qk_mm, 2 * step_no(b, g, st) + p + 1)
                        nc.scalar.activation(probs[l % RING][:, 2 * p:2 * p + 2, :], scores[p][:], ACT.Exp,
                                             bias=small["shift"][:]).then_inc(exp_done, 1)
                hh = None if alone else ended_at(g, st, ROWS)
                if hh is not None:
                    n = b * NG * NH + hh
                    act.wait_ge(rs_mm, n + 1)
                    act.wait_ge(o_done, n)
                    nc.scalar.activation(inverse[:], aux[:], ACT.Copy).then_inc(rows_moved, 1)
                    act.wait_ge(rows_moved, n + 1)
                    act.dma_start(dram["rows"], inverse[0:P:DH, :]).then_inc(rows_stored, 16)
                hh = None if alone else ended_at(g, st, COMPACT)
                if hh is not None:
                    act.wait_ge(rows_stored, 16 * (spread_no(b, hh) + 1))
                    act.dma_start(compact[:], dram["rows"].rearrange("h (r n) -> (h r) n", n=SEEN)).then_inc(compact_in, 16)
                hh = None if alone else ended_at(g, st, INVERTED)
                if hh is not None:
                    act.wait_ge(inverted, spread_no(b, hh) + 1)
                    act.dma_start(dram["inverse"].rearrange("h (r n) -> (h r) n", n=SEEN), compact[:]).then_inc(inverse_stored, 16)
                hh = None if alone else ended_at(g, st, SPREAD)
                if hh is not None:
                    act.wait_ge(inverse_stored, 16 * (spread_no(b, hh) + 1))
                    for h in range(HG):
                        act.dma_start(inverse[h * DH:(h + 1) * DH, :], dram["inverse"][h:h + 1, :].broadcast_to([DH, CH])).then_inc(inverse_in, 16)
                un = unit_at(INV, b, g, st, more, alone)
                if un:
                    n = unit_no(*un)
                    act.wait_ge(ss_moved, n + 1)
                    nc.scalar.activation(norms[:], norms[:], ACT.Ln, scale=LN_SCALE).then_inc(ln_done, 1)
                    act.wait_ge(ln_done, n + 1)
                    nc.scalar.activation(norms[:], norms[:], ACT.Exp, scale=-0.5, bias=small["ln_bias"][:]).then_inc(norm_done, 1)

            stages(step, act.Fori)

        @block.gpsimd
        def _(pool):
            def add(b, l):
                j = l % NT
                heads = heads_of("gpsimd", b, l)
                hh = b * NG * NH + l // NT
                if j == 0:
                    return
                pool.wait_ge(exp_done, 2 * (b * BSTEPS + l) + 2)
                if j == 1:
                    pool.wait_ge(rs_mm, hh)
                    a = probs[(l - 1) % RING][:, heads, :]
                else:
                    pool.wait_ge(add_p, hh * ADDS + j - 1)
                    a = sums[:, heads, :]
                nc.gpsimd.tensor_tensor(sums[:, heads, :], a, probs[l % RING][:, heads, :], ALU.add).then_inc(add_p, 1)

            def step(b, g, st, more, alone=False):
                l = g * STEPS + st
                t = tile_at(FAST_SPLIT, b, g, st, more)
                if t:
                    c = slice(t[1] * P, (t[1] + 1) * P)
                    pool.wait_ge(hi_done, t[0] * NT + t[1] + 1)
                    nc.gpsimd.tensor_tensor(h_lo[:, :, c], h_full[:], full(h_hi[:, :, c]), ALU.subtract).then_inc(lo_done, 1)
                if not alone and l > 0:
                    add(b, l - 1)
                t = tile_at(FAST_STAT, b, g, st, more)
                if t:
                    n, k = t[0] * NT + t[1], t[1]
                    pool.wait_ge(stat_clamped, n + 1)
                    nc.gpsimd.tensor_tensor(x_inv[:, k:k + 1], x_sqc[:, k:k + 1], small["minus_half"][:, 0:1], ALU.pow).then_inc(inv_done, 1)
                un = unit_at(RAW, b, g, st, more, alone)
                if un:
                    n, r = unit_no(*un), raw[un[2] % 2]
                    pool.wait_ge(raw_done, n + 1)
                    pool.wait_ge(ss_mm, n)
                    nc.gpsimd.tensor_tensor(squares[:], r[:], r[:], ALU.mult).then_inc(sq_done, 1)

            stages(step, pool.Fori)

        @block.vector
        def _(dve):
            def add(b, l):
                j = l % NT
                heads = heads_of("vector", b, l)
                hh = b * NG * NH + l // NT
                if j == 0:
                    return
                dve.wait_ge(exp_done, 2 * (b * BSTEPS + l) + (heads.stop + 1) // 2)
                if j == 1:
                    dve.wait_ge(rs_mm, hh)
                    a = probs[(l - 1) % RING][:, heads, :]
                else:
                    dve.wait_ge(add_v, hh * ADDS + j - 1)
                    a = sums[:, heads, :]
                nc.vector.tensor_tensor(sums[:, heads, :], a, probs[l % RING][:, heads, :], ALU.add).then_inc(add_v, 1)

            def output(b, hh):
                n = b * NG * NH + hh
                if hh == 0:
                    dve.wait_ge(ada_stored, 16 * NA_LATER * NH)
                if hh < NG * NH - 1:
                    dve.wait_ge(inverse_in, 16 * HG * (spread_no(b, hh) + 1))
                else:
                    dve.wait_ge(rs_mm, n + 1)
                    dve.wait_ge(o_done, n)
                    nc.vector.reciprocal(inverse[:], aux[:]).then_inc(rows_moved, 1)
                    dve.wait_ge(rows_moved, n + 1)
                dve.wait_ge(pv_mm, b * BSTEPS + (hh + 1) * NT)
                dve.wait_ge(o_stored, 16 * n)
                nc.vector.tensor_tensor(o_out[:], pv[hh % NH][:], inverse[:], ALU.mult).then_inc(o_done, 1)

            def invert(b, hh):
                dve.wait_ge(compact_in, 16 * (spread_no(b, hh) + 1))
                nc.vector.reciprocal(compact[:], compact[:]).then_inc(inverted, 1)

            def raw_out(un, alone):
                n = unit_no(*un)
                which, _ = UNITS[un[2]]
                col = (0 if which == "q" else NG) + un[1]
                dve.wait_ge(unit_mm, n + 1)
                if not alone or un[2] >= 2:
                    dve.wait_ge(part_lo, n - 1)
                nc.vector.tensor_scalar(raw[un[2] % 2][:], gemm[:], qk_bias[:, col:col + 1], None, ALU.add).then_inc(raw_done, 1)

            def v_out(b, t):
                dve.wait_ge(v_mm, b * NT + t + 1)
                if t == 0:
                    dve.wait_ge(const_in, 32)
                dve.wait_ge(v_copied, b * NT)
                nc.vector.tensor_tensor(v_next[:, t, :], gemm[:], v_bias[:], ALU.add).then_inc(v_moved, 1)

            def statistics(b, t):
                n = b * NT + t
                dve.wait_ge(x_in[t % XS], 16 * (b * len(range(t % XS, NT, XS)) + t // XS + 1))
                dve.wait_ge(stat_clamped, n)
                nc.vector.tensor_tensor_reduce(unused[:], xt[t % XS][:], xt[t % XS][:], 1.0, 0.0, ALU.mult, ALU.add,
                                               x_sq[:, t:t + 1]).then_inc(stat, 1)
                dve.wait_ge(stat, n + 1)
                nc.vector.tensor_scalar(x_sqc[:, t:t + 1], x_sq[:, t:t + 1], EPS2, None, ALU.max).then_inc(stat_clamped, 1)

            def normalise(b, t):
                dve.wait_ge(inv_done, b * NT + t + 1)
                nc.vector.tensor_scalar(xt[t % XS][:], xt[t % XS][:], x_inv[:, t:t + 1], small["x_gain"][:],
                                        ALU.mult, ALU.mult).then_inc(x_normed, 1)

            def h_out(b, t):
                n = b * NT + t
                if t == 0:
                    dve.wait_ge(mod_in, 16 * (b + 1))
                    dve.wait_ge(h_moved, n)
                    nc.vector.tensor_scalar(scale1[:], mod[:, KT:2 * KT], 1.0, None, ALU.add).then_inc(mod_ready, 1)
                dve.wait_ge(turned, n + 1)
                dve.wait_ge(mod_ready, b + 1)
                dve.wait_ge(lo_done, n)
                for k in range(KT):
                    mv = nc.vector.tensor_scalar(h_full[:, k, :], aux[:, k * P:(k + 1) * P], scale1[:, k:k + 1],
                                                 mod[:, k:k + 1], ALU.mult, ALU.add)
                mv.then_inc(h_moved, 1)

            def sums_out(un):
                dve.wait_ge(ss_mm, unit_no(*un) + 1)
                dve.wait_ge(normed, unit_no(*un))
                nc.vector.tensor_scalar(norms[:], aux[:], EPS2, None, ALU.max).then_inc(ss_moved, 1)

            def make_parts(un):
                n, r = unit_no(*un), raw[un[2] % 2]
                dve.wait_ge(norm_done, n + 1)
                nc.vector.scalar_tensor_tensor(r[:], norms[:], 1.0 / EPS2 ** 0.5, r[:], ALU.min, ALU.mult).then_inc(normed, 1)
                dve.wait_ge(normed, n + 1)
                dve.wait_ge(parts_stored, 16 * n)
                gain = small["s_gain"][:] if UNITS[un[2]][0] == "q" else 1.0
                nc.vector.tensor_scalar(parts[:, 0, :], r[:], gain, None, ALU.mult).then_inc(part_hi, 1)
                dve.wait_ge(part_hi, n + 1)
                nc.vector.scalar_tensor_tensor(parts[:, 1, :], r[:], gain, full(parts[:, 0, :]), ALU.mult, ALU.subtract).then_inc(part_lo, 1)

            def step(b, g, st, more, alone=False):
                l = g * STEPS + st
                if not alone and l < NT - AHEAD:
                    take_v(b, l + AHEAD)
                raw_u = unit_at(RAW, b, g, st, more, alone)
                sum_u = unit_at(INV, b, g, st, more, alone)
                fin_u = unit_at(FIN, b, g, st, more, alone)
                fin_first = fin_u and raw_u and (raw_u[2] - fin_u[2]) % 2 == 0
                fin_second = fin_u and sum_u and not fin_first
                if fin_first:
                    make_parts(fin_u)
                if raw_u:
                    raw_out(raw_u, alone)
                t = tile_at(FAST_VOUT, b, g, st, more)
                if t:
                    v_out(*t)
                t = tile_at(FAST_TURN, b, g, st, more)
                if t:
                    normalise(*t)
                if fin_second:
                    make_parts(fin_u)
                if not alone and ended_at(g, st, OUT) is not None:
                    output(b, ended_at(g, st, OUT))
                if not alone and ended_at(g, st, INVERT) is not None:
                    invert(b, ended_at(g, st, INVERT))
                if sum_u:
                    sums_out(sum_u)
                if not alone and l > 0:
                    add(b, l - 1)
                t = tile_at(FAST_HOUT, b, g, st, more)
                if t:
                    h_out(*t)
                t = tile_at(FAST_STAT, b, g, st, more)
                if t:
                    statistics(*t)
                if fin_u and not fin_first and not fin_second:
                    make_parts(fin_u)
                if alone and st == ADA_MADE:
                    dve.wait_ge(ada_mm, 1)
                    dve.wait_ge(ada_bias_in, 16 * NA_LATER)
                    for r in ada_rows:
                        nc.vector.tensor_tensor(o_out[r, :], scores[0][r, 0, :], inverse[r, :], ALU.add).then_inc(ada_made, 1)
                if st == STEPS and more:
                    dve.wait_ge(pv_mm, (b + 1) * BSTEPS)
                    for j in range(AHEAD):
                        take_v(b + 1, j)
                if not alone and st == STEPS:
                    output(b, NG * NH - 1)

            def take_v(b, j):
                dve.wait_ge(v_moved, b * NT + j + 1)
                nc.vector.tensor_copy(v_now[:, j, :], v_next[:, j, :]).then_inc(v_copied, 1)

            stages(step, dve.Fori)


def build_mlp(nc, small, dram):
    with ExitStack() as ctx:
        def sb(name, shape, dt=F32):
            return ctx.enter_context(nc.sbuf_tensor(name, shape, dt))

        def sem(name):
            return ctx.enter_context(nc.semaphore(name))

        wp = [sb(f"wp_{x}", [P, KT, D], F32R) for x in ("hi", "lo")]
        w1 = [sb(f"w1_{x}", [P, KT, FF], F32R) for x in ("hi", "lo")]
        w2 = [sb(f"w2_{x}", [P, NM, D], F32R) for x in ("hi", "lo")]
        z = [sb(f"z_{x}", [P, KT, CH], F32R) for x in ("hi", "lo")]
        act_full = [sb(f"act_full{s}", [P, CH]) for s in range(2)]
        act_parts = [sb(f"act_parts{s}", [P, 2, CH], F32R) for s in range(2)]
        heads = [sb(f"heads{s}", [P, KT, P]) for s in range(2)]
        heads_parts = sb("heads_parts", [P, 2, KT, P], F32R)
        y = sb("y", [P, CT, D])
        y_next = sb("y_next", [P, CT, D])
        x_tile = sb("x_tile", [P, D])
        y_norm = [sb(f"y_norm{s}", [P, D]) for s in range(2)]
        z_full = [sb(f"z_full{s}", [P, KT, P]) for s in range(2)]
        result = [sb(f"result{s}", [P, D]) for s in range(2)]
        gate1, gate2 = sb("gate1", [P, D]), sb("gate2", [P, D])
        p_bias, f2_bias = sb("p_bias", [P, D]), sb("f2_bias", [P, D])
        f1_bias = sb("f1_bias", [P, NM])
        gated_bias = sb("gated_bias", [P, D])
        mod = sb("mod_mlp", [P, 2 * KT])
        scale1 = sb("scale1_mlp", [P, KT])
        y_sq, y_sqc, y_inv = sb("y_sq", [P, CT]), sb("y_sqc", [P, CT]), sb("y_inv", [P, CT])
        heads_first = [heads[0][:], heads[1][:]] + [a.rearrange("p (k n) -> p k n", k=KT) for a in (act_full[0], act_full[1])]
        x_first = [x_tile[:]] + [a.rearrange("p k n -> p (k n)") for a in (z_full[0], z_full[1])] + [gated_bias[:]]
        stage = [y[:, s, :] for s in range(CT)] + [result[0][:], result[1][:]]

        acc = [ctx.enter_context(nc.psum_tensor(f"acc{t}", [P, D], F32)) for t in range(CT)]
        up = [ctx.enter_context(nc.psum_tensor(f"up{s}", [P, CH], F32)) for s in range(2)]
        proj = ctx.enter_context(nc.psum_tensor("proj", [P, D], F32))
        turn = ctx.enter_context(nc.psum_tensor("turn", [P, KT * P], F32))

        const_in, p_bias_in = sem("const_in_mlp"), sem("p_bias_in")
        proj_bias_gated, x_biased, z_moved_too = sem("proj_bias_gated"), sem("x_biased"), sem("z_moved_too")
        w_in = [sem(f"w_in{s}") for s in range(len(stage))]
        heads_first_in = [sem(f"heads_first_in{t}") for t in range(CT)]
        x_first_in = [sem(f"x_first_in{t}") for t in range(CT)]
        w_high, w_low = sem("w_high"), sem("w_low")
        x_in, gate1_in, gate2_in, mod_in = sem("x_in_mlp"), sem("gate1_in"), sem("gate2_in"), sem("mod_in_mlp")
        heads_hi, heads_lo, proj_mm, proj_moved = sem("heads_hi"), sem("heads_lo"), sem("proj_mm"), sem("proj_moved")
        heads_in = [sem(f"heads_in{s}") for s in range(2)]
        y_taken = sem("y_taken")
        y_gated, y_done, y_stat, y_clamped, y_inverse = sem("y_gated"), sem("y_done"), sem("y_stat"), sem("y_clamped"), sem("y_inverse")
        mod_ready, y_normed, turned, z_moved, z_hi, z_lo = (sem(x) for x in ("mod_ready_mlp", "y_normed", "turned_mlp", "z_moved", "z_hi_done", "z_lo_done"))
        up_mm, gelu_done, act_hi, act_lo = sem("up_mm"), sem("gelu_done"), sem("act_hi"), sem("act_lo")
        down_mm, acc_mm, acc_moved, out_done = (sem(x) for x in ("down_mm", "acc_mm", "acc_moved", "out_done"))
        bias_gated, y_biased = sem("bias_gated"), sem("y_biased")
        out_stored = [sem(f"out_stored{s}") for s in range(2)]
        block = ctx.enter_context(nc.Block())

        pieces = [(wp, slice(None), k) for k in range(KT)]
        for m in range(NM):
            pieces += [(w1, m, None), (w2, None, m)]
        NW = len(pieces)
        EARLY = 2 * len(stage)
        LATE = len(stage) - CT
        slot = [n % len(stage) if n < EARLY else CT + (n - EARLY) % LATE for n in range(NW)]
        turn_of = [slot[:n].count(slot[n]) for n in range(NW)]
        before = [max([k for k in range(n) if slot[k] == slot[n]], default=None) for n in range(NW)]

        def piece(parts_of, which):
            w, a, b = parts_of
            if w is w1:
                return w[which][:, :, a * P:(a + 1) * P]
            return w[which][:, b, :]

        def piece_shape(n, ap):
            return ap.rearrange("p (k m) -> p k m", k=KT) if pieces[n][0] is w1 else ap

        SPLIT = {2 + 3 * t: t for t in range(CT)}
        PROJ = {3 + 3 * t: t for t in range(CT)}
        MAKE = {4 + 3 * t: t for t in range(CT)}
        NORM = 13
        BIAS = 2
        LAG = 2

        def turn_bank(c, t, k):
            if is_first(c):
                return acc[t] if k < KT // 2 else (up[0], up[1], proj, turn)[t]
            return turn

        def late(m):
            return range(EARLY + LATE * m, min(NW, EARLY + LATE * (m + 1)))

        def nothing(*_):
            pass

        def is_first(c):
            return isinstance(c, int) and c == 0

        def chunks(first, prepare, turn_tile, mlp, finish, fori):
            def chunk(c, more):
                for m in range(NM - 1):
                    mlp(c, m)
                    if more:
                        prepare(c + 1, m)
                for t in range(CT):
                    if t == CT // 2:
                        mlp(c, NM - 1)
                    if more:
                        turn_tile(c + 1, t)
                for t in range(CT):
                    finish(c, t)

            first()
            chunk(0, True)
            with fori(1, NC - 1) as c:
                chunk(c, True)
            chunk(NC - 1, False)

        @block.sync
        def _(sp):
            def load_heads(c, t, tile, signal):
                sp.dma_start(tile, dram["heads_out"][c, :, t * P:(t + 1) * P].rearrange("(k p) n -> p k n", p=P)).then_inc(signal, 16)

            def load_x(c, t, tile, signal):
                sp.dma_start(tile, dram["x"].rearrange("b (h n) d -> (b h) n d", h=NH)[c, t * P:(t + 1) * P, :]).then_inc(signal, 16)

            def load_gate(c):
                sp.dma_start(gate1[:], dram["ada_c"][bass.ts(c, 1), 0:D].broadcast_to([P, D])).then_inc(gate1_in, 16)

            def load_mod(c):
                sp.dma_start(mod[:], dram["ada_c"][c, D:3 * D].rearrange("(j p) -> p j", p=P),
                             allow_slow_non_contiguous=True).then_inc(mod_in, 16)

            def first():
                for t in range(CT):
                    load_heads(0, t, heads_first[t], heads_first_in[t])
                    if t == 0:
                        sp.dma_start(p_bias[:], dram["bproj"].rearrange("(a n) -> a n", a=1).broadcast_to([P, D])).then_inc(p_bias_in, 16)
                        load_gate(0)
                    load_x(0, t, x_first[t], x_first_in[t])
                load_mod(0)
                sp.dma_start(f1_bias[:], dram["bfc1T"]).then_inc(const_in, 16)
                sp.dma_start(f2_bias[:], dram["bfc2"].rearrange("(a n) -> a n", a=1).broadcast_to([P, D])).then_inc(const_in, 16)

            def prepare(c, m):
                if m == 0:
                    sp.wait_ge(y_done, CT * c)
                    load_gate(c)
                    sp.wait_ge(z_hi, CT * c)
                    load_mod(c)
                if m + 1 in SPLIT:
                    t = SPLIT[m + 1]
                    sp.wait_ge(heads_lo, CT * c + max(0, t - 1))
                    load_heads(c, t, heads[t % 2][:], heads_in[t % 2])
                    sp.wait_ge(y_done, CT * c + t)
                    load_x(c, t, x_tile[:], x_in)

            def mlp(c, m):
                if m == 0:
                    sp.wait_ge(out_done, CT * c)
                    sp.wait_ge(bias_gated, c)
                    sp.dma_start(gate2[:], dram["ada_c"][bass.ts(c, 1), 3 * D:4 * D].broadcast_to([P, D])).then_inc(gate2_in, 16)

            def finish(c, t):
                sp.wait_ge(out_done, CT * c + t + 1)
                sp.dma_start(dram["out"].rearrange("b (h n) d -> (b h) n d", h=NH)[c, t * P:(t + 1) * P, :],
                             result[t % 2][:]).then_inc(out_stored[t % 2], 16)

            chunks(first, prepare, nothing, mlp, finish, sp.Fori)
            for s in range(2):
                sp.wait_ge(out_stored[s], 16 * NC * CT // 2)

        @block.scalar
        def _(act):
            w_dram = {id(wp): dram["wprojT"], id(w1): dram["wfc1T"], id(w2): dram["wfc2T"]}

            def load(n):
                w, a, b = pieces[n]
                src = w_dram[id(w)].rearrange("(k p) n -> p k n", p=P)
                src = src[:, :, a * P:(a + 1) * P] if w is w1 else src[:, b, :]
                if before[n] is not None:
                    act.wait_ge(w_low, before[n] + 1)
                act.dma_start(piece_shape(n, stage[slot[n]]), src).then_inc(w_in[slot[n]], 16)

            def split_high(n):
                act.wait_ge(w_in[slot[n]], 16 * (turn_of[n] + 1))
                nc.scalar.activation(piece(pieces[n], 0), piece_shape(n, stage[slot[n]]), ACT.Copy).then_inc(w_high, 1)

            def first():
                for n in range(len(stage)):
                    load(n)
                act.preload_act_table(ACT.Gelu_apprx_tanh)
                for k in range(KT):
                    split_high(k)
                    act.wait_ge(heads_first_in[k], 16)
                    nc.scalar.activation(z[0][:, :, k * P:(k + 1) * P], heads_first[k], ACT.Copy).then_inc(heads_hi, 1)
                for n in range(KT, len(stage)):
                    split_high(n)
                for n in range(len(stage), EARLY):
                    load(n)
                split_high(len(stage))
                for t in range(CT):
                    turn_tile(0, t)
                for n in range(len(stage) + 1, EARLY):
                    split_high(n)
                act.wait_ge(const_in, 32)

            def turn_tile(c, t):
                act.wait_ge(up_mm, NM * c)
                if is_first(c):
                    act.wait_ge(turned, t + 1)
                    act.wait_ge(mod_ready, 1)
                    if t >= 2:
                        act.wait_ge(z_lo, t - 1)
                    for k in range(KT // 2, KT):
                        mv = nc.scalar.activation(z_full[t % 2][:, k, :], turn_bank(c, t, k)[:, k * P:(k + 1) * P], ACT.Identity,
                                                  scale=scale1[:, k:k + 1], bias=mod[:, k:k + 1])
                    mv.then_inc(z_moved_too, 1)
                    act.wait_ge(z_moved_too, t + 1)
                act.wait_ge(z_moved, CT * c + t + 1)
                nc.scalar.activation(z[0][:, :, t * P:(t + 1) * P], z_full[t % 2][:], ACT.Copy).then_inc(z_hi, 1)

            def mlp(c, m):
                n = NM * c + m
                more_weights = late(m) if is_first(c) else ()
                for k in more_weights:
                    load(k)
                act.wait_ge(up_mm, n + 1)
                if m >= 2:
                    act.wait_ge(act_lo, n - 1)
                else:
                    act.wait_ge(act_lo, NM * c)
                nc.scalar.activation(act_full[m % 2][:], up[m % 2][:], ACT.Gelu_apprx_tanh, bias=f1_bias[:, m:m + 1]).then_inc(gelu_done, 1)
                act.wait_ge(gelu_done, n + 1)
                if m >= 2:
                    act.wait_ge(down_mm, (NM - 1) * c + m - 1)
                else:
                    act.wait_ge(acc_mm, CT * c)
                nc.scalar.activation(act_parts[m % 2][:, 0, :], act_full[m % 2][:], ACT.Copy).then_inc(act_hi, 1)
                for k in more_weights:
                    split_high(k)

            chunks(first, nothing, turn_tile, mlp, nothing, act.Fori)

        @block.gpsimd
        def _(pool):
            def first():
                gated = y_next[:, CT - 1, :]
                for t in range(CT):
                    r = slice(t * P, (t + 1) * P)
                    pool.wait_ge(heads_hi, t + 1)
                    nc.gpsimd.tensor_tensor(z[1][:, :, r], heads_first[t], full(z[0][:, :, r]), ALU.subtract).then_inc(heads_lo, 1)
                    if t == 0:
                        pool.wait_ge(p_bias_in, 16)
                        pool.wait_ge(gate1_in, 16)
                        nc.gpsimd.tensor_tensor(gated, gate1[:], p_bias[:], ALU.mult).then_inc(proj_bias_gated, 1)
                        pool.wait_ge(proj_bias_gated, 1)
                    pool.wait_ge(x_first_in[t], 16)
                    nc.gpsimd.tensor_tensor(x_first[t], x_first[t], gated, ALU.add).then_inc(x_biased, 1)
                prepare(0, NORM)
                for t in range(CT):
                    turn_tile(0, t)
                pool.wait_ge(const_in, 32)

            def prepare(c, m):
                if m == NORM:
                    pool.wait_ge(y_clamped, c + 1)
                    nc.gpsimd.tensor_tensor(y_inv[:], y_sqc[:], small["minus_half"][:, 0:CT], ALU.pow).then_inc(y_inverse, 1)

            def turn_tile(c, t):
                r = slice(t * P, (t + 1) * P)
                pool.wait_ge(z_hi, CT * c + t + 1)
                nc.gpsimd.tensor_tensor(z[1][:, :, r], z_full[t % 2][:], full(z[0][:, :, r]), ALU.subtract).then_inc(z_lo, 1)

            def mlp(c, m):
                if m == BIAS:
                    pool.wait_ge(gate2_in, 16 * (c + 1))
                    nc.gpsimd.tensor_tensor(gated_bias[:], gate2[:], f2_bias[:], ALU.mult).then_inc(bias_gated, 1)
                if BIAS < m <= BIAS + CT:
                    t = m - BIAS - 1
                    pool.wait_ge(bias_gated, c + 1)
                    pool.wait_ge(y_taken, c + 1)
                    nc.gpsimd.tensor_tensor(y[:, t, :], y[:, t, :], gated_bias[:], ALU.add).then_inc(y_biased, 1)
                pool.wait_ge(act_hi, NM * c + m + 1)
                nc.gpsimd.tensor_tensor(act_parts[m % 2][:, 1, :], act_full[m % 2][:], full(act_parts[m % 2][:, 0, :]), ALU.subtract).then_inc(act_lo, 1)

            chunks(first, prepare, turn_tile, mlp, nothing, pool.Fori)

        @block.tensor
        def _(pe):
            pairs = ((0, 0), (0, 1), (1, 0))

            def prepare(c, m):
                if m in PROJ:
                    t = PROJ[m]
                    pe.wait_ge(heads_lo, CT * c + t + 1)
                    pe.wait_ge(proj_moved, CT * c + t)
                    for k in range(KT):
                        for i, (a, b) in enumerate(pairs):
                            mm = nc.tensor.matmul(proj[:], heads_parts[:, b, k, :], wp[a][:, k, :],
                                                  start=(k == 0 and i == 0), stop=(k == KT - 1 and i == 2))
                    mm.then_inc(proj_mm, 1)

            def turn_tile(c, t):
                pe.wait_ge(y_normed, CT * c + t + 1)
                if not is_first(c):
                    pe.wait_ge(z_moved, CT * c + t)
                for k in range(KT):
                    mm = nc.tensor.transpose(turn_bank(c, t, k)[:, k * P:(k + 1) * P], y_norm[t % 2][:, k * P:(k + 1) * P], small["ident"][:])
                mm.then_inc(turned, 1)

            def down(c, m, tiles):
                if tiles[0] == 0:
                    pe.wait_ge(act_lo, NM * c + m + 1)
                    pe.wait_ge(w_low, KT + 2 * m + 2)
                for t in tiles:
                    if m == 0:
                        pe.wait_ge(acc_moved, CT * c)
                    for i, (a, b) in enumerate(pairs):
                        mm = nc.tensor.matmul(acc[t][:], act_parts[m % 2][:, b, t * P:(t + 1) * P], w2[a][:, m, :],
                                              start=(m == 0 and i == 0), stop=(m == NM - 1 and i == 2))
                    if m == NM - 1:
                        mm.then_inc(acc_mm, 1)
                    elif t == CT - 1:
                        mm.then_inc(down_mm, 1)

            def lift(c, m):
                n = NM * c + m
                if m == 0:
                    pe.wait_ge(z_lo, CT * (c + 1))
                pe.wait_ge(w_low, KT + 2 * m + 1)
                pe.wait_ge(gelu_done, n - 1 if m >= 2 else NM * c)
                for k in range(KT):
                    for i, (a, b) in enumerate(pairs):
                        mm = nc.tensor.matmul(up[m % 2][:], w1[a][:, k, m * P:(m + 1) * P], z[b][:, k, :],
                                              start=(k == 0 and i == 0), stop=(k == KT - 1 and i == 2))
                mm.then_inc(up_mm, 1)

            def chunk(c, more):
                first_two, last_two = (0, 1), (2, 3)
                for m in range(NM - 1):
                    lift(c, m)
                    if more and m == NM - 2:
                        turn_tile(c + 1, 0)
                    if m >= LAG:
                        down(c, m - LAG, first_two + last_two)
                    if more:
                        prepare(c + 1, m)
                if more:
                    turn_tile(c + 1, 1)
                lift(c, NM - 1)
                down(c, NM - 3, first_two + last_two)
                if more:
                    turn_tile(c + 1, 2)
                down(c, NM - 2, first_two)
                if more:
                    turn_tile(c + 1, 3)
                down(c, NM - 2, last_two)
                down(c, NM - 1, first_two + last_two)

            for t in range(CT):
                r = slice(t * P, (t + 1) * P)
                pe.wait_ge(heads_lo, t + 1)
                for k in range(KT):
                    if t == 0:
                        pe.wait_ge(w_low, k + 1)
                    for i, (a, b) in enumerate(pairs):
                        mm = nc.tensor.matmul(acc[t][:], z[b][:, k, r], wp[a][:, k, :],
                                              start=(k == 0 and i == 0), stop=(k == KT - 1 and i == 2))
                mm.then_inc(proj_mm, 1)
            for t in range(CT):
                turn_tile(0, t)
            chunk(0, True)
            with pe.Fori(1, NC - 1) as c:
                chunk(c, True)
            chunk(NC - 1, False)

        @block.vector
        def _(dve):
            def split_low(n):
                dve.wait_ge(w_high, n + 1)
                nc.vector.tensor_tensor(piece(pieces[n], 1), piece_shape(n, stage[slot[n]]), full(piece(pieces[n], 0)),
                                        ALU.subtract).then_inc(w_low, 1)

            def make_y(c, t):
                n = CT * c + t
                yt = y_next[:, t, :]
                dve.wait_ge(proj_mm, n + 1)
                dve.wait_ge(y_taken, c)
                nc.vector.tensor_tensor(yt, proj[:], p_bias[:], ALU.add).then_inc(proj_moved, 1)
                if t == 0:
                    dve.wait_ge(gate1_in, 16 * (c + 1))
                dve.wait_ge(proj_moved, n + 1)
                nc.vector.tensor_tensor(yt, yt, gate1[:], ALU.mult).then_inc(y_gated, 1)
                dve.wait_ge(y_gated, n + 1 - CT)
                dve.wait_ge(x_in, 16 * (n + 1 - CT))
                nc.vector.tensor_tensor(yt, yt, x_tile[:], ALU.add).then_inc(y_done, 1)
                square(c, t)

            def square(c, t):
                n = CT * c + t
                yt = y_next[:, t, :]
                dve.wait_ge(y_done, n + 1)
                dve.wait_ge(y_stat, n)
                dve.wait_ge(y_clamped, c)
                nc.vector.tensor_tensor_reduce(y_norm[t % 2][:], yt, yt, 1.0, 0.0, ALU.mult, ALU.add, y_sq[:, t:t + 1]).then_inc(y_stat, 1)

            def prepare(c, m):
                if m in SPLIT:
                    n = CT * c + SPLIT[m]
                    t = SPLIT[m]
                    dve.wait_ge(heads_in[t % 2], 16 * ((c - 1) * (CT // 2) + t // 2 + 1))
                    dve.wait_ge(proj_mm, n)
                    nc.vector.tensor_copy(heads_parts[:, 0, :, :], heads[t % 2][:]).then_inc(heads_hi, 1)
                    dve.wait_ge(heads_hi, n + 1)
                    nc.vector.tensor_tensor(heads_parts[:, 1, :, :], heads[t % 2][:], full(heads_parts[:, 0, :, :]), ALU.subtract).then_inc(heads_lo, 1)
                if m in MAKE:
                    make_y(c, MAKE[m])
                if m == NORM:
                    clamp(c)

            def clamp(c):
                dve.wait_ge(y_stat, CT * (c + 1))
                dve.wait_ge(y_inverse, c)
                dve.wait_ge(z_hi, CT * c)
                nc.vector.tensor_scalar(y_sqc[:], y_sq[:], EPS2, None, ALU.max).then_inc(y_clamped, 1)
                dve.wait_ge(mod_in, 16 * (c + 1))
                nc.vector.tensor_scalar(scale1[:], mod[:, KT:2 * KT], 1.0, None, ALU.add).then_inc(mod_ready, 1)

            def normalise(c, t):
                nc.vector.tensor_scalar(y_norm[t % 2][:], y_next[:, t, :], y_inv[:, t:t + 1], small["y_gain"][:],
                                        ALU.mult, ALU.mult).then_inc(y_normed, 1)

            def turn_tile(c, t):
                n = CT * c + t
                if t == 0:
                    dve.wait_ge(y_inverse, c + 1)
                    dve.wait_ge(mod_ready, c + 1)
                    normalise(c, 0)
                    normalise(c, 1)
                dve.wait_ge(turned, n + 1)
                if t + 2 < CT:
                    normalise(c, t + 2)
                dve.wait_ge(z_lo, CT * c + max(0, t - 1))
                for k in range(KT // 2 if is_first(c) else KT):
                    mv = nc.vector.tensor_scalar(z_full[t % 2][:, k, :], turn_bank(c, t, k)[:, k * P:(k + 1) * P], scale1[:, k:k + 1], mod[:, k:k + 1],
                                                 ALU.mult, ALU.add)
                mv.then_inc(z_moved, 1)

            def take_over(c):
                dve.wait_ge(out_done, CT * (c + 1))
                nc.vector.tensor_copy(y[:], y_next[:]).then_inc(y_taken, 1)

            def mlp(c, m):
                if is_first(c):
                    for n in late(m):
                        split_low(n)

            def first():
                for k in range(KT):
                    split_low(k)
                dve.wait_ge(gate1_in, 16)
                for t in range(CT):
                    dve.wait_ge(x_biased, t + 1)
                    dve.wait_ge(proj_mm, t + 1)
                    nc.vector.tensor_tensor(y_next[:, t, :], acc[t][:], gate1[:], ALU.mult).then_inc(proj_moved, 1)
                    dve.wait_ge(proj_moved, t + 1)
                    nc.vector.tensor_tensor(y_next[:, t, :], y_next[:, t, :], x_first[t], ALU.add).then_inc(y_done, 1)
                    square(0, t)
                clamp(0)
                for n in range(KT, len(stage)):
                    split_low(n)
                for t in range(CT):
                    turn_tile(0, t)
                for n in range(len(stage), EARLY):
                    split_low(n)
                dve.wait_ge(w_low, EARLY)
                take_over(-1)

            def finish(c, t):
                n = CT * c + t
                r = result[t % 2]
                dve.wait_ge(acc_mm, n + 1)
                dve.wait_ge(out_stored[t % 2], 16 * (CT // 2 * c + t // 2))
                if t == 0:
                    dve.wait_ge(gate2_in, 16 * (c + 1))
                    dve.wait_ge(y_biased, CT * (c + 1))
                nc.vector.tensor_tensor(r[:], acc[t][:], gate2[:], ALU.mult).then_inc(acc_moved, 1)
                dve.wait_ge(acc_moved, n + 1)
                nc.vector.tensor_tensor(r[:], r[:], y[:, t, :], ALU.add).then_inc(out_done, 1)
                if t == CT - 1 and not (isinstance(c, int) and c == NC - 1):
                    take_over(c)

            chunks(first, prepare, turn_tile, mlp, finish, dve.Fori)


def program(nc, x, cT, wadaT, bada, wqkvT, bqkv, bqkT, wprojT, bproj, wfc1T, bfc1T, wfc2T, bfc2, g1, g2, gq, gk, out):
    dram = dict(x=x, cT=cT, wadaT=wadaT, bada=bada, wqkvT=wqkvT, bqkv=bqkv, bqkT=bqkT, wprojT=wprojT, bproj=bproj,
                wfc1T=wfc1T, bfc1T=bfc1T, wfc2T=wfc2T, bfc2=bfc2, g1=g1, g2=g2, gq=gq, gk=gk, out=out)
    dram["ada_b"] = nc.dram_tensor("ada_b", [B, NA_NOW * CH], F32, kind="Internal").ap()
    dram["ada_c"] = nc.dram_tensor("ada_c", [NC, NA_LATER * CH], F32, kind="Internal").ap()
    dram["parts"] = nc.dram_tensor("parts_scratch", [NU, 2, P, CH], F32, kind="Internal").ap()
    dram["rows"] = nc.dram_tensor("rows_scratch", [HG, CH], F32, kind="Internal").ap()
    dram["inverse"] = nc.dram_tensor("inverse_scratch", [HG, CH], F32, kind="Internal").ap()
    dram["heads_out"] = nc.dram_tensor("heads_out", [NC, D, CH], F32, kind="Internal").ap()
    with ExitStack() as ctx:
        small = {}
        for name, cols in (("ident", P), ("head_ones", P), ("ones", DH), ("minus_half", CT), ("ln_bias", 1), ("shift", 1),
                           ("silu", KT * B), ("x_gain", 1), ("y_gain", 1), ("s_gain", 1)):
            small[name] = ctx.enter_context(nc.sbuf_tensor(name, [P, cols], F32))
        with ExitStack() as weights:
            wq_hi = weights.enter_context(nc.sbuf_tensor("wqkv_hi", [P, KT, 3 * D], F32R))
            wq_lo = weights.enter_context(nc.sbuf_tensor("wqkv_lo", [P, KT, 3 * D], F32R))
            build_setup(nc, small, dram, wq_hi, wq_lo)
            build_attention(nc, small, dram, wq_hi, wq_lo)
        build_mlp(nc, small, dram)


def kernel(x, cond_1024, L0_cond_g1, L0_cond_g2, L0_cond_gq, L0_cond_gk, L0_cond_Wqkv, L0_cond_bqkv, L0_cond_Wproj,
           L0_cond_bproj, L0_cond_Wfc1, L0_cond_bfc1, L0_cond_Wfc2, L0_cond_bfc2, L0_cond_Wada, L0_cond_bada):
    import numpy as np
    import concourse.bacc as bacc
    from concourse.bass_utils import run_bass_kernel_spmd

    def turned(a):
        return np.ascontiguousarray(np.asarray(a).T)

    bqkv = np.ascontiguousarray(L0_cond_bqkv)
    arrays = {
        "x": np.ascontiguousarray(x), "cT": turned(cond_1024), "wadaT": turned(L0_cond_Wada),
        "bada": np.ascontiguousarray(L0_cond_bada), "wqkvT": turned(L0_cond_Wqkv), "bqkv": bqkv,
        "bqkT": turned(bqkv[:2 * D].reshape(2 * NG, P)), "wprojT": turned(L0_cond_Wproj),
        "bproj": np.ascontiguousarray(L0_cond_bproj), "wfc1T": turned(L0_cond_Wfc1),
        "bfc1T": turned(np.asarray(L0_cond_bfc1).reshape(NM, P)), "wfc2T": turned(L0_cond_Wfc2),
        "bfc2": np.ascontiguousarray(L0_cond_bfc2), "g1": np.ascontiguousarray(L0_cond_g1),
        "g2": np.ascontiguousarray(L0_cond_g2), "gq": np.ascontiguousarray(L0_cond_gq), "gk": np.ascontiguousarray(L0_cond_gk),
    }
    nc = bacc.Bacc("TRN2", target_bir_lowering=False, num_devices=1, dynamic_dma_scratch_size=1024)
    args = [nc.dram_tensor(f"in_{n}", a.shape, mybir.dt.from_np(a.dtype), kind="ExternalInput").ap() for n, a in arrays.items()]
    args.append(nc.dram_tensor("out", (B, T, D), F32, kind="ExternalOutput").ap())
    program(nc, *args)
    r = run_bass_kernel_spmd(nc, [{f"in_{n}": a for n, a in arrays.items()}], core_ids=[0])
    return r.results[0]["out"]
```
